# Optimizing a Trainium2 kernel written in Bass

```python
import numpy as np
import jax
import jax.numpy as jnp

def _softmax(x, axis=-1):
    return jax.nn.softmax(x, axis=axis)

def _gelu(x):
    return jax.nn.gelu(x, approximate=True)

def _silu(x):
    return jax.nn.silu(x)

def _sigmoid(x):
    return jax.nn.sigmoid(x)

def _layernorm(x, axis=-1, eps=1e-05):
    m = jnp.mean(x, axis=axis, keepdims=True)
    v = jnp.var(x, axis=axis, keepdims=True)
    return (x - m) / jnp.sqrt(v + eps)

def _scatter_add(tgt, idx, src, axis=0):
    return tgt.at[idx].add(src)

def _segment_sum(src, seg, n):
    return jax.ops.segment_sum(src, seg, n)
kernel_name = 'mk_gnn_resnorm_d4_gnn_r8_2a2450'

def setup_inputs(seed: int=0):
    np.random.seed(seed)
    _w = jnp.asarray

    def _rec_inputs():
        import jax
        import jax.numpy as jnp
        _gk = jax.random.key(seed)
        x = -0.0004942 + 1 * jax.random.normal(jax.random.fold_in(_gk, 1), (3750, 128), jnp.float32)
        _s = jax.random.randint(jax.random.fold_in(_gk, 2), (60000,), 0, 3750, jnp.int32)
        _d = jax.random.randint(jax.random.fold_in(_gk, 3), (60000,), 0, 3750, jnp.int32)
        _loop = jnp.arange(3750, dtype=jnp.int32)
        src = jnp.concatenate([_s, _d, _loop])
        dst = jnp.concatenate([_d, _s, _loop])
        _o = jnp.argsort(dst, stable=True)
        src = src[_o]
        dst = dst[_o]
        edge_attr_10 = jax.random.uniform(jax.random.fold_in(_gk, 12), (123750, 10), jnp.float32, 0.0, 1)
        edge_attr_4 = 0.00109026 + 0.999989 * jax.random.normal(jax.random.fold_in(_gk, 13), (123750, 4), jnp.float32)
        edge_type_32 = jax.random.randint(jax.random.fold_in(_gk, 15), (123750,), 0, 32, jnp.int32)
        edge_weight = jax.random.uniform(jax.random.fold_in(_gk, 16), (123750,), jnp.float32, 0.0, 0.999998)
        edge_weight1 = jax.random.uniform(jax.random.fold_in(_gk, 17), (123750, 1), jnp.float32, 0.0, 0.999994)
        node_vec1 = jax.random.uniform(jax.random.fold_in(_gk, 18), (3750, 1), jnp.float32, 0.0, 1)
        return (x, src, dst, edge_attr_10, edge_attr_4, edge_type_32, edge_weight, edge_weight1, node_vec1)
    x, src, dst, edge_attr_10, edge_attr_4, edge_type_32, edge_weight, edge_weight1, node_vec1 = _rec_inputs()

    def _L0_gnn_setup():
        import jax, jax.numpy as jnp
        import numpy as np
        N = 3750
        E = 60000
        D = 128
        R = 32
        B = 8

        def _rel_graph_conv(h, basis, coeff, bias, src, dst, etype, norm):
            W = jnp.einsum('rb,bdf->rdf', coeff, basis)
            Hr = jnp.einsum('nd,rdf->nrf', h, W)
            msg = Hr[src, etype] * norm
            agg = jax.ops.segment_sum(msg, dst, num_segments=N)
            return agg + bias
        key = jax.random.key(seed)
        ks = jax.random.split(key, 11)
        return {'feat': jax.random.normal(ks[0], (N, D), jnp.float32), 'norm': jax.random.uniform(ks[1], (E, 1), jnp.float32), 'basis1': jax.random.normal(ks[2], (B, D, D), jnp.float32) * 0.05, 'coeff1': jax.random.normal(ks[3], (R, B), jnp.float32) * 0.3, 'bias1': jnp.zeros((D,), jnp.float32), 'basis2': jax.random.normal(ks[4], (B, D, D), jnp.float32) * 0.05, 'coeff2': jax.random.normal(ks[5], (R, B), jnp.float32) * 0.3, 'bias2': jnp.zeros((D,), jnp.float32), 'src': jax.random.randint(ks[6], (E,), 0, N, jnp.int32), 'dst': jax.random.randint(ks[7], (E,), 0, N, jnp.int32), 'etype': jax.random.randint(ks[8], (E,), 0, R, jnp.int32)}
    _L0_gnn_all = _L0_gnn_setup()
    _L0_gnn_in = {k: v for k, v in _L0_gnn_all.items() if k in ('basis1', 'coeff1', 'bias1', 'basis2', 'coeff2', 'bias2')}
    del _L0_gnn_all

    def _L1_gnn_setup():
        import jax, jax.numpy as jnp
        import numpy as np
        N_NODES = 12500
        N_EDGES = 80000
        D_IN = 128
        D_OUT = 128
        key = jax.random.key(seed)
        k1, k2, k3, k4, k5 = jax.random.split(key, 5)
        x = jax.random.normal(k1, (N_NODES, D_IN), dtype=jnp.float32)
        edge_index = jax.random.randint(k2, (2, N_EDGES), 0, N_NODES, dtype=jnp.int64)
        edge_weight = jax.random.uniform(k3, (N_EDGES,), dtype=jnp.float32)
        weight = jax.random.normal(k4, (D_IN, D_OUT), dtype=jnp.float32) * (1.0 / np.sqrt(D_IN))
        bias = jax.random.normal(k5, (D_OUT,), dtype=jnp.float32) * 0.01
        return {'x': x, 'edge_index': edge_index, 'edge_weight': edge_weight, 'weight': weight, 'bias': bias}
    _L1_gnn_all = _L1_gnn_setup()
    _L1_gnn_in = {k: v for k, v in _L1_gnn_all.items() if k in ('weight', 'bias')}
    del _L1_gnn_all

    def _L2_gnn_setup():
        import jax, jax.numpy as jnp
        import numpy as np
        NEG_SLOPE = 0.2

        def gat_layer(x, src, dst, W, att_src, att_dst, bias, num_nodes):
            H, C = att_src.shape
            h = (x @ W).reshape(num_nodes, H, C)
            a_src = (h * att_src).sum(-1)
            a_dst = (h * att_dst).sum(-1)
            e = jax.nn.leaky_relu(a_src[src] + a_dst[dst], NEG_SLOPE)
            m = jax.ops.segment_max(e, dst, num_segments=num_nodes)
            ex = jnp.exp(e - m[dst])
            denom = jax.ops.segment_sum(ex, dst, num_segments=num_nodes)
            alpha = ex / denom[dst]
            out = jax.ops.segment_sum(alpha[:, :, None] * h[src], dst, num_segments=num_nodes)
            return out.reshape(num_nodes, H * C) + bias
        key = jax.random.key(seed)
        ks = jax.random.split(key, 12)
        N, E, D, H = (6250, 100000, 128, 8)
        C = D // H
        x = jax.random.normal(ks[0], (N, D), dtype=jnp.float32)
        edge_index = jax.random.randint(ks[1], (2, E), 0, N, dtype=jnp.int64)
        s = 0.1
        return {'x': x, 'edge_index': edge_index, 'W1': s * jax.random.normal(ks[2], (D, H * C), dtype=jnp.float32), 'as1': s * jax.random.normal(ks[3], (H, C), dtype=jnp.float32), 'ad1': s * jax.random.normal(ks[4], (H, C), dtype=jnp.float32), 'b1': jnp.zeros((H * C,), dtype=jnp.float32), 'W2': s * jax.random.normal(ks[5], (D, H * C), dtype=jnp.float32), 'as2': s * jax.random.normal(ks[6], (H, C), dtype=jnp.float32), 'ad2': s * jax.random.normal(ks[7], (H, C), dtype=jnp.float32), 'b2': jnp.zeros((H * C,), dtype=jnp.float32)}
    _L2_gnn_all = _L2_gnn_setup()
    _L2_gnn_in = {k: v for k, v in _L2_gnn_all.items() if k in ('W1', 'as1', 'ad1', 'b1', 'W2', 'as2', 'ad2', 'b2')}
    del _L2_gnn_all

    def _L3_gnn_setup():
        import math
        import jax
        import jax.numpy as jnp
        import numpy as np
        MUL = 32
        N_NODES = 6250
        N_EDGES = 100000
        N_BASIS = 10
        N_HID = 100
        NUM_NEIGHBORS = 16.0

        def _fctp(x0, x1, attr, W0, W1):
            inv = 1.0 / math.sqrt(W0.shape[0])
            o0 = attr * (x0 @ W0) * inv
            o1 = attr[:, :, None] * jnp.einsum('nud,uw->nwd', x1, W1) * inv
            return (o0, o1)

        def _forward(node_input, node_attr, edge_attr, edge_length_embedded, W_sc0, W_sc1, W_l10, W_l11, W_l20, W_l21, W_fc1, W_fc2, edge_src, edge_dst):
            N = node_input.shape[0]
            x0 = node_input[:, :MUL]
            x1 = node_input[:, MUL:].reshape(N, MUL, 3)
            s0, s1 = _fctp(x0, x1, node_attr, W_sc0, W_sc1)
            y0, y1 = _fctp(x0, x1, node_attr, W_l10, W_l11)
            h = jax.nn.silu(edge_length_embedded @ W_fc1 * (1.0 / math.sqrt(N_BASIS)))
            w = h @ W_fc2 * (1.0 / math.sqrt(N_HID))
            w1, w2, w3, w4 = (w[:, 0 * MUL:1 * MUL], w[:, 1 * MUL:2 * MUL], w[:, 2 * MUL:3 * MUL], w[:, 3 * MUL:4 * MUL])
            x0s = y0[edge_src]
            x1s = y1[edge_src]
            ea0 = edge_attr[:, :1]
            ea1 = edge_attr[:, 1:]
            mid0a = w1 * x0s * ea0
            mid0b = w4 * jnp.einsum('eum,em->eu', x1s, ea1) * (1.0 / math.sqrt(3.0))
            mid1a = (w2 * x0s)[:, :, None] * ea1[:, None, :]
            mid1b = w3[:, :, None] * x1s * ea0[:, None, :]
            E = edge_attr.shape[0]
            edge_features = jnp.concatenate([mid0a, mid0b, mid1a.reshape(E, -1), mid1b.reshape(E, -1)], axis=1)
            agg = jax.ops.segment_sum(edge_features, edge_dst, num_segments=N)
            agg = agg * (1.0 / math.sqrt(NUM_NEIGHBORS))
            m0 = agg[:, :2 * MUL]
            m1 = agg[:, 2 * MUL:].reshape(N, 2 * MUL, 3)
            z0, z1 = _fctp(m0, m1, node_attr, W_l20, W_l21)
            c_s = math.sin(math.pi / 8.0)
            c_x = math.cos(math.pi / 8.0)
            out0 = c_s * s0 + c_x * z0
            out1 = c_s * s1 + c_x * z1
            return jnp.concatenate([out0, out1.reshape(N, -1)], axis=1)
        key = jax.random.key(seed)
        ks = jax.random.split(key, 14)
        return {'node_input': jax.random.normal(ks[0], (N_NODES, 4 * MUL), jnp.float32), 'node_attr': jnp.ones((N_NODES, 1), jnp.float32), 'edge_src': jax.random.randint(ks[1], (N_EDGES,), 0, N_NODES, dtype=jnp.int32), 'edge_dst': jax.random.randint(ks[2], (N_EDGES,), 0, N_NODES, dtype=jnp.int32), 'edge_attr': jax.random.normal(ks[3], (N_EDGES, 4), jnp.float32), 'edge_length_embedded': jax.random.uniform(ks[4], (N_EDGES, N_BASIS), dtype=jnp.float32), 'W_sc0': jax.random.normal(ks[5], (MUL, MUL), jnp.float32), 'W_sc1': jax.random.normal(ks[6], (MUL, MUL), jnp.float32), 'W_l10': jax.random.normal(ks[7], (MUL, MUL), jnp.float32), 'W_l11': jax.random.normal(ks[8], (MUL, MUL), jnp.float32), 'W_l20': jax.random.normal(ks[9], (2 * MUL, MUL), jnp.float32), 'W_l21': jax.random.normal(ks[10], (2 * MUL, MUL), jnp.float32), 'W_fc1': jax.random.normal(ks[11], (N_BASIS, N_HID), jnp.float32), 'W_fc2': jax.random.normal(ks[12], (N_HID, 4 * MUL), jnp.float32)}
    _L3_gnn_all = _L3_gnn_setup()
    _L3_gnn_in = {k: v for k, v in _L3_gnn_all.items() if k in ('W_sc0', 'W_sc1', 'W_l10', 'W_l11', 'W_l20', 'W_l21', 'W_fc1', 'W_fc2')}
    del _L3_gnn_all
    return {'x': x, 'src': src, 'dst': dst, 'edge_attr_10': edge_attr_10, 'edge_attr_4': edge_attr_4, 'edge_type_32': edge_type_32, 'edge_weight': edge_weight, 'edge_weight1': edge_weight1, 'node_vec1': node_vec1, 'L0_gnn_basis1': _L0_gnn_in['basis1'], 'L0_gnn_coeff1': _L0_gnn_in['coeff1'], 'L0_gnn_bias1': _L0_gnn_in['bias1'], 'L0_gnn_basis2': _L0_gnn_in['basis2'], 'L0_gnn_coeff2': _L0_gnn_in['coeff2'], 'L0_gnn_bias2': _L0_gnn_in['bias2'], 'L1_gnn_weight': _L1_gnn_in['weight'], 'L1_gnn_bias': _L1_gnn_in['bias'], 'L2_gnn_W1': _L2_gnn_in['W1'], 'L2_gnn_as1': _L2_gnn_in['as1'], 'L2_gnn_ad1': _L2_gnn_in['ad1'], 'L2_gnn_b1': _L2_gnn_in['b1'], 'L2_gnn_W2': _L2_gnn_in['W2'], 'L2_gnn_as2': _L2_gnn_in['as2'], 'L2_gnn_ad2': _L2_gnn_in['ad2'], 'L2_gnn_b2': _L2_gnn_in['b2'], 'L3_gnn_W_sc0': _L3_gnn_in['W_sc0'], 'L3_gnn_W_sc1': _L3_gnn_in['W_sc1'], 'L3_gnn_W_l10': _L3_gnn_in['W_l10'], 'L3_gnn_W_l11': _L3_gnn_in['W_l11'], 'L3_gnn_W_l20': _L3_gnn_in['W_l20'], 'L3_gnn_W_l21': _L3_gnn_in['W_l21'], 'L3_gnn_W_fc1': _L3_gnn_in['W_fc1'], 'L3_gnn_W_fc2': _L3_gnn_in['W_fc2']}

def reference(x, src, dst, edge_attr_10, edge_attr_4, edge_type_32, edge_weight, edge_weight1, node_vec1, L0_gnn_basis1, L0_gnn_coeff1, L0_gnn_bias1, L0_gnn_basis2, L0_gnn_coeff2, L0_gnn_bias2, L1_gnn_weight, L1_gnn_bias, L2_gnn_W1, L2_gnn_as1, L2_gnn_ad1, L2_gnn_b1, L2_gnn_W2, L2_gnn_as2, L2_gnn_ad2, L2_gnn_b2, L3_gnn_W_sc0, L3_gnn_W_sc1, L3_gnn_W_l10, L3_gnn_W_l11, L3_gnn_W_l20, L3_gnn_W_l21, L3_gnn_W_fc1, L3_gnn_W_fc2):
    import jax
    import jax.numpy as jnp

    def _L0_gnn_ref(feat, norm, basis1, coeff1, bias1, basis2, coeff2, bias2, src, dst, etype):
        import jax, jax.numpy as jnp
        import numpy as np
        N = 3750
        E = 60000
        D = 128
        R = 32
        B = 8

        def _rel_graph_conv(h, basis, coeff, bias, src, dst, etype, norm):
            W = jnp.einsum('rb,bdf->rdf', coeff, basis)
            Hr = jnp.einsum('nd,rdf->nrf', h, W)
            msg = Hr[src, etype] * norm
            agg = jax.ops.segment_sum(msg, dst, num_segments=N)
            return agg + bias
        h = jax.nn.relu(_rel_graph_conv(feat, basis1, coeff1, bias1, src, dst, etype, norm))
        out = _rel_graph_conv(h, basis2, coeff2, bias2, src, dst, etype, norm)
        return out

    def _L1_gnn_ref(x, edge_index, edge_weight, weight, bias):
        import jax, jax.numpy as jnp
        import numpy as np
        N_NODES = 12500
        N_EDGES = 80000
        D_IN = 128
        D_OUT = 128
        num_nodes = x.shape[0]
        h = jnp.matmul(x, weight)
        src = edge_index[0]
        tgt = edge_index[1]
        weighted = h[src] * edge_weight[:, None]
        aggregated = jax.ops.segment_sum(weighted, tgt, num_segments=num_nodes)
        in_deg = jax.ops.segment_sum(edge_weight, tgt, num_segments=num_nodes)
        in_deg = jnp.maximum(in_deg, 1.0)
        dinv = jax.lax.rsqrt(in_deg)[:, None]
        out = h * dinv + aggregated * dinv
        return out + bias

    def _L2_gnn_ref(x, edge_index, W1, as1, ad1, b1, W2, as2, ad2, b2):
        import jax, jax.numpy as jnp
        import numpy as np
        NEG_SLOPE = 0.2

        def gat_layer(x, src, dst, W, att_src, att_dst, bias, num_nodes):
            H, C = att_src.shape
            h = (x @ W).reshape(num_nodes, H, C)
            a_src = (h * att_src).sum(-1)
            a_dst = (h * att_dst).sum(-1)
            e = jax.nn.leaky_relu(a_src[src] + a_dst[dst], NEG_SLOPE)
            m = jax.ops.segment_max(e, dst, num_segments=num_nodes)
            ex = jnp.exp(e - m[dst])
            denom = jax.ops.segment_sum(ex, dst, num_segments=num_nodes)
            alpha = ex / denom[dst]
            out = jax.ops.segment_sum(alpha[:, :, None] * h[src], dst, num_segments=num_nodes)
            return out.reshape(num_nodes, H * C) + bias
        n = x.shape[0]
        loop = jnp.arange(n, dtype=edge_index.dtype)
        src = jnp.concatenate([edge_index[0], loop])
        dst = jnp.concatenate([edge_index[1], loop])
        h = jax.nn.relu(gat_layer(x, src, dst, W1, as1, ad1, b1, n))
        return gat_layer(h, src, dst, W2, as2, ad2, b2, n)

    def _L3_gnn_ref(node_input, node_attr, edge_src, edge_dst, edge_attr, edge_length_embedded, W_sc0, W_sc1, W_l10, W_l11, W_l20, W_l21, W_fc1, W_fc2):
        import math
        import jax
        import jax.numpy as jnp
        import numpy as np
        MUL = 32
        N_NODES = 6250
        N_EDGES = 100000
        N_BASIS = 10
        N_HID = 100
        NUM_NEIGHBORS = 16.0

        def _fctp(x0, x1, attr, W0, W1):
            inv = 1.0 / math.sqrt(W0.shape[0])
            o0 = attr * (x0 @ W0) * inv
            o1 = attr[:, :, None] * jnp.einsum('nud,uw->nwd', x1, W1) * inv
            return (o0, o1)

        def _forward(node_input, node_attr, edge_attr, edge_length_embedded, W_sc0, W_sc1, W_l10, W_l11, W_l20, W_l21, W_fc1, W_fc2, edge_src, edge_dst):
            N = node_input.shape[0]
            x0 = node_input[:, :MUL]
            x1 = node_input[:, MUL:].reshape(N, MUL, 3)
            s0, s1 = _fctp(x0, x1, node_attr, W_sc0, W_sc1)
            y0, y1 = _fctp(x0, x1, node_attr, W_l10, W_l11)
            h = jax.nn.silu(edge_length_embedded @ W_fc1 * (1.0 / math.sqrt(N_BASIS)))
            w = h @ W_fc2 * (1.0 / math.sqrt(N_HID))
            w1, w2, w3, w4 = (w[:, 0 * MUL:1 * MUL], w[:, 1 * MUL:2 * MUL], w[:, 2 * MUL:3 * MUL], w[:, 3 * MUL:4 * MUL])
            x0s = y0[edge_src]
            x1s = y1[edge_src]
            ea0 = edge_attr[:, :1]
            ea1 = edge_attr[:, 1:]
            mid0a = w1 * x0s * ea0
            mid0b = w4 * jnp.einsum('eum,em->eu', x1s, ea1) * (1.0 / math.sqrt(3.0))
            mid1a = (w2 * x0s)[:, :, None] * ea1[:, None, :]
            mid1b = w3[:, :, None] * x1s * ea0[:, None, :]
            E = edge_attr.shape[0]
            edge_features = jnp.concatenate([mid0a, mid0b, mid1a.reshape(E, -1), mid1b.reshape(E, -1)], axis=1)
            agg = jax.ops.segment_sum(edge_features, edge_dst, num_segments=N)
            agg = agg * (1.0 / math.sqrt(NUM_NEIGHBORS))
            m0 = agg[:, :2 * MUL]
            m1 = agg[:, 2 * MUL:].reshape(N, 2 * MUL, 3)
            z0, z1 = _fctp(m0, m1, node_attr, W_l20, W_l21)
            c_s = math.sin(math.pi / 8.0)
            c_x = math.cos(math.pi / 8.0)
            out0 = c_s * s0 + c_x * z0
            out1 = c_s * s1 + c_x * z1
            return jnp.concatenate([out0, out1.reshape(N, -1)], axis=1)
        return _forward(node_input, node_attr, edge_attr, edge_length_embedded, W_sc0, W_sc1, W_l10, W_l11, W_l20, W_l21, W_fc1, W_fc2, edge_src, edge_dst)
    edge_index = jnp.stack([src, dst])
    x = _layernorm(x + _L0_gnn_ref(x, edge_weight1, L0_gnn_basis1, L0_gnn_coeff1, L0_gnn_bias1, L0_gnn_basis2, L0_gnn_coeff2, L0_gnn_bias2, src, dst, edge_type_32), axis=-1)
    x = _layernorm(x + _L1_gnn_ref(x, edge_index, edge_weight, L1_gnn_weight, L1_gnn_bias), axis=-1)
    x = _layernorm(x + _L2_gnn_ref(x, edge_index, L2_gnn_W1, L2_gnn_as1, L2_gnn_ad1, L2_gnn_b1, L2_gnn_W2, L2_gnn_as2, L2_gnn_ad2, L2_gnn_b2), axis=-1)
    x = _layernorm(x + _L3_gnn_ref(x, node_vec1, src, dst, edge_attr_4, edge_attr_10, L3_gnn_W_sc0, L3_gnn_W_sc1, L3_gnn_W_l10, L3_gnn_W_l11, L3_gnn_W_l20, L3_gnn_W_l21, L3_gnn_W_fc1, L3_gnn_W_fc2), axis=-1)
    return x

_drawn_inputs = setup_inputs


def setup_inputs(seed=0):
    import zlib

    import numpy as np

    out = dict(_drawn_inputs(seed))
    spreads = {'L0_gnn_bias1': (0.0, 0.1),
     'L0_gnn_bias2': (0.0, 0.1),
     'L2_gnn_b1': (0.0, 0.1),
     'L2_gnn_b2': (0.0, 0.1)}
    factors = {'L1_gnn_bias': 8.0,
     'L2_gnn_as1': 3.048,
     'L2_gnn_ad1': 25.106,
     'L2_gnn_as2': 42.35,
     'L2_gnn_ad2': 64.0}
    for name, (base, spread) in spreads.items():
        noise = np.random.default_rng([zlib.crc32(name.encode()), seed]).standard_normal(out[name].shape)
        drawn = base * np.exp(spread * noise) if base else spread * noise
        out[name] = jnp.asarray(drawn.astype(out[name].dtype))
    for name, factor in factors.items():
        out[name] = (out[name] * factor).astype(out[name].dtype)
    return out
```

```python
from contextlib import ExitStack
import math

import concourse.bass as bass
from concourse import mybir

F32 = mybir.dt.float32
BF16 = mybir.dt.bfloat16
I32 = mybir.dt.int32
ALU = mybir.AluOpType
ACT = mybir.ActivationFunctionType
AX_X = mybir.AxisListType.X
DVE_ENGINE = mybir.EngineType.DVE

P = 128
N, E, D = 3750, 123750, 128
REL, BASES = 32, 8
HEADS, CH = 8, 16
MUL, HID, LEN = 32, 100, 10
BLKS = -(-N // P)
NPAD = BLKS * P
LAST = N - (BLKS - 1) * P
ACC = NPAD + P

CHUNKS = 16
GRPS = 64
TILES = CHUNKS * GRPS
SLOTS = TILES * P
CHUNK = GRPS * P
assert N + E <= SLOTS

EP, EC = 125, 990
assert EP * EC == E
SB = 15
SBATCHES = EC // SB
REC = 20
R_SRC, R_TAB, R_DST, R_W, R_W1, R_START, R_EA, R_LEN = 0, 1, 2, 3, 4, 5, 6, 10
SLOT_BUFS = 16
AHEAD = 3
BIG = 1e30
EPS = 1e-5


class Signal:

    def __init__(self, sem):
        self.sem, self.base = sem, 0

    def at(self, n):
        return self.base + n

    def passed(self, n):
        self.base += n


class Env:

    def __init__(self, nc, ctx):
        self.nc, self.ctx, self.signals = nc, ctx, {}

    def sig(self, name):
        if name not in self.signals:
            self.signals[name] = Signal(self.ctx.enter_context(self.nc.semaphore(name)))
        return self.signals[name]

    def keep(self, name, shape, dt):
        t = self.ctx.enter_context(self.nc.sbuf_tensor(name, shape, dt))
        return t


def stage_memory(nc, ctx, tag):
    def sb(name, shape, dt):
        return ctx.enter_context(nc.sbuf_tensor(f"{tag}_{name}", shape, dt))

    def ps(name, shape, dt):
        return ctx.enter_context(nc.psum_tensor(f"{tag}_{name}", shape, dt))

    return sb, ps


def over_columns(ap, count):
    return ap.unsqueeze(2).to_broadcast([ap.shape[0], ap.shape[1], count])


def over_rows(ap, count):
    return ap.unsqueeze(1).to_broadcast([ap.shape[0], count, ap.shape[1]])


def setup(env, inp):
    nc = env.nc
    env.ident = env.keep("ident", [P, P], F32)
    env.ident_bf = env.keep("ident_bf", [P, P], BF16)
    env.iota_bf = env.keep("iota_bf", [P, P], BF16)
    env.iota_row = env.keep("iota_row", [P, P], F32)
    env.above = env.keep("above", [P, P], F32)
    env.below = env.keep("below", [P, P], F32)
    env.ones = env.keep("ones", [P, P], F32)
    env.chunk_mask = env.keep("chunk_mask", [P, CHUNKS], F32)
    env.head_mask = env.keep("head_mask", [P, HEADS], F32)
    env.head_sel = env.keep("head_sel", [P, HEADS], F32)
    env.head_sel_t = env.keep("head_sel_t", [HEADS, P], F32)
    env.x = env.keep("x", [P, BLKS + 1, D], F32)
    env.stats = env.keep("stats", [P, BLKS, 6], F32)
    env.mean = env.keep("mean", [P, BLKS], F32)
    env.spread = env.keep("spread", [P, BLKS], F32)
    env.rstd = env.keep("rstd", [P, BLKS], F32)
    env.eps = env.keep("eps", [P, 1], F32)
    env.src_idx = env.keep("src_idx", [P, TILES + SLOT_BUFS], I32)
    env.tab_idx = env.keep("tab_idx", [P, TILES + SLOT_BUFS], I32)
    env.dst_rel = env.keep("dst_rel", [P, TILES + SLOT_BUFS], F32)
    env.w = env.keep("w", [P, TILES + SLOT_BUFS], F32)
    env.w1 = env.keep("w1", [P, TILES + SLOT_BUFS], F32)
    env.start = env.keep("start", [P, TILES + SLOT_BUFS], F32)
    env.win = env.keep("win", [1, 1 + TILES], I32)
    env.idx_stage = env.keep("idx_stage", [P, SLOT_BUFS], I32)
    zeroed, consts, x_in = env.sig("x_zeroed"), env.sig("consts"), env.sig("x_loaded")
    sel_t, stepped = env.sig("sel_transposed"), env.sig("const_step")
    with ExitStack() as ctx:
        sb, ps = stage_memory(nc, ctx, "setup")
        pt = ps("pt", [P, 512], F32)
        block = ctx.enter_context(nc.Block())

        @block.gpsimd
        def _(pool):
            pool.memset(env.ident[:, :], 0.0)
            pool.memset(env.above[:, :], 1.0)
            pool.memset(env.below[:, :], 1.0)
            pool.memset(env.ones[:, :], 1.0)
            pool.memset(env.chunk_mask[:, :], 1.0)
            pool.memset(env.head_mask[:, :], 1.0)
            pool.memset(env.eps[:, :], EPS)
            pool.iota(env.iota_row[:, :], pattern=[[1, P]], base=0, channel_multiplier=0,
                      allow_small_or_imprecise_dtypes=True).then_inc(stepped.sem, 1)
            pool.wait_ge(stepped.sem, 1)
            pool.affine_select(out=env.ident[:, :], in_=env.ident[:, :], compare_op=ALU.not_equal,
                               fill=1.0, base=0, pattern=[[-1, P]], channel_multiplier=1)
            pool.affine_select(out=env.above[:, :], in_=env.above[:, :], compare_op=ALU.is_gt,
                               fill=0.0, base=0, pattern=[[1, P]], channel_multiplier=-1)
            pool.affine_select(out=env.below[:, :], in_=env.below[:, :], compare_op=ALU.is_gt,
                               fill=0.0, base=0, pattern=[[-1, P]], channel_multiplier=1)
            for mask, width, count in ((env.chunk_mask, P // CHUNKS, CHUNKS), (env.head_mask, CH, HEADS)):
                pool.affine_select(out=mask[:, :], in_=mask[:, :], compare_op=ALU.is_ge, fill=0.0,
                                   base=0, pattern=[[-width, count]], channel_multiplier=1)
            pool.memset(env.win[:, 0:1], N)
            pool.memset(env.idx_stage[:, :], 0).then_inc(stepped.sem, 1)
            pool.wait_ge(stepped.sem, 2)
            for mask, width, count in ((env.chunk_mask, P // CHUNKS, CHUNKS), (env.head_mask, CH, HEADS)):
                pool.affine_select(out=mask[:, :], in_=mask[:, :], compare_op=ALU.is_ge, fill=0.0,
                                   base=width - 1, pattern=[[width, count]],
                                   channel_multiplier=-1).then_inc(consts.sem, 1)

        @block.vector
        def _(dve):
            dve.memset(env.x[:, BLKS - 1:, :], 0.0).then_inc(zeroed.sem, 1)
            for t, fill in ((env.src_idx, 0), (env.tab_idx, 0), (env.dst_rel, 200.0), (env.w, 0.0),
                            (env.w1, 0.0), (env.start, 0.0)):
                dve.memset(t[:, TILES:], fill)
            dve.wait_ge(consts.sem, 2)
            dve.tensor_copy(env.ident_bf[:, :], env.ident[:, :])
            dve.tensor_copy(env.iota_bf[:, :], env.iota_row[:, :])
            dve.tensor_reduce(env.head_sel[:, :], env.ident[:, :].rearrange("p (c h) -> p h c", h=HEADS),
                              AX_X, ALU.add).then_inc(consts.sem, 1)
            dve.wait_ge(sel_t.sem, 1)
            dve.tensor_copy(env.head_sel_t[:, :], pt[0:HEADS, 0:P])

        @block.tensor
        def _(pe):
            pe.wait_ge(consts.sem, 3)
            pe.transpose(pt[0:HEADS, 0:P], env.head_sel[:, :], env.ident[:, :]).then_inc(sel_t.sem, 1)

        @block.sync
        def _(sp):
            sp.dma_start(env.x[:, 0:BLKS - 1, :],
                         inp["x"][0:(BLKS - 1) * P, :].rearrange("(b p) f -> p b f", p=P)).then_inc(x_in.sem, 16)
            sp.wait_ge(zeroed.sem, 1)
            sp.dma_start(env.x[0:LAST, BLKS - 1, :], inp["x"][(BLKS - 1) * P:N, :]).then_inc(x_in.sem, 16)
            sp.wait_ge(x_in.sem, 32)


def slot_rows(dve, rows_out, at, low, tile_no, scaled, chunk, row):
    dve.tensor_scalar(low, at, P - 1, None, ALU.bitwise_and)
    dve.tensor_scalar(tile_no, at, 7, None, ALU.arith_shift_right)
    dve.drain()
    dve.tensor_scalar(chunk, tile_no, 6, None, ALU.arith_shift_right)
    dve.tensor_scalar(row, low, float(TILES), None, ALU.mult)
    dve.drain()
    dve.scalar_tensor_tensor(scaled, tile_no, float(CHUNKS), row, ALU.mult, ALU.add)
    dve.drain()
    return dve.scalar_tensor_tensor(rows_out, chunk, float(1 - CHUNKS * GRPS), scaled, ALU.mult, ALU.add)


def one_hots(dve, env, hot_lo, hot_hi, lo, hi, b, h):
    for k in range(SB):
        c = bass.ds(b * SB + k, 1)
        dve.tensor_scalar(hot_lo[:, h, k, :], env.iota_bf[0:EP, :], lo[:, c], None, ALU.is_equal)
        last = dve.tensor_scalar(hot_hi[:, h, k, :], env.iota_bf[0:EP, 0:BLKS], hi[:, c], None, ALU.is_equal)
    return last


def sort_edges(env, inp, records):
    assert GRPS == 64 and P == 128
    nc = env.nc
    with ExitStack() as ctx:
        sb, ps = stage_memory(nc, ctx, "sort")
        src_i = sb("src_i", [EP, EC], I32)
        dst_i = sb("dst_i", [EP, EC], I32)
        typ_i = sb("typ_i", [EP, EC], I32)
        tab_f = sb("tab_f", [EP, EC], F32)
        dst_f = sb("dst_f", [EP, EC], F32)
        lo_i = sb("lo_i", [EP, EC], I32)
        hi_i = sb("hi_i", [EP, EC], I32)
        lo = sb("lo", [EP, EC], F32)
        hi = sb("hi", [EP, EC], F32)
        w_in = sb("w_in", [EP, EC], F32)
        w1_in = sb("w1_in", [EP, EC], F32)
        ea_in = sb("ea_in", [EP, EC, 4], F32)
        len_in = sb("len_in", [EP, EC, LEN], F32)
        hot_lo = sb("hot_lo", [EP, 2, SB, P], BF16)
        hot_hi = sb("hot_hi", [EP, 2, SB, BLKS], BF16)
        zero_lo = sb("zero_lo", [EP, P], BF16)
        count1 = sb("count1", [P, BLKS], F32)
        totals = sb("totals", [P, BLKS], F32)
        cum = sb("cum", [P, BLKS], F32)
        zeros = sb("zeros", [P, BLKS], F32)
        first = sb("first", [P, BLKS], F32)
        next_slot = sb("next_slot", [P, BLKS], F32)
        node_i = sb("node_i", [P, BLKS, 7], I32)
        node_row = sb("node_row", [P, BLKS], I32)
        node_rec = sb("node_rec", [P, BLKS, REC], F32)
        pad_rec = sb("pad_rec", [P, GRPS, REC], F32)
        recs = sb("recs", [EP, 2, SB, REC], F32)
        sigs = {n: env.sig(f"sort_{n}") for n in (
            "loaded", "prepared", "hot", "counted", "summed", "count1_ready", "node_rows", "node_recs",
            "self_written", "pads_written", "first_ready")}
        s = {n: v.sem for n, v in sigs.items()}

        with ExitStack() as inner:
            cnt = inner.enter_context(nc.psum_tensor("sort_cnt", [P, 512], F32))
            sums = inner.enter_context(nc.psum_tensor("sort_sums", [P, 512], F32))
            block = inner.enter_context(nc.Block())

            @block.sync
            def _(sp):
                for tile, name in ((dst_i, "dst"), (src_i, "src"), (typ_i, "edge_type_32"), (w_in, "edge_weight")):
                    sp.dma_start(tile[:, :], inp[name].rearrange("(p c) -> p c", c=EC)).then_inc(s["loaded"], 16)
                sp.dma_start(w1_in[:, :], inp["edge_weight1"].rearrange("(p c) o -> p (c o)", c=EC)).then_inc(s["loaded"], 16)
                sp.dma_start(ea_in[:, :, :], inp["edge_attr_4"].rearrange("(p c) k -> p c k", c=EC)).then_inc(s["loaded"], 16)
                sp.dma_start(len_in[:, :, :], inp["edge_attr_10"].rearrange("(p c) k -> p c k", c=EC)).then_inc(s["loaded"], 16)
                sp.wait_ge(s["loaded"], 7 * 16)
                sp.wait_ge(s["node_recs"], 2)
                lane, tile0 = (N + E) % P, (N + E) // P
                chunk, g0 = tile0 // GRPS, tile0 % GRPS
                assert chunk == CHUNKS - 1 and lane
                rows = records.rearrange("(p g c) k -> p g c k", p=P, c=CHUNKS)
                sp.dma_start(rows[:, g0 + 1:GRPS, chunk, :], pad_rec[:, g0 + 1:GRPS, :]).then_inc(s["pads_written"], 16)
                sp.dma_start(rows[lane:P, g0, chunk, :], pad_rec[lane:P, g0, :]).then_inc(s["pads_written"], 16)
                sp.wait_ge(s["pads_written"], 32)

            @block.vector
            def _(dve):
                dve.memset(zero_lo[:, :], 0.0)
                dve.memset(zeros[:, :], 0.0)
                dve.memset(recs[:, :, :, :], 0.0)
                dve.wait_ge(s["loaded"], 7 * 16)
                dve.tensor_scalar(lo_i[:, :], dst_i[:, :], P - 1, None, ALU.bitwise_and)
                dve.tensor_scalar(hi_i[:, :], dst_i[:, :], 7, None, ALU.arith_shift_right)
                dve.drain()
                dve.tensor_copy(lo[:, :], lo_i[:, :])
                dve.tensor_copy(hi[:, :], hi_i[:, :])
                dve.tensor_copy(dst_f[:, :], dst_i[:, :])
                dve.tensor_copy(tab_f[:, :], typ_i[:, :])
                dve.drain()
                dve.scalar_tensor_tensor(tab_f[:, :], src_i[:, :], float(REL), tab_f[:, :], ALU.mult,
                                         ALU.add).then_inc(s["prepared"], 1)
                dve.drain()
                with dve.Fori(0, SBATCHES // 2) as i:
                    for h in range(2):
                        b = i * 2 + h
                        dve.wait_ge(s["counted"], b + 1)
                        one_hots(dve, env, hot_lo, hot_hi, lo, hi, b, h).then_inc(s["hot"], 1)
                dve.wait_ge(s["counted"], SBATCHES + 3)
                dve.tensor_scalar(count1[:, :], cnt[:, 0:BLKS], 1.0, None, ALU.add).then_inc(s["count1_ready"], 1)
                dve.wait_ge(s["summed"], 1)
                dve.tensor_copy(totals[:, :], sums[:, BLKS:2 * BLKS])
                dve.drain()
                dve.tensor_tensor_scan(cum[:, :], zeros[:, :], totals[:, :], 0.0, ALU.add, ALU.add)
                dve.drain()
                dve.tensor_tensor(cum[:, :], cum[:, :], totals[:, :], ALU.subtract)
                dve.drain()
                dve.tensor_tensor(first[:, :], cum[:, :], sums[:, 0:BLKS], ALU.add)
                dve.drain()
                dve.tensor_scalar(next_slot[:, :], first[:, :], 1.0, None, ALU.add)
                dve.tensor_copy(node_i[:, :, 0], first[:, :])
                dve.drain()
                slot_rows(dve, node_row[:, :], *(node_i[:, :, k] for k in range(6))).then_inc(s["node_rows"], 1)

            @block.tensor
            def _(pe):
                pe.wait_ge(s["prepared"], 1)
                pe.matmul(cnt[:, 0:BLKS], zero_lo[:, :], zero_lo[:, 0:BLKS], start=True, stop=True,
                          skip_group_check=True).then_inc(s["counted"], 2)
                with pe.Fori(0, SBATCHES // 2) as i:
                    for h in range(2):
                        pe.wait_ge(s["hot"], i * 2 + h + 1)
                        for k in range(SB):
                            mm = pe.matmul(cnt[:, 0:BLKS], hot_lo[:, h, k, :], hot_hi[:, h, k, :], start=False,
                                           stop=False, skip_group_check=True)
                        mm.then_inc(s["counted"], 1)
                pe.matmul(cnt[:, 0:BLKS], zero_lo[:, :], zero_lo[:, 0:BLKS], start=False, stop=True,
                          skip_group_check=True).then_inc(s["counted"], 1)
                pe.wait_ge(s["count1_ready"], 1)
                pe.matmul(sums[:, 0:BLKS], env.above[:, :], count1[:, :], start=True, stop=True)
                pe.matmul(sums[:, BLKS:2 * BLKS], env.ones[:, :], count1[:, :], start=True,
                          stop=True).then_inc(s["summed"], 1)

            @block.gpsimd
            def _(pool):
                pool.memset(node_rec[:, :, :], 0.0)
                pool.memset(pad_rec[:, :, :], 0.0).then_inc(s["node_recs"], 1)
                pool.wait_ge(s["node_recs"], 1)
                pool.memset(node_rec[:, :, R_START:R_START + 1], 1.0)
                for col, mult in ((R_SRC, 1), (R_DST, 1), (R_TAB, REL)):
                    pool.iota(node_rec[:, :, col], pattern=[[P * mult, BLKS]], base=0, channel_multiplier=mult,
                              allow_small_or_imprecise_dtypes=True)
                pool.memset(pad_rec[:, :, R_DST:R_DST + 1], float(N))
                pool.memset(pad_rec[:, :, R_START:R_START + 1], 1.0).then_inc(s["node_recs"], 1)
                pool.wait_ge(s["node_recs"], 2)
                pool.wait_ge(s["node_rows"], 1)
                for b in range(BLKS):
                    m = P if b < BLKS - 1 else LAST
                    pool.indirect_dma_start(records, bass.IndirectOffsetOnAxis(ap=node_row[0:m, b:b + 1], axis=0),
                                            node_rec[0:m, b, :], None).then_inc(s["self_written"], 16)
                pool.wait_ge(s["self_written"], 16 * BLKS)

        dst_now = sb("dst_now", [EP, 2, SB], F32)
        hot_lo_t = sb("hot_lo_t", [P, 2, EP], F32)
        heads = sb("heads", [P, 2, BLKS], F32)
        same = sb("same", [EP, 2, EP], F32)
        own_head = sb("own_head", [EP, BLKS], F32)
        in_column = sb("in_column", [EP, SB], F32)
        before = sb("before", [EP, SB], F32)
        slot_i = sb("slot_i", [EP, 6, SB], I32)
        rows = sb("rows", [EP, 2, SB], I32)
        taken = ps("taken", [P, 512], F32)
        hot_ps = [ps(f"hot_ps{j}", [P, 1024], BF16) for j in range(2)]
        dst_ps = [ps(f"dst_ps{j}", [EP, 512], F32) for j in range(2)]
        head_ps = [ps(f"head_ps{j}", [EP, 512], F32) for j in range(2)]
        s = {n: env.sig(f"rank_{n}").sem for n in (
            "hot", "dst_staged", "recs_staged", "turned", "copied", "dst_wide", "ranked", "heads_ready",
            "looked", "added", "rows_ready")}
        scattered = [env.sig(f"rank_scattered{h}").sem for h in range(2)]
        issued = env.sig("dma_turn").sem
        block = ctx.enter_context(nc.Block())
        half = SBATCHES // 2
        per_batch = 16 * SB

        @block.scalar
        def _(act):
            def batch(i, h):
                b = i * 2 + h
                cols = bass.ds(b * SB, SB)
                if not (isinstance(i, int) and i == 0):
                    act.wait_ge(scattered[h], i * per_batch)
                act.copy(dst_now[:, h, :], dst_f[:, cols]).then_inc(s["dst_staged"], 1)
                for k in range(SB):
                    j = (h * SB + k) % 2
                    act.wait_ge(s["turned"], b * SB + k + 1)
                    act.wait_ge(s["looked"], b * SB + k + 1)
                    act.copy(hot_lo_t[:, j, :], hot_ps[j][:, 0:EP]).then_inc(s["copied"], 1)
                act.copy(recs[:, h, :, R_SRC], src_i[:, cols])
                act.copy(recs[:, h, :, R_TAB], tab_f[:, cols])
                act.copy(recs[:, h, :, R_DST], dst_f[:, cols])
                act.copy(recs[:, h, :, R_W], w_in[:, cols])
                act.copy(recs[:, h, :, R_W1], w1_in[:, cols])
                act.copy(recs[:, h, :, R_EA:R_EA + 4], ea_in[:, cols, :])
                act.copy(recs[:, h, :, R_LEN:R_LEN + LEN], len_in[:, cols, :]).then_inc(s["recs_staged"], 1)

            for h in range(2):
                batch(0, h)
            with act.Fori(1, half) as i:
                for h in range(2):
                    batch(i, h)

        @block.vector
        def _(dve):
            dve.sem_inc(s["ranked"], 2)
            def batch(i, h):
                b = i * 2 + h
                one_hots(dve, env, hot_lo, hot_hi, lo, hi, b, h).then_inc(s["hot"], 1)
                for k in range(SB):
                    c, j = b * SB + k, (h * SB + k) % 2
                    dve.wait_ge(s["added"], c + 1)
                    dve.tensor_tensor(heads[:, j, :], taken[:, 0:BLKS], next_slot[:, :],
                                      ALU.add).then_inc(s["heads_ready"], 1)
                    dve.wait_ge(s["dst_wide"], c + 1)
                    dve.scalar_tensor_tensor(same[:, j, :], dst_ps[j][:, 0:EP], dst_now[:, h, k:k + 1],
                                             env.below[0:EP, 0:EP], ALU.is_equal, ALU.mult,
                                             accum_out=in_column[:, k:k + 1]).then_inc(s["ranked"], 1)
                    dve.wait_ge(s["looked"], c + 3)
                    dve.tensor_tensor_reduce(own_head[:, :], head_ps[j][:, 0:BLKS], hot_hi[:, h, k, :], 1.0, 0.0,
                                             ALU.mult, ALU.add, before[:, k:k + 1])
                dve.drain()
                if not (isinstance(i, int) and i == 0):
                    dve.wait_ge(scattered[h], i * per_batch)
                dve.tensor_tensor(slot_i[:, 0, :], in_column[:, :], before[:, :], ALU.add)
                dve.drain()
                slot_rows(dve, rows[:, h, :], *(slot_i[:, m, :] for m in range(6))).then_inc(s["rows_ready"], 1)

            for h in range(2):
                batch(0, h)
            with dve.Fori(1, half) as i:
                for h in range(2):
                    batch(i, h)

        @block.tensor
        def _(pe):
            pe.sem_inc(s["looked"], 2)
            pe.matmul(taken[:, 0:BLKS], zero_lo[:, :], zero_lo[:, 0:BLKS], start=True, stop=True,
                      skip_group_check=True).then_inc(s["added"], 1)

            def ahead(b, h, k):
                j = (h * SB + k) % 2
                pe.transpose(hot_ps[j][:, 0:EP], hot_lo[:, h, k, :], env.ident_bf[0:EP, 0:EP]).then_inc(s["turned"], 1)
                pe.wait_ge(s["ranked"], b * SB + k + 1)
                pe.matmul(dst_ps[j][:, 0:EP], dst_now[:, h, k:k + 1].to_broadcast([EP, EP]),
                          env.ident[0:EP, 0:EP], start=True, stop=True).then_inc(s["dst_wide"], 1)

            with pe.Fori(0, half) as i:
                for h in range(2):
                    b = i * 2 + h
                    pe.wait_ge(s["hot"], b + 1)
                    pe.wait_ge(s["dst_staged"], b + 1)
                    ahead(b, h, 0)
                    ahead(b, h, 1)
                    for k in range(SB):
                        c, j = b * SB + k, (h * SB + k) % 2
                        pe.wait_ge(s["copied"], c + 1)
                        pe.wait_ge(s["heads_ready"], c + 1)
                        pe.matmul(head_ps[j][:, 0:BLKS], hot_lo_t[:, j, :], heads[:, j, :], start=True,
                                  stop=True).then_inc(s["looked"], 1)
                        pe.matmul(taken[:, 0:BLKS], hot_lo[:, h, k, :], hot_hi[:, h, k, :], start=False, stop=True,
                                  skip_group_check=True).then_inc(s["added"], 1)
                        if k + 2 < SB:
                            ahead(b, h, k + 2)

        @block.gpsimd
        def _(pool):
            with pool.Fori(0, half) as i:
                for h in range(2):
                    pool.wait_ge(s["recs_staged"], i * 2 + (h + 1))
                    pool.wait_ge(s["rows_ready"], i * 2 + (h + 1))
                    pool.sem_inc(issued, 1)
                    for k in range(SB):
                        pool.indirect_dma_start(records, bass.IndirectOffsetOnAxis(ap=rows[:, h, k:k + 1], axis=0),
                                                recs[:, h, k, :], None).then_inc(scattered[h], 16)
            for h in range(2):
                pool.wait_ge(scattered[h], half * per_batch)


def load_sorted(env, records):
    nc = env.nc
    with ExitStack() as ctx:
        sb, ps = stage_memory(nc, ctx, "reload")
        rec = sb("rec", [P, TILES, REC], F32)
        dst = sb("dst", [P, TILES], F32)
        base = ps("base", [P, TILES], F32)
        got, dst_ready, wide = (env.sig(f"reload_{n}").sem for n in ("got", "dst_ready", "wide"))
        block = ctx.enter_context(nc.Block())

        @block.sync
        def _(sp):
            sp.dma_start(rec[:, :, :], records.rearrange("(p q) k -> p q k", p=P)).then_inc(got, 16)

        @block.vector
        def _(dve):
            dve.wait_ge(got, 16)
            dve.tensor_copy(dst[:, :], rec[:, :, R_DST]).then_inc(dst_ready, 1)
            dve.tensor_copy(env.win[:, 1:], rec[0:1, :, R_DST])
            dve.tensor_copy(env.src_idx[:, 0:TILES], rec[:, :, R_SRC])
            dve.tensor_copy(env.tab_idx[:, 0:TILES], rec[:, :, R_TAB])
            dve.wait_ge(wide, 1)
            dve.tensor_tensor(env.dst_rel[:, 0:TILES], dst[:, :], base[:, :], ALU.subtract)

        @block.scalar
        def _(act):
            act.wait_ge(got, 16)
            act.copy(env.w[:, 0:TILES], rec[:, :, R_W])
            act.copy(env.w1[:, 0:TILES], rec[:, :, R_W1])
            act.copy(env.start[:, 0:TILES], rec[:, :, R_START])

        @block.tensor
        def _(pe):
            pe.wait_ge(dst_ready, 1)
            for half in range(2):
                cols = slice(half * 512, half * 512 + 512)
                mm = pe.matmul(base[:, cols], env.ones[0:1, :], dst[0:1, cols], start=True, stop=True)
            mm.then_inc(wide, 1)


def relation_weights(env, tag, basis, coeff, weights_dram, weights):
    nc = env.nc
    cols = 512
    chunks = D * D // cols
    with ExitStack() as ctx:
        sb, ps = stage_memory(nc, ctx, tag)
        basis_sb = sb("basis", [BASES, D * D], F32)
        coeff_t = sb("coeff_t", [BASES, P], F32)
        mixed = sb("mixed", [REL, 2, 4 * cols], F32)
        mix_ps = [ps(f"mix{j}", [P, cols], F32) for j in range(4)]
        sig = {n: env.sig(f"relw_{n}") for n in ("loaded", "zeroed", "mixed", "copied", "back")}
        stored = [env.sig(f"relw_stored{h}") for h in range(2)]
        groups = chunks // 4
        block = ctx.enter_context(nc.Block())

        def copy_out(eng, copy, parity):
            for c in range(parity, chunks, 2):
                group, k = c // 4, c % 4
                eng.wait_ge(sig["mixed"].sem, sig["mixed"].at(c + 1))
                if group >= 2 and k == parity:
                    eng.wait_ge(stored[group % 2].sem, stored[group % 2].at(16 * (group // 2)))
                copy(mixed[:, group % 2, k * cols:(k + 1) * cols], mix_ps[c % 4][0:REL, :]).then_inc(sig["copied"].sem, 1)

        @block.vector
        def _(dve):
            dve.memset(coeff_t[:, :], 0.0).then_inc(sig["zeroed"].sem, 1)
            copy_out(dve, dve.tensor_copy, 1)

        @block.scalar
        def _(act):
            copy_out(act, act.copy, 0)

        @block.tensor
        def _(pe):
            pe.wait_ge(sig["loaded"].sem, sig["loaded"].at(32))
            for c in range(chunks):
                if c >= 4 and c % 4 == 0:
                    pe.wait_ge(sig["copied"].sem, sig["copied"].at(c))
                pe.matmul(mix_ps[c % 4][:, :], coeff_t[:, :], basis_sb[:, c * cols:(c + 1) * cols], start=True,
                          stop=True).then_inc(sig["mixed"].sem, 1)

        @block.sync
        def _(sp):
            sp.dma_start(basis_sb[:, :], basis.rearrange("b d f -> b (d f)")).then_inc(sig["loaded"].sem, 16)
            sp.wait_ge(sig["zeroed"].sem, sig["zeroed"].at(1))
            sp.dma_start(coeff_t[:, 0:REL], coeff.rearrange("r b -> b r"),
                         allow_slow_non_contiguous=True).then_inc(sig["loaded"].sem, 16)
            for group in range(groups):
                sp.wait_ge(sig["copied"].sem, sig["copied"].at(4 * group + 4))
                sp.dma_start(weights_dram[:, group * 4 * cols:(group + 1) * 4 * cols],
                             mixed[:, group % 2, :]).then_inc(stored[group % 2].sem, 16)
            for h in range(2):
                sp.wait_ge(stored[h].sem, stored[h].at(16 * groups // 2))
            sp.dma_start(weights[:, :, :], weights_dram.rearrange("r (d f) -> d r f", d=D)).then_inc(sig["back"].sem, 16)
            sp.wait_ge(sig["back"].sem, sig["back"].at(16))

        for name, n in (("loaded", 32), ("zeroed", 1), ("mixed", chunks), ("copied", chunks), ("back", 16)):
            sig[name].passed(n)
        for h in range(2):
            stored[h].passed(16 * groups // 2)


def relation_table(env, tag, weights, table, hidden=None, bias=None):
    nc = env.nc
    cols = 512
    chunks = REL * D // cols
    with ExitStack() as ctx:
        sb, ps = stage_memory(nc, ctx, tag)
        x_now = sb("x_now", [P, 2, D], F32)
        h_t = sb("h_t", [P, 2, P], F32)
        row = sb("row", [P, 2, REL * D], F32)
        bias_sb = sb("bias", [P, 1], F32)
        turn_ps = ps("turn", [P, 512], F32)
        out_ps = [ps(f"out{j}", [P, cols], F32) for j in range(4)]
        names = ("bias_in", "x_staged", "turned", "ready", "made", "out_act", "out_dve")
        sig = {n: env.sig(f"reltab_{n}") for n in names}
        s = {n: v.sem for n, v in sig.items()}
        v = {n: v.at for n, v in sig.items()}
        stored = [env.sig(f"reltab_stored{h}") for h in range(2)]
        rows = table.rearrange("(n r) f -> n (r f)", r=REL)
        block = ctx.enter_context(nc.Block())

        @block.scalar
        def _(act):
            def produce(blk, h):
                act.wait_ge(s["made"], v["made"](blk * chunks + chunks))
                if hidden is None:
                    act.copy(x_now[:, h, :], env.x[:, bass.ds(blk, 1), :]).then_inc(s["x_staged"], 1)
                    act.wait_ge(s["turned"], v["turned"](blk + 1))
                    act.copy(h_t[:, h, :], turn_ps[:, 0:P]).then_inc(s["ready"], 1)
                else:
                    act.activation(h_t[:, h, :], hidden[:, bass.ds(blk * P, P)], ACT.Relu,
                                   bias=bias_sb[:, 0:1]).then_inc(s["ready"], 1)

            act.sem_inc(s["out_act"], 2)
            if hidden is not None:
                act.wait_ge(s["bias_in"], v["bias_in"](16))
            produce(0, 0)
            with act.Fori(0, BLKS // 2) as i:
                for h in range(2):
                    blk = i * 2 + h
                    produce(blk + 1, 1 - h)
                    act.wait_ge(stored[h].sem, (i * 16) + stored[h].at(16))
                    for c in range(0, chunks, 2):
                        act.wait_ge(s["made"], blk * chunks + v["made"](2 * chunks + c + 1))
                        act.copy(row[:, h, c * cols:(c + 1) * cols], out_ps[c % 4][:, :]).then_inc(s["out_act"], 1)

        @block.vector
        def _(dve):
            dve.sem_inc(s["out_dve"], 2)
            with dve.Fori(0, BLKS // 2) as i:
                for h in range(2):
                    blk = i * 2 + h
                    dve.wait_ge(stored[h].sem, (i * 16) + stored[h].at(16))
                    for c in range(1, chunks, 2):
                        dve.wait_ge(s["made"], blk * chunks + v["made"](2 * chunks + c + 1))
                        dve.tensor_copy(row[:, h, c * cols:(c + 1) * cols], out_ps[c % 4][:, :]).then_inc(s["out_dve"], 1)

        @block.tensor
        def _(pe):
            def turn(blk, h):
                pe.wait_ge(s["x_staged"], v["x_staged"](blk + 1))
                pe.transpose(turn_ps[:, 0:P], x_now[:, h, :], env.ident[:, :]).then_inc(s["turned"], 1)

            pe.sem_inc(s["made"], 2 * chunks)
            if hidden is None:
                turn(0, 0)
            with pe.Fori(0, BLKS // 2) as i:
                for h in range(2):
                    blk = i * 2 + h
                    pe.wait_ge(s["ready"], blk + v["ready"](1))
                    if hidden is None:
                        turn(blk + 1, 1 - h)
                    for c in range(chunks):
                        out_name = "out_act" if c % 2 == 0 else "out_dve"
                        pe.wait_ge(s[out_name], blk * (chunks // 2) + v[out_name](c // 2 + 1))
                        pe.matmul(out_ps[c % 4][:, :], h_t[:, h, :],
                                  weights[:, 4 * c:4 * c + 4, :].rearrange("d r f -> d (r f)"),
                                  start=True, stop=True).then_inc(s["made"], 1)

        @block.sync
        def _(sp):
            if hidden is not None:
                sp.dma_start(bias_sb[:, :], bias.rearrange("(f o) -> f o", o=1)).then_inc(s["bias_in"], 16)
            for h in range(2):
                sp.sem_inc(stored[h].sem, 16)
            with sp.Fori(0, BLKS // 2) as i:
                for h in range(2):
                    blk = i * 2 + h
                    sp.wait_ge(s["out_act"], blk * (chunks // 2) + v["out_act"](chunks // 2 + 2))
                    sp.wait_ge(s["out_dve"], blk * (chunks // 2) + v["out_dve"](chunks // 2 + 2))
                    sp.dma_start(rows[bass.ds(blk * P, P), :], row[:, h, :]).then_inc(stored[h].sem, 16)
            for h in range(2):
                sp.wait_ge(stored[h].sem, stored[h].at(16 * (BLKS // 2) + 16))

        turns = BLKS + 1 if hidden is None else 0
        counts = dict(bias_in=16 if hidden is not None else 0, x_staged=turns, turned=turns, ready=BLKS + 1,
                      made=chunks * BLKS + 2 * chunks, out_act=chunks // 2 * BLKS + 2, out_dve=chunks // 2 * BLKS + 2)
        for n in names:
            sig[n].passed(counts[n])
        for h in range(2):
            stored[h].passed(16 * (BLKS // 2) + 16)


def gather_program(pool, env, table, bufs, landed, free, free_at, staged, staged_at):
    with pool.Fori(0, GRPS) as g:
        for k in range(SLOT_BUFS):
            if k % 4 == 0:
                pool.wait_ge(staged, g * 4 + staged_at(k // 4 + 1))
                pool.wait_ge(free, g * SLOT_BUFS + free_at(k + 4))
                pool.sem_inc(env.sig("dma_turn").sem, 1)
            pool.indirect_dma_start(bufs[:, k, :], None, table,
                                    bass.IndirectOffsetOnAxis(ap=env.idx_stage[:, k:k + 1], axis=0)
                                    ).then_inc(landed[k].sem, 16)


def stage_indices(act, env, idx, g, turn, staged):
    cols = slice(4 * turn, 4 * turn + 4)
    act.copy(env.idx_stage[:, cols], idx[:, bass.ds(g * SLOT_BUFS + 4 * turn, 4)]).then_inc(staged, 1)


def window_starts(env, g, late=0):
    return env.nc.values_load_multi_w_load_instructions(
        env.win[0:1, bass.ds(g * SLOT_BUFS + (1 - late), SLOT_BUFS)], engines=[DVE_ENGINE], min_val=0, max_val=N,
        skip_runtime_bounds_check_because="sorted destinations are node numbers")[1]


def sum_over_slots(env, tag, idx, table, weight, acc, degree=False):
    nc = env.nc
    parts = 2 if degree else 1
    with ExitStack() as ctx:
        sb, ps = stage_memory(nc, ctx, tag)
        rows = sb("rows", [P, SLOT_BUFS, D], F32)
        hot = sb("hot", [P, 4, P], F32)
        sums = [ps(f"sums{j}", [P, 512], F32) for j in range(4)]
        landed = [env.sig(f"landed{k}") for k in range(SLOT_BUFS)]
        names = ("idx_staged", "hot_ready", "multiplied", "added")
        sig = {n: env.sig(f"sum_{n}") for n in names}
        s = {n: v.sem for n, v in sig.items()}
        v = {n: v.at for n, v in sig.items()}
        block = ctx.enter_context(nc.Block())

        @block.gpsimd
        def _(pool):
            gather_program(pool, env, table, rows, landed, s["multiplied"], v["multiplied"], s["idx_staged"],
                           v["idx_staged"])

        @block.scalar
        def _(act):
            for turn in range(4):
                stage_indices(act, env, idx, 0, turn, s["idx_staged"])
            with act.Fori(0, GRPS) as g:
                for turn in range(4):
                    act.wait_ge(s["multiplied"], g * SLOT_BUFS + v["multiplied"](SLOT_BUFS + 4 * turn + 4))
                    stage_indices(act, env, idx, g + 1, turn, s["idx_staged"])

        @block.vector
        def _(dve):
            def build(tile, j):
                c = bass.ds(tile, 1)
                dve.tensor_scalar(hot[:, j, :], env.iota_row[:, :], env.dst_rel[:, c], weight[:, c], ALU.is_equal,
                                  ALU.mult).then_inc(s["hot_ready"], 1)

            dve.memset(acc[:, :, :], 0.0)
            dve.drain().then_inc(s["added"], 4)
            for t in range(AHEAD):
                build(t, t)
            with dve.Fori(0, GRPS) as g:
                starts = window_starts(env, g)
                for k in range(SLOT_BUFS):
                    tile = g * SLOT_BUFS + k
                    build(tile + AHEAD, (k + AHEAD) % 4)
                    dve.wait_ge(s["multiplied"], g * SLOT_BUFS + v["multiplied"](SLOT_BUFS + k + 1))
                    window = acc[:, :, bass.ds(starts[k], P)]
                    dve.tensor_tensor(window, window, sums[k % 4][:, 0:parts * P].rearrange("p (a n) -> p a n", a=parts),
                                      ALU.add).then_inc(s["added"], 1)

        @block.tensor
        def _(pe):
            pe.sem_inc(s["multiplied"], SLOT_BUFS)
            with pe.Fori(0, GRPS) as g:
                for k in range(SLOT_BUFS):
                    j = k % 4
                    pe.wait_ge(landed[k].sem, g * 16 + landed[k].at(16))
                    pe.wait_ge(s["hot_ready"], g * SLOT_BUFS + v["hot_ready"](k + 1))
                    pe.wait_ge(s["added"], g * SLOT_BUFS + v["added"](k + 1))
                    mm = pe.matmul(sums[j][:, 0:P], rows[:, k, :], hot[:, j, :], start=True, stop=True)
                    if degree:
                        mm = pe.matmul(sums[j][:, P:2 * P], env.ones[:, :], hot[:, j, :], start=True, stop=True)
                    mm.then_inc(s["multiplied"], 1)

        for n, count in (("idx_staged", 4 * GRPS + 4), ("hot_ready", TILES + AHEAD), ("multiplied", TILES + SLOT_BUFS),
                         ("added", TILES + 4)):
            sig[n].passed(count)
        for k in range(SLOT_BUFS):
            landed[k].passed(16 * GRPS)


def per_node_block(env, tag, from_x, prepare, apply, use, memory):
    nc = env.nc
    with ExitStack() as ctx:
        sb, ps = stage_memory(nc, ctx, tag)
        mem = memory(sb, ps)
        x_now = sb("x_now", [P, 2, D], F32)
        x_t = sb("x_t", [P, 2, P], F32)
        turn_ps = [ps(f"turn{h}", [P, 512], F32) for h in range(2)]
        out_ps = [ps(f"out{h}", [P, 512], F32) for h in range(2)]
        names = ("x_staged", "turned", "prepared", "applied", "used")
        sig = {n: env.sig(f"node_{n}") for n in names}
        s = {n: v.sem for n, v in sig.items()}
        v = {n: v.at for n, v in sig.items()}
        block = ctx.enter_context(nc.Block())

        @block.scalar
        def _(act):
            with act.Fori(0, BLKS // 2) as i:
                for h in range(2):
                    blk = i * 2 + h
                    act.wait_ge(s["applied"], blk + v["applied"](1))
                    if from_x:
                        act.copy(x_now[:, h, :], env.x[:, bass.ds(blk, 1), :]).then_inc(s["x_staged"], 1)
                    last = prepare(act, mem, blk, h)
                    if from_x:
                        act.wait_ge(s["turned"], blk + v["turned"](1))
                        last = act.copy(x_t[:, h, :], turn_ps[h][:, 0:P])
                    last.then_inc(s["prepared"], 1)

        @block.tensor
        def _(pe):
            pe.sem_inc(s["applied"], 2)
            with pe.Fori(0, BLKS // 2) as i:
                for h in range(2):
                    blk = i * 2 + h
                    if from_x:
                        pe.wait_ge(s["x_staged"], blk + v["x_staged"](1))
                        pe.transpose(turn_ps[h][:, 0:P], x_now[:, h, :], env.ident[:, :]).then_inc(s["turned"], 1)
                    pe.wait_ge(s["prepared"], blk + v["prepared"](1))
                    pe.wait_ge(s["used"], blk + v["used"](1))
                    apply(pe, mem, h, x_t[:, h, :], out_ps[h]).then_inc(s["applied"], 1)

        @block.vector
        def _(dve):
            dve.sem_inc(s["used"], 2)
            with dve.Fori(0, BLKS // 2) as i:
                for h in range(2):
                    blk = i * 2 + h
                    dve.wait_ge(s["applied"], blk + v["applied"](3))
                    use(dve, mem, blk, h, out_ps[h]).then_inc(s["used"], 1)

        turns = BLKS if from_x else 0
        for n, count in (("x_staged", turns), ("turned", turns), ("prepared", BLKS), ("applied", BLKS + 2),
                         ("used", BLKS + 2)):
            sig[n].passed(count)


def add_and_measure(env, dve, mem, blk, h, update, scale=None, bias_row=None):
    x_blk = env.x[:, bass.ds(blk, 1), :].rearrange("p o f -> p (o f)")
    if scale is None:
        dve.tensor_tensor(x_blk, x_blk, update, ALU.add)
    else:
        dve.scalar_tensor_tensor(x_blk, update, scale[:, bass.ds(blk, 1)], x_blk, ALU.mult, ALU.add)
    dve.drain()
    if bias_row is not None:
        dve.tensor_tensor(x_blk, x_blk, bias_row, ALU.add)
        dve.drain()
    return dve.bn_stats(env.stats[:, bass.ds(blk, 1), :].rearrange("p o t -> p (o t)"), x_blk)


def normalize(env, tag, store=None):
    nc = env.nc
    measured, rooted, normed, stored = (env.sig(f"norm_{n}") for n in ("measured", "rooted", "normed", "stored"))
    with nc.Block() as block:
        @block.scalar
        def _(act):
            act.wait_ge(measured.sem, measured.at(1))
            act.activation(env.rstd[:, :], env.rstd[:, :], ACT.Sqrt, bias=env.eps[:, 0:1]).then_inc(rooted.sem, 1)

        @block.vector
        def _(dve):
            (even_mean, even_m2), (odd_mean, odd_m2) = ((env.stats[:, :, k + 1], env.stats[:, :, k + 2]) for k in (0, 3))
            dve.tensor_tensor(env.mean[:, :], even_mean, odd_mean, ALU.add)
            dve.tensor_tensor(env.spread[:, :], even_mean, odd_mean, ALU.subtract)
            dve.tensor_tensor(env.rstd[:, :], even_m2, odd_m2, ALU.add)
            dve.drain()
            dve.tensor_scalar(env.mean[:, :], env.mean[:, :], 0.5, None, ALU.mult)
            dve.scalar_tensor_tensor(env.spread[:, :], env.spread[:, :], 0.25, env.spread[:, :], ALU.mult, ALU.mult)
            dve.drain()
            dve.scalar_tensor_tensor(env.rstd[:, :], env.rstd[:, :], 1.0 / D, env.spread[:, :], ALU.mult,
                                     ALU.add).then_inc(measured.sem, 1)
            dve.wait_ge(rooted.sem, rooted.at(1))
            dve.reciprocal(env.rstd[:, :], env.rstd[:, :])
            dve.drain()
            with dve.Fori(0, BLKS // 2) as i:
                for h in range(2):
                    blk = bass.ds(i * 2 + h, 1)
                    x_blk = env.x[:, blk, :].rearrange("p o f -> p (o f)")
                    dve.tensor_scalar(x_blk, x_blk, env.mean[:, blk], env.rstd[:, blk], ALU.subtract,
                                      ALU.mult).then_inc(normed.sem, 1)

        if store is not None:
            @block.sync
            def _(sp):
                sp.wait_ge(normed.sem, normed.at(BLKS))
                count = store(sp, stored.sem)
                sp.wait_ge(stored.sem, stored.at(16 * count))
                stored.passed(16 * count)

    measured.passed(1)
    rooted.passed(1)
    normed.passed(BLKS)


def store_x(env, table):
    def store(sp, stored):
        sp.dma_start(table.rearrange("(b p) f -> p b f", p=P), env.x[:, 0:BLKS, :]).then_inc(stored, 16)
        return 1
    return store


def store_output(env, out):
    def store(sp, stored):
        sp.dma_start(out[0:(BLKS - 1) * P, :].rearrange("(b p) f -> p b f", p=P), env.x[:, 0:BLKS - 1, :]).then_inc(stored, 16)
        sp.dma_start(out[(BLKS - 1) * P:N, :], env.x[0:LAST, BLKS - 1, :]).then_inc(stored, 16)
        return 2
    return store


def relational_layer(env, inp, x_table):
    nc = env.nc
    table = nc.dram_tensor("relation_table", (NPAD * REL, D), F32, kind="Internal").ap()
    weights_dram = nc.dram_tensor("relation_weights", (REL, D * D), F32, kind="Internal").ap()
    with ExitStack() as ctx:
        acc = ctx.enter_context(nc.sbuf_tensor("rel_acc", [P, 1, ACC], F32))
        weights = ctx.enter_context(nc.sbuf_tensor("rel_weights", [P, REL, D], F32))
        relation_weights(env, "relw1", inp["L0_gnn_basis1"], inp["L0_gnn_coeff1"], weights_dram, weights)
        relation_table(env, "reltab1", weights, table)
        relation_weights(env, "relw2", inp["L0_gnn_basis2"], inp["L0_gnn_coeff2"], weights_dram, weights)
        sum_over_slots(env, "relsum1", env.tab_idx, table, env.w1, acc)
        relation_table(env, "reltab2", weights, table, hidden=acc[:, 0, :], bias=inp["L0_gnn_bias1"])
        sum_over_slots(env, "relsum2", env.tab_idx, table, env.w1, acc)
        add_rows(env, "relout", acc, inp["L0_gnn_bias2"])
    normalize(env, "norm0", store_x(env, x_table))


def load_columns(env, tag, pairs):
    sig = env.sig("small_loaded")
    with env.nc.Block() as block:
        @block.sync
        def _(sp):
            for to, frm in pairs:
                sp.dma_start(to, frm, allow_slow_non_contiguous=True).then_inc(sig.sem, 16)
            sp.wait_ge(sig.sem, sig.at(16 * len(pairs)))
    sig.passed(16 * len(pairs))


def add_rows(env, tag, acc, bias):
    with ExitStack() as ctx:
        bias_sb = ctx.enter_context(env.nc.sbuf_tensor(f"{tag}_bias", [P, 1], F32))
        load_columns(env, tag, [(bias_sb[:, :], bias.rearrange("(f o) -> f o", o=1))])

        def memory(sb, ps):
            return {"val": sb("val", [P, 2, P], F32)}

        def prepare(act, mem, blk, h):
            return act.activation(mem["val"][:, h, :], acc[:, 0, bass.ds(blk * P, P)], ACT.Identity, bias=bias_sb[:, 0:1])

        def apply(pe, mem, h, x_t, out):
            return pe.transpose(out[:, 0:P], mem["val"][:, h, :], env.ident[:, :])

        def use(dve, mem, blk, h, out):
            return add_and_measure(env, dve, mem, blk, h, out[:, 0:P])

        per_node_block(env, tag, False, prepare, apply, use, memory)


def gcn_layer(env, inp, x_in):
    nc = env.nc
    with ExitStack() as ctx:
        acc = ctx.enter_context(nc.sbuf_tensor("gcn_acc", [P, 2, ACC], F32))
        weight = ctx.enter_context(nc.sbuf_tensor("gcn_weight", [P, D], F32))
        bias_row = ctx.enter_context(nc.sbuf_tensor("gcn_bias", [P, D], F32))
        dinv = ctx.enter_context(nc.sbuf_tensor("gcn_dinv", [P, BLKS], F32))
        load_columns(env, "gcn", [(weight[:, :], inp["L1_gnn_weight"]),
                                  (bias_row[:, :], inp["L1_gnn_bias"].partition_broadcast(P))])
        sum_over_slots(env, "gcnsum", env.src_idx, x_in, env.w, acc, degree=True)
        with ExitStack() as inner:
            deg_ps = inner.enter_context(nc.psum_tensor("gcn_deg", [P, 512], F32))
            turned, floored, rooted = (env.sig(f"gcn_{n}").sem for n in ("deg_turned", "deg_floored", "deg_rooted"))
            block = inner.enter_context(nc.Block())

            @block.tensor
            def _(pe):
                for b in range(BLKS):
                    mm = pe.matmul(deg_ps[:, b:b + 1], acc[0:1, 1, b * P:(b + 1) * P], env.ones[0:1, 0:1], start=True,
                                   stop=True)
                mm.then_inc(turned, 1)

            @block.vector
            def _(dve):
                dve.wait_ge(turned, 1)
                dve.tensor_scalar(dinv[:, :], deg_ps[:, 0:BLKS], 1.0, None, ALU.max).then_inc(floored, 1)
                dve.wait_ge(rooted, 1)
                dve.reciprocal(dinv[:, :], dinv[:, :])

            @block.scalar
            def _(act):
                act.wait_ge(floored, 1)
                act.activation(dinv[:, :], dinv[:, :], ACT.Sqrt).then_inc(rooted, 1)

        def memory(sb, ps):
            return {"agg": sb("agg", [P, 2, P], F32)}

        def prepare(act, mem, blk, h):
            return act.copy(mem["agg"][:, h, :], acc[:, 0, bass.ds(blk * P, P)])

        def apply(pe, mem, h, x_t, out):
            pe.matmul(out[:, 0:D], x_t, weight[:, :], start=True, stop=False)
            return pe.matmul(out[:, 0:D], mem["agg"][:, h, :], weight[:, :], start=False, stop=True)

        def use(dve, mem, blk, h, out):
            return add_and_measure(env, dve, mem, blk, h, out[:, 0:D], scale=dinv, bias_row=bias_row[:, :])

        per_node_block(env, "gcnout", True, prepare, apply, use, memory)
    normalize(env, "norm1")


def project_nodes(env, tag, from_x, prepare, weights, width, table, scale=None):
    nc = env.nc
    with ExitStack() as ctx:
        rows = ctx.enter_context(nc.sbuf_tensor(f"{tag}_rows", [P, BLKS, width], F32))

        def memory(sb, ps):
            return {"own": None if from_x else sb("own", [P, 2, P], F32)}

        def ready(act, mem, blk, h):
            return None if from_x else prepare(act, mem, blk, h)

        def apply(pe, mem, h, x_t, out):
            return pe.matmul(out[:, 0:width], x_t if from_x else mem["own"][:, h, :], weights[:, 0:width], start=True,
                             stop=True)

        def use(dve, mem, blk, h, out):
            to = rows[:, bass.ds(blk, 1), :].rearrange("p o f -> p (o f)")
            if scale is None:
                return dve.tensor_copy(to, out[:, 0:width])
            return dve.tensor_scalar(to, out[:, 0:width], scale[:, bass.ds(blk, 1)], None, ALU.mult)

        per_node_block(env, tag, from_x, ready, apply, use, memory)
        sig = env.sig("table_stored")
        with nc.Block() as block:
            @block.sync
            def _(sp):
                sp.dma_start(table.rearrange("(b p) f -> p b f", p=P), rows[:, :, :]).then_inc(sig.sem, 16)
                sp.wait_ge(sig.sem, sig.at(16))
        sig.passed(16)


def attention_weights(env, tag, w_in, att_src, att_dst, combined):
    nc = env.nc
    with ExitStack() as ctx:
        sb, ps = stage_memory(nc, ctx, tag)
        att = sb("att", [P, 2], F32)
        load_columns(env, tag, [(combined[:, 0:D], w_in), (att[:, 0:1], att_src.rearrange("h (c o) -> (h c) o", o=1)),
                                (att[:, 1:2], att_dst.rearrange("h (c o) -> (h c) o", o=1))])
        per_head = sb("per_head", [P, 2 * HEADS], F32)
        w_t = sb("w_t", [P, P], F32)
        turn_ps, score_ps = ps("turn", [P, 512], F32), ps("score", [P, 512], F32)
        sig = {n: env.sig(f"att_{n}") for n in ("turned", "copied", "scored")}
        block = ctx.enter_context(nc.Block())

        @block.tensor
        def _(pe):
            pe.transpose(turn_ps[:, 0:P], combined[:, 0:D], env.ident[:, :]).then_inc(sig["turned"].sem, 1)
            pe.wait_ge(sig["copied"].sem, sig["copied"].at(1))
            pe.matmul(score_ps[:, 0:2 * HEADS], w_t[:, :], per_head[:, :], start=True, stop=True).then_inc(sig["scored"].sem, 1)

        @block.vector
        def _(dve):
            for k in range(2):
                dve.tensor_scalar(per_head[:, k * HEADS:(k + 1) * HEADS], env.head_mask[:, :], att[:, k:k + 1], None, ALU.mult)
            dve.wait_ge(sig["turned"].sem, sig["turned"].at(1))
            dve.tensor_copy(w_t[:, :], turn_ps[:, 0:P]).then_inc(sig["copied"].sem, 1)
            dve.wait_ge(sig["scored"].sem, sig["scored"].at(1))
            dve.tensor_copy(combined[:, D:D + 2 * HEADS], score_ps[:, 0:2 * HEADS])

        for n in sig:
            sig[n].passed(1)


def gather_to_stash(env, tag, table, stash, score_src, score_dst):
    nc = env.nc
    width = D + 2 * HEADS
    with ExitStack() as ctx:
        sb, ps = stage_memory(nc, ctx, tag)
        rows = sb("rows", [P, SLOT_BUFS, width], F32)
        scores = sb("scores", [P, 2, 2, CHUNKS, HEADS], F32)
        turn_ps = [[ps(f"turn{h}{k}", [P, 512], F32) for k in range(2)] for h in range(2)]
        landed = [env.sig(f"landed{k}") for k in range(SLOT_BUFS)]
        left = [env.sig(f"stash_left{k}") for k in range(4)]
        names = ("taken", "free", "idx_staged", "turned", "kept")
        sig = {n: env.sig(f"stash_{n}") for n in names}
        s = {n: x.sem for n, x in sig.items()}
        v = {n: x.at for n, x in sig.items()}
        block = ctx.enter_context(nc.Block())

        @block.gpsimd
        def _(pool):
            gather_program(pool, env, table, rows, landed, s["free"], v["free"], s["idx_staged"], v["idx_staged"])

        @block.sync
        def _(sp):
            sp.sem_inc(s["free"], SLOT_BUFS)

            def stash_turn(g, turn):
                sp.wait_ge(s["taken"], g * 4 + v["taken"](turn + 1))
                sp.dma_start(stash[:, bass.ds(g * SLOT_BUFS + 4 * turn, 4), :],
                             rows[:, 4 * turn:4 * turn + 4, 0:D]).then_inc(left[turn].sem, 16)

            def release(g, turn):
                sp.wait_ge(left[turn].sem, g * 16 + left[turn].at(16))
                sp.sem_inc(s["free"], 4)

            stash_turn(0, 0)
            with sp.Fori(0, GRPS - 1) as g:
                for turn in range(4):
                    stash_turn(g + (turn + 1) // 4, (turn + 1) % 4)
                    release(g, turn)
            for turn in range(4):
                if turn < 3:
                    stash_turn(GRPS - 1, turn + 1)
                release(GRPS - 1, turn)

        @block.scalar
        def _(act):
            for turn in range(4):
                stage_indices(act, env, env.src_idx, 0, turn, s["idx_staged"])
            with act.Fori(0, GRPS // 2) as i:
                for h in range(2):
                    g = i * 2 + h
                    act.wait_ge(s["turned"], g + v["turned"](1))
                    for turn in range(4):
                        four = slice(4 * turn, 4 * turn + 4)
                        for k in range(4 * turn, 4 * turn + 4):
                            act.wait_ge(landed[k].sem, g * 16 + landed[k].at(16))
                        act.copy(scores[:, h, 0, four, :], rows[:, four, D:D + HEADS])
                        last = act.copy(scores[:, h, 1, four, :], rows[:, four, D + HEADS:width])
                        last.then_inc(s["taken"], 1)
                        stage_indices(act, env, env.src_idx, g + 1, turn, s["idx_staged"])

        @block.tensor
        def _(pe):
            pe.sem_inc(s["turned"], 2)
            with pe.Fori(0, GRPS // 2) as i:
                for h in range(2):
                    g = i * 2 + h
                    pe.wait_ge(s["taken"], g * 4 + v["taken"](4))
                    pe.wait_ge(s["kept"], g + v["kept"](1))
                    for k in range(2):
                        mm = pe.transpose(turn_ps[h][k][:, 0:P], scores[:, h, k, :, :].rearrange("p c h -> p (c h)"),
                                          env.ident[:, :])
                    mm.then_inc(s["turned"], 1)

        @block.vector
        def _(dve):
            dve.sem_inc(s["kept"], 2)
            with dve.Fori(0, GRPS // 2) as i:
                for h in range(2):
                    g = i * 2 + h
                    dve.wait_ge(s["turned"], g + v["turned"](3))
                    dve.tensor_copy(score_src[:, bass.ds(g * P, P)], turn_ps[h][0][:, 0:P])
                    dve.tensor_copy(score_dst[:, bass.ds(g * P, P)], turn_ps[h][1][:, 0:P]).then_inc(s["kept"], 1)

        for n, count in (("taken", 4 * GRPS), ("free", TILES + SLOT_BUFS), ("idx_staged", 4 * GRPS + 4),
                         ("turned", GRPS + 2), ("kept", GRPS + 2)):
            sig[n].passed(count)
        for k in range(SLOT_BUFS):
            landed[k].passed(16 * GRPS)
        for k in range(4):
            left[k].passed(16 * GRPS)


def segment_flags(env, goes_on, reset, chunk_whole, chunk_reset, chunk_reset_back):
    nc = env.nc
    with ExitStack() as ctx:
        sb, ps = stage_memory(nc, ctx, "flags")
        wide = sb("wide", [P, 2, CHUNKS, HEADS], F32)
        col = sb("col", [P, 3], F32)
        per_chunk = sb("per_chunk", [P, 3, CHUNKS], F32)
        turn_ps = [ps(f"turn{h}", [P, 512], F32) for h in range(2)]
        fold_ps = ps("fold", [P, 512], F32)
        s = {n: env.sig(f"flags_{n}").sem for n in ("wide", "turned", "kept", "first_ready", "shifted", "cols", "folded")}
        block = ctx.enter_context(nc.Block())

        @block.scalar
        def _(act):
            with act.Fori(0, GRPS // 2) as i:
                for h in range(2):
                    g = i * 2 + h
                    act.wait_ge(s["turned"], g + 1)
                    act.copy(wide[:, h, :, :], over_columns(env.start[:, bass.ds(g * CHUNKS, CHUNKS)], HEADS)).then_inc(s["wide"], 1)

        @block.tensor
        def _(pe):
            pe.sem_inc(s["turned"], 2)
            with pe.Fori(0, GRPS // 2) as i:
                for h in range(2):
                    g = i * 2 + h
                    pe.wait_ge(s["wide"], g + 1)
                    pe.wait_ge(s["kept"], g + 1)
                    pe.transpose(turn_ps[h][:, 0:P], wide[:, h, :, :].rearrange("p c h -> p (c h)"),
                                 env.ident[:, :]).then_inc(s["turned"], 1)
            pe.wait_ge(s["cols"], 1)
            pe.matmul(fold_ps[0:HEADS, 0:3 * CHUNKS], env.head_sel[:, :], per_chunk[:, :, :].rearrange("p k c -> p (k c)"),
                      start=True, stop=True).then_inc(s["folded"], 1)

        @block.sync
        def _(sp):
            sp.wait_ge(s["first_ready"], 1)
            sp.dma_start(reset[0:P - HEADS, CHUNK:CHUNK + 1], reset[HEADS:P, 0:1],
                         allow_slow_non_contiguous=True).then_inc(s["shifted"], 16)

        @block.vector
        def _(dve):
            dve.sem_inc(s["kept"], 2)
            dve.memset(reset[:, CHUNK:CHUNK + 1], -BIG)
            with dve.Fori(0, GRPS // 2) as i:
                for h in range(2):
                    g = i * 2 + h
                    cols = bass.ds(g * P, P)
                    dve.wait_ge(s["turned"], g + 3)
                    dve.tensor_scalar(goes_on[:, cols], turn_ps[h][:, 0:P], -1.0, 1.0, ALU.mult, ALU.add)
                    dve.tensor_scalar(reset[:, cols], turn_ps[h][:, 0:P], -BIG, None, ALU.mult).then_inc(s["kept"], 1)
            dve.drain().then_inc(s["first_ready"], 1)
            dve.tensor_reduce(col[:, 0:1], goes_on[:, :], AX_X, ALU.min)
            dve.tensor_reduce(col[:, 1:2], reset[:, 0:CHUNK], AX_X, ALU.min)
            dve.wait_ge(s["shifted"], 16)
            dve.tensor_reduce(col[:, 2:3], reset[:, 1:CHUNK + 1], AX_X, ALU.min)
            dve.drain()
            for k in range(3):
                last = dve.tensor_scalar(per_chunk[:, k, :], env.chunk_mask[:, :], col[:, k:k + 1], None, ALU.mult)
            last.then_inc(s["cols"], 1)
            dve.wait_ge(s["folded"], 1)
            for k, to in enumerate((chunk_whole, chunk_reset, chunk_reset_back)):
                dve.tensor_copy(to[:, :], fold_ps[0:HEADS, k * CHUNKS:(k + 1) * CHUNKS])


def softmax_numerators(env, tag, score_src, score_dst, goes_on, reset, chunk_flags):
    nc = env.nc
    chunk_whole, chunk_reset, chunk_reset_back = chunk_flags
    with ExitStack() as ctx:
        sb, ps = stage_memory(nc, ctx, tag)
        work = sb("work", [P, CHUNK], F32)
        per_chunk = sb("per_chunk", [P, CHUNKS], F32)
        ends = sb("ends", [HEADS, CHUNKS], F32)
        carried = sb("carried", [HEADS, CHUNKS + 1], F32)
        picked = sb("picked", [P, CHUNKS], F32)
        entry = sb("entry", [P, 1], F32)
        fold_ps, spread_ps = ps("fold", [P, 512], F32), ps("spread", [P, 512], F32)
        names = ("spread_in", "folded", "carried", "spread", "shifted", "exped")
        sig = {n: env.sig(f"soft_{n}") for n in names}
        s = {n: x.sem for n, x in sig.items()}
        v = {n: x.at for n, x in sig.items()}
        block = ctx.enter_context(nc.Block())

        @block.tensor
        def _(pe):
            for k in range(3):
                pe.wait_ge(s["spread_in"], v["spread_in"](k + 1))
                pe.matmul(fold_ps[0:HEADS, 0:CHUNKS], env.head_sel[:, :], per_chunk[:, :], start=True, stop=True).then_inc(s["folded"], 1)
                pe.wait_ge(s["carried"], v["carried"](k + 1))
                entries = carried[:, 0:CHUNKS] if k < 2 else carried[:, 1:CHUNKS + 1]
                pe.matmul(spread_ps[:, 0:CHUNKS], env.head_sel_t[:, :], entries, start=True, stop=True).then_inc(s["spread"], 1)

        @block.vector
        def _(dve):
            def carry(k, end, through, op0, op1, nothing):
                dve.drain()
                dve.tensor_scalar(per_chunk[:, :], env.chunk_mask[:, :], end, None, ALU.mult).then_inc(s["spread_in"], 1)
                dve.memset(carried[:, 0:1] if k < 2 else carried[:, CHUNKS:CHUNKS + 1], nothing)
                dve.wait_ge(s["folded"], v["folded"](k + 1))
                dve.tensor_copy(ends[:, :], fold_ps[0:HEADS, 0:CHUNKS])
                dve.drain()
                if k < 2:
                    dve.tensor_tensor_scan(carried[:, 1:CHUNKS + 1], through[:, :], ends[:, :], nothing, op0,
                                           op1).then_inc(s["carried"], 1)
                else:
                    dve.tensor_tensor_scan(carried[:, 0:CHUNKS][:, ::-1], through[:, ::-1], ends[:, ::-1], nothing, op0,
                                           op1).then_inc(s["carried"], 1)
                dve.wait_ge(s["spread"], v["spread"](k + 1))
                dve.tensor_tensor_reduce(picked[:, :], spread_ps[:, 0:CHUNKS], env.chunk_mask[:, :], 1.0, 0.0, ALU.mult,
                                         ALU.add, entry[:, 0:1])
                dve.drain()

            dve.scalar_tensor_tensor(score_dst[:, :], goes_on[:, :], 1.0, score_dst[:, :], ALU.subtract, ALU.mult)
            dve.drain()
            dve.tensor_tensor_scan(work[:, :], goes_on[:, :], score_dst[:, :], 0.0, ALU.mult, ALU.add)
            carry(0, work[:, CHUNK - 1:CHUNK], chunk_whole, ALU.mult, ALU.add, 0.0)
            dve.tensor_tensor_scan(work[:, :], goes_on[:, :], score_dst[:, :], entry[:, 0:1], ALU.mult, ALU.add)
            dve.drain()
            dve.tensor_tensor(score_src[:, :], score_src[:, :], work[:, :], ALU.subtract)
            dve.drain()
            dve.scalar_tensor_tensor(score_src[:, :], score_src[:, :], 0.2, score_src[:, :], ALU.mult, ALU.max)
            dve.drain()
            dve.tensor_tensor_scan(work[:, :], reset[:, 0:CHUNK], score_src[:, :], -BIG, ALU.add, ALU.max)
            carry(1, work[:, CHUNK - 1:CHUNK], chunk_reset, ALU.add, ALU.max, -BIG)
            dve.tensor_tensor_scan(work[:, :], reset[:, 0:CHUNK], score_src[:, :], entry[:, 0:1], ALU.add, ALU.max)
            dve.drain()
            back, out = reset[:, 1:CHUNK + 1][:, ::-1], score_dst[:, :][:, ::-1]
            dve.tensor_tensor_scan(out, back, work[:, :][:, ::-1], -BIG, ALU.add, ALU.max)
            carry(2, score_dst[:, 0:1], chunk_reset_back, ALU.add, ALU.max, -BIG)
            dve.tensor_tensor_scan(out, back, work[:, :][:, ::-1], entry[:, 0:1], ALU.add, ALU.max)
            dve.drain()
            dve.tensor_tensor(score_src[:, :], score_src[:, :], score_dst[:, :], ALU.subtract).then_inc(s["shifted"], 1)

        @block.scalar
        def _(act):
            act.wait_ge(s["shifted"], v["shifted"](1))
            act.activation(score_src[:, :], score_src[:, :], ACT.Exp).then_inc(s["exped"], 1)

        for n, count in (("spread_in", 3), ("folded", 3), ("carried", 3), ("spread", 3), ("shifted", 1), ("exped", 1)):
            sig[n].passed(count)


def attend(env, tag, stash, numer, acc):
    nc = env.nc
    with ExitStack() as ctx:
        sb, ps = stage_memory(nc, ctx, tag)
        rows = sb("rows", [P, SLOT_BUFS, D], F32)
        p_row = sb("p_row", [P, 2, P], F32)
        p_col = sb("p_col", [P, 2, CHUNKS, HEADS], F32)
        wide = sb("wide", [P, 4, HEADS, CH], F32)
        scaled = sb("scaled", [P, 4, HEADS, CH], F32)
        hot = sb("hot", [P, 4, P], F32)
        turn_ps = [ps(f"turn{h}", [P, 512], F32) for h in range(2)]
        sums = [ps(f"sums{j}", [P, 512], F32) for j in range(4)]
        back = [env.sig(f"attend_back{k}") for k in range(4)]
        names = ("p_staged", "turned", "p_ready", "wide_ready", "scaled_ready", "hot_ready", "multiplied", "added")
        sig = {n: env.sig(f"attend_{n}") for n in names}
        s = {n: x.sem for n, x in sig.items()}
        v = {n: x.at for n, x in sig.items()}
        block = ctx.enter_context(nc.Block())

        @block.sync
        def _(sp):
            with sp.Fori(0, GRPS) as g:
                for turn in range(4):
                    sp.wait_ge(s["multiplied"], g * SLOT_BUFS + v["multiplied"](4 * turn + 4))
                    sp.dma_start(rows[:, 4 * turn:4 * turn + 4, :],
                                 stash[:, bass.ds(g * SLOT_BUFS + 4 * turn, 4), :]).then_inc(back[turn].sem, 16)

        @block.scalar
        def _(act):
            def numerators(g, h):
                act.wait_ge(s["multiplied"], g * SLOT_BUFS + v["multiplied"](1))
                act.copy(p_row[:, h, :], numer[:, bass.ds(g * P, P)]).then_inc(s["p_staged"], 1)
                act.wait_ge(s["turned"], g + v["turned"](1))
                act.copy(p_col[:, h, :, :].rearrange("p c h -> p (c h)"), turn_ps[h][:, 0:P]).then_inc(s["p_ready"], 1)
                act.wait_ge(s["p_ready"], g + v["p_ready"](1))

            def widen(tile, h, k):
                act.wait_ge(s["multiplied"], tile + v["multiplied"](SLOT_BUFS - 3))
                act.copy(wide[:, k % 4, :, :], over_columns(p_col[:, h, k, :], CH)).then_inc(s["wide_ready"], 1)

            with act.Fori(0, GRPS // 2) as i:
                for h in range(2):
                    numerators(i * 2 + h, h)
                    for k in range(SLOT_BUFS):
                        widen(i * (2 * SLOT_BUFS) + (h * SLOT_BUFS + k), h, k)

        @block.gpsimd
        def _(pool):
            with pool.Fori(0, GRPS // 2) as i:
                for h in range(2):
                    for k in range(SLOT_BUFS):
                        tile = i * (2 * SLOT_BUFS) + (h * SLOT_BUFS + k)
                        if k % 4 == 0:
                            pool.wait_ge(back[k // 4].sem, (i * 2 + h) * 16 + back[k // 4].at(16))
                        pool.wait_ge(s["wide_ready"], tile + v["wide_ready"](1))
                        pool.tensor_tensor(scaled[:, k % 4, :, :], rows[:, k, :].rearrange("p (h c) -> p h c", h=HEADS),
                                           wide[:, k % 4, :, :], ALU.mult).then_inc(s["scaled_ready"], 1)

        @block.vector
        def _(dve):
            def build(tile, j):
                dve.tensor_scalar(hot[:, j, :], env.iota_row[:, :], env.dst_rel[:, bass.ds(tile, 1)], None,
                                  ALU.is_equal).then_inc(s["hot_ready"], 1)

            dve.memset(acc[:, :, :], 0.0)
            dve.drain().then_inc(s["added"], 4)
            for t in range(AHEAD):
                build(t, t)
            with dve.Fori(0, GRPS) as g:
                starts = window_starts(env, g)
                for k in range(SLOT_BUFS):
                    build(g * SLOT_BUFS + (k + AHEAD), (k + AHEAD) % 4)
                    dve.wait_ge(s["multiplied"], g * SLOT_BUFS + v["multiplied"](SLOT_BUFS + k + 1))
                    window = acc[:, :, bass.ds(starts[k], P)]
                    dve.tensor_tensor(window, window, sums[k % 4][:, 0:2 * P].rearrange("p (a n) -> p a n", a=2),
                                      ALU.add).then_inc(s["added"], 1)

        @block.tensor
        def _(pe):
            def turn(g, h):
                pe.wait_ge(s["p_staged"], g + v["p_staged"](1))
                pe.transpose(turn_ps[h][:, 0:P], p_row[:, h, :], env.ident[:, :]).then_inc(s["turned"], 1)

            pe.sem_inc(s["multiplied"], SLOT_BUFS)
            with pe.Fori(0, GRPS // 2) as i:
                for h in range(2):
                    g = i * 2 + h
                    turn(g, h)
                    for k in range(SLOT_BUFS):
                        tile, j = i * (2 * SLOT_BUFS) + (h * SLOT_BUFS + k), k % 4
                        pe.wait_ge(s["scaled_ready"], tile + v["scaled_ready"](1))
                        pe.wait_ge(s["hot_ready"], tile + v["hot_ready"](1))
                        pe.wait_ge(s["added"], tile + v["added"](1))
                        pe.matmul(sums[j][:, 0:P], scaled[:, j, :, :].rearrange("p h c -> p (h c)"), hot[:, j, :],
                                  start=True, stop=True)
                        pe.matmul(sums[j][:, P:2 * P], wide[:, j, :, :].rearrange("p h c -> p (h c)"), hot[:, j, :],
                                  start=True, stop=True).then_inc(s["multiplied"], 1)

        for n, count in (("p_staged", GRPS), ("turned", GRPS), ("p_ready", GRPS), ("wide_ready", TILES),
                         ("scaled_ready", TILES), ("hot_ready", TILES + AHEAD), ("multiplied", TILES + SLOT_BUFS),
                         ("added", TILES + 4)):
            sig[n].passed(count)
        for k in range(4):
            back[k].passed(16 * GRPS)


def divide_sums(env, acc):
    with env.nc.Block() as block:
        @block.vector
        def _(dve):
            dve.tensor_scalar(acc[:, 1, 0:NPAD], acc[:, 1, 0:NPAD], 1e-30, None, ALU.max)
            dve.drain()
            dve.reciprocal(acc[:, 1, 0:NPAD], acc[:, 1, 0:NPAD])
            dve.drain()
            dve.tensor_tensor(acc[:, 0, 0:NPAD], acc[:, 0, 0:NPAD], acc[:, 1, 0:NPAD], ALU.mult)


def gat_layer(env, inp):
    nc = env.nc
    width = D + 2 * HEADS
    table = nc.dram_tensor("gat_table", (NPAD, width), F32, kind="Internal").ap()
    stash = nc.dram_tensor("gat_stash", (P, TILES, D), F32, kind="Internal").ap()
    with ExitStack() as ctx:
        def sb(name, shape, dt):
            return ctx.enter_context(nc.sbuf_tensor(f"gat_{name}", shape, dt))

        goes_on = sb("goes_on", [P, CHUNK], BF16)
        reset = sb("reset", [P, CHUNK + 1], BF16)
        chunk_flags = [sb(n, [HEADS, CHUNKS], F32) for n in ("chunk_whole", "chunk_reset", "chunk_reset_back")]
        combined = sb("combined", [P, width], F32)
        bias = sb("bias", [P, 1], F32)
        segment_flags(env, goes_on, reset, *chunk_flags)
        numer = sb("numer", [P, CHUNK], F32)
        attention_weights(env, "gat1w", inp["L2_gnn_W1"], inp["L2_gnn_as1"], inp["L2_gnn_ad1"], combined)
        project_nodes(env, "gat1tab", True, None, combined, width, table)
        for n in (1, 2):
            with ExitStack() as inner:
                score_dst = inner.enter_context(nc.sbuf_tensor(f"gat{n}_score_dst", [P, CHUNK], F32))
                gather_to_stash(env, f"gat{n}gather", table, stash, numer, score_dst)
                softmax_numerators(env, f"gat{n}soft", numer, score_dst, goes_on, reset, chunk_flags)
            with ExitStack() as inner:
                acc = inner.enter_context(nc.sbuf_tensor(f"gat{n}_acc", [P, 2, ACC], F32))
                attend(env, f"gat{n}sum", stash, numer, acc)
                divide_sums(env, acc)
                if n == 1:
                    load_columns(env, "gat1bias", [(bias[:, :], inp["L2_gnn_b1"].rearrange("(f o) -> f o", o=1))])
                    attention_weights(env, "gat2w", inp["L2_gnn_W2"], inp["L2_gnn_as2"], inp["L2_gnn_ad2"], combined)

                    def hidden(act, mem, blk, h, acc=acc):
                        return act.activation(mem["own"][:, h, :], acc[:, 0, bass.ds(blk * P, P)], ACT.Relu, bias=bias[:, 0:1])

                    project_nodes(env, "gat2tab", False, hidden, combined, width, table)
                else:
                    add_rows(env, "gatout", acc, inp["L2_gnn_b2"])
    normalize(env, "norm2")


def tensor_weights(env, inp, wy, w_out, fc1, w2):
    nc = env.nc
    mix, keep = math.cos(math.pi / 8.0), math.sin(math.pi / 8.0)
    fan, fan_two, neighbors = math.sqrt(MUL), math.sqrt(2 * MUL), math.sqrt(16.0)
    edge_part = mix / (fan_two * neighbors)
    scales = (keep / fan, edge_part, edge_part, edge_part / math.sqrt(3.0))
    with ExitStack() as ctx:
        sb, ps = stage_memory(nc, ctx, "tpw")
        wy_in = sb("wy_in", [P, D], F32)
        w_in = sb("w_in", [P, 4, 4, MUL], F32)
        fc2_in = sb("fc2_in", [HID, 4 * MUL], F32)
        zeroed, loaded = env.sig("tpw_zeroed").sem, env.sig("tpw_loaded").sem
        block = ctx.enter_context(nc.Block())

        @block.sync
        def _(sp):
            def vectors(m):
                return slice(MUL + m, D, 3)

            l20, l21 = inp["L3_gnn_W_l20"], inp["L3_gnn_W_l21"]
            loads = [(wy_in[0:MUL, 0:MUL], inp["L3_gnn_W_l10"]), (w_in[0:MUL, 0, 0, :], inp["L3_gnn_W_sc0"]),
                     (w_in[0:MUL, 1, 0, :], l20[0:MUL, :]), (fc2_in[:, :], inp["L3_gnn_W_fc2"])]
            for m in range(3):
                lo = MUL + MUL * m
                loads += [(wy_in[vectors(m), lo:lo + MUL], inp["L3_gnn_W_l11"]),
                          (w_in[vectors(m), 0, 1 + m, :], inp["L3_gnn_W_sc1"]),
                          (w_in[lo:lo + MUL, 1, 1 + m, :], l21[MUL:2 * MUL, :]),
                          (w_in[MUL * m:MUL * (m + 1), 2, 1 + m, :], l21[0:MUL, :]),
                          (w_in[MUL * m:MUL * (m + 1), 3, 0, :], l20[MUL:2 * MUL, :])]
            for i in range(8):
                loads.append((fc1[LEN * i:LEN * (i + 1), i, :], inp["L3_gnn_W_fc1"]))
            sp.wait_ge(zeroed, 1)
            for to, frm in loads:
                sp.dma_start(to, frm).then_inc(loaded, 16)
            sp.wait_ge(loaded, 16 * len(loads))
            sp.sem_inc(zeroed, 1)

        @block.vector
        def _(dve):
            dve.memset(wy_in[:, :], 0.0)
            dve.memset(w_in[:, :, :, :], 0.0)
            dve.memset(fc1[:, :, :], 0.0)
            dve.drain().then_inc(zeroed, 1)
            dve.wait_ge(zeroed, 2)
            dve.tensor_scalar(wy[:, :], wy_in[:, :], 1.0 / fan, None, ALU.mult)
            for i, scale in enumerate(scales):
                dve.tensor_scalar(w_out[:, i, 0:MUL], w_in[:, i, 0, :], scale, None, ALU.mult)
                dve.tensor_scalar(w_out[:, i, MUL:D].rearrange("p (w m) -> p m w", m=3), w_in[:, i, 1:4, :], scale, None,
                                  ALU.mult)
            norm = 1.0 / math.sqrt(HID)
            for to, frm in ((0, 0), (1, 2), (2, 2), (3, 2), (4, 1), (5, 3)):
                dve.tensor_scalar(w2[:, to * MUL:(to + 1) * MUL], fc2_in[:, frm * MUL:(frm + 1) * MUL], norm, None, ALU.mult)


def convolve(env, tag, table, records, fc1, w2, acc):
    nc = env.nc
    vec = 3 * MUL
    octets, turns = 2 * GRPS, 4 * GRPS
    with ExitStack() as ctx:
        sb, ps = stage_memory(nc, ctx, tag)
        rec = sb("rec", [P, TILES + SLOT_BUFS, REC], F32)
        rows = sb("rows", [P, SLOT_BUFS, D], F32)
        hot = sb("hot", [P, 4, P], F32)
        message = sb("message", [P, 4, D + 2 * vec], F32)
        lens = sb("lens", [P, 2, 8, LEN], F32)
        lens_t = sb("lens_t", [8 * LEN, 2, P], F32)
        hidden = sb("hidden", [HID, 2, 4, P], F32)
        lens_ps = ps("lens_ps", [P, 512], F32)
        hidden_ps = ps("hidden_ps", [P, 512], F32)
        w_ps = [ps(f"w{j}", [P, 2, 256], F32) for j in range(2)]
        sums = [ps(f"sums{j}", [P, 512], F32) for j in range(4)]
        landed = [env.sig(f"landed{k}") for k in range(SLOT_BUFS)]
        names = ("loaded", "tail_zeroed", "idx_staged", "lens_staged", "lens_turned", "lens_ready", "hidden_made",
                 "hidden_ready", "w_made", "hot_ready", "message_ready", "multiplied", "added")
        s = {n: env.sig(f"conv_{n}").sem for n in names}
        block = ctx.enter_context(nc.Block())

        @block.sync
        def _(sp):
            sp.dma_start(rec[:, 0:TILES, :], records.rearrange("(p q) k -> p q k", p=P)).then_inc(s["loaded"], 16)

        @block.gpsimd
        def _(pool):
            gather_program(pool, env, table, rows, landed, s["multiplied"], lambda n: n, s["idx_staged"], lambda n: n)

        @block.scalar
        def _(act):
            def stage_lens(octet, u):
                act.copy(lens[:, u, :, :], rec[:, bass.ds(octet * 8, 8), R_LEN:REC]).then_inc(s["lens_staged"], 1)

            def keep_lens(octet, u):
                act.wait_ge(s["lens_turned"], octet + 1)
                act.copy(lens_t[:, u, :], lens_ps[0:8 * LEN, u * P:(u + 1) * P]).then_inc(s["lens_ready"], 1)

            def activate(turn, h):
                act.wait_ge(s["hidden_made"], turn + 1)
                act.activation(hidden[:, h, :, :].rearrange("p k e -> p (k e)"), hidden_ps[0:HID, :], ACT.Silu,
                               scale=1.0 / math.sqrt(LEN)).then_inc(s["hidden_ready"], 1)

            for turn in range(4):
                stage_indices(act, env, env.src_idx, 0, turn, s["idx_staged"])
            act.wait_ge(s["loaded"], 16)
            act.wait_ge(s["tail_zeroed"], 1)
            stage_lens(0, 0)
            stage_lens(1, 1)
            keep_lens(0, 0)
            activate(0, 0)
            with act.Fori(0, GRPS) as g:
                for t in range(4):
                    if t % 2 == 0:
                        octet, u = g * 2 + t // 2, t // 2
                        keep_lens(octet + 1, 1 - u)
                        stage_lens(octet + 2, u)
                    act.wait_ge(s["w_made"], g * (SLOT_BUFS // 2) + (2 * t + 2))
                    activate(g * 4 + (t + 1), (t + 1) % 2)
                    act.wait_ge(s["multiplied"], g * SLOT_BUFS + (SLOT_BUFS + 4 * t + 4))
                    stage_indices(act, env, env.src_idx, g + 1, t, s["idx_staged"])

        @block.vector
        def _(dve):
            def build(tile, j):
                dve.tensor_scalar(hot[:, j, :], env.iota_row[:, :], env.dst_rel[:, bass.ds(tile, 1)], None,
                                  ALU.is_equal).then_inc(s["hot_ready"], 1)

            dve.memset(rec[:, TILES:, :], 0.0).then_inc(s["tail_zeroed"], 1)
            dve.memset(acc[:, :, :], 0.0)
            for j in range(4):
                dve.memset(sums[j][:, :], 0.0)
            dve.drain().then_inc(s["added"], 4)
            dve.wait_ge(s["loaded"], 16)
            for t in range(2):
                build(t, t)
            with dve.Fori(0, GRPS) as g:
                starts = window_starts(env, g, late=1)
                for k in range(SLOT_BUFS):
                    tile, j = g * SLOT_BUFS + k, k % 4
                    build(tile + 2, (k + 2) % 4)
                    dve.wait_ge(landed[k].sem, g * 16 + landed[k].at(16))
                    dve.wait_ge(s["w_made"], g * (SLOT_BUFS // 2) + (k // 2 + 3))
                    w = w_ps[k // 2 % 2][:, k % 2, :]

                    def attr(m):
                        return rec[:, bass.ds(tile, 1), R_EA + m:R_EA + m + 1].rearrange("p o k -> p (o k)")

                    dve.scalar_tensor_tensor(message[:, j, 0:D], w[:, 0:D], attr(0), rows[:, k, :], ALU.mult, ALU.mult)
                    by_block = rows[:, k, :].rearrange("p (b u) -> p b u", b=4)
                    for m in range(3):
                        to = message[:, j, D:].rearrange("p (i m u) -> p m i u", i=2, m=3)[:, m, :, :]
                        last = dve.scalar_tensor_tensor(to, w[:, D:D + 2 * MUL].rearrange("p (i u) -> p i u", i=2), attr(1 + m),
                                                        by_block[:, 0:m + 2:m + 1, :], ALU.mult, ALU.mult)
                    last.then_inc(s["message_ready"], 1)
                    dve.wait_ge(s["multiplied"], tile + SLOT_BUFS)
                    window = acc[:, :, bass.ds(starts[k], P)]
                    dve.tensor_tensor(window, window, sums[(k - 1) % 4][:, 0:3 * P].rearrange("p (a n) -> p a n", a=3),
                                      ALU.add).then_inc(s["added"], 1)
            assert SLOTS - (N + E) >= P

        @block.tensor
        def _(pe):
            def turn_lens(octet, u):
                pe.wait_ge(s["lens_staged"], octet + 1)
                pe.transpose(lens_ps[0:8 * LEN, u * P:(u + 1) * P], lens[:, u, :, :].rearrange("p k l -> p (k l)"),
                             env.ident[:, :]).then_inc(s["lens_turned"], 1)

            def make_hidden(octet, u, half):
                pe.wait_ge(s["lens_ready"], octet + 1)
                for i in range(4):
                    mm = pe.matmul(hidden_ps[0:HID, i * P:(i + 1) * P], fc1[:, 4 * half + i, :], lens_t[:, u, :], start=True,
                                   stop=True)
                mm.then_inc(s["hidden_made"], 1)

            def make_w(first):
                for k in (first, first + 1):
                    mm = pe.matmul(w_ps[k // 2 % 2][:, k % 2, 0:D + 2 * MUL], hidden[:, k // 4 % 2, k % 4, :], w2[:, :],
                                   start=True, stop=True)
                mm.then_inc(s["w_made"], 1)

            pe.sem_inc(s["multiplied"], SLOT_BUFS)
            pe.sem_inc(s["w_made"], 2)
            turn_lens(0, 0)
            make_hidden(0, 0, 0)
            pe.wait_ge(s["hidden_ready"], 1)
            make_w(0)
            with pe.Fori(0, GRPS) as g:
                for k in range(SLOT_BUFS):
                    t, j, tile = k // 4, k % 4, g * SLOT_BUFS + k
                    octet, u = g * 2 + t // 2, t // 2
                    if k % 8 == 0:
                        turn_lens(octet + 1, 1 - u)
                    if k % 4 == 0:
                        if t % 2 == 0:
                            make_hidden(octet, u, 1)
                        else:
                            make_hidden(octet + 1, 1 - u, 0)
                    if k % 4 == 2:
                        pe.wait_ge(s["hidden_ready"], g * 4 + (t + 2))
                    if k % 2 == 0:
                        make_w(k + 2)
                    pe.wait_ge(s["hot_ready"], tile + 1)
                    pe.wait_ge(s["message_ready"], tile + 1)
                    pe.wait_ge(s["added"], tile + 1)
                    pe.matmul(sums[j][:, 0:P], message[:, j, 0:D], hot[:, j, :], start=True, stop=True)
                    for i in range(2):
                        mm = pe.matmul(sums[j][0:vec, (i + 1) * P:(i + 2) * P], message[:, j, D + i * vec:D + (i + 1) * vec],
                                       hot[:, j, :], start=True, stop=True)
                    mm.then_inc(s["multiplied"], 1)

        for k in range(SLOT_BUFS):
            landed[k].passed(16 * GRPS)


def tensor_layer(env, inp, records, out):
    nc = env.nc
    table = nc.dram_tensor("tensor_table", (NPAD, D), F32, kind="Internal").ap()
    with ExitStack() as ctx:
        def sb(name, shape):
            return ctx.enter_context(nc.sbuf_tensor(f"tp_{name}", shape, F32))

        attr = sb("attr", [P, BLKS])
        wy, w_out = sb("wy", [P, D]), sb("w_out", [P, 4, D])
        fc1, w2 = sb("fc1", [8 * LEN, 8, HID]), sb("w2", [HID, D + 2 * MUL])
        tensor_weights(env, inp, wy, w_out, fc1, w2)
        with nc.Block() as block:
            @block.vector
            def _(dve):
                dve.memset(attr[:, :], 0.0)
        whole = (BLKS - 1) * P
        load_columns(env, "attr", [(attr[:, 0:BLKS - 1], inp["node_vec1"][0:whole, :].rearrange("(b p) o -> p (b o)", p=P)),
                                   (attr[0:LAST, BLKS - 1:BLKS], inp["node_vec1"][whole:N, :])])
        project_nodes(env, "tptab", True, None, wy, D, table, scale=attr)
        acc = ctx.enter_context(nc.sbuf_tensor("tp_acc", [P, 3, ACC], F32))
        convolve(env, "conv", table, records, fc1, w2, acc)

        def memory(sb, ps):
            return {"sums": sb("sums", [P, 2, 3, P], F32)}

        def prepare(act, mem, blk, h):
            return act.copy(mem["sums"][:, h, :, :], acc[:, :, bass.ds(blk * P, P)])

        def apply(pe, mem, h, x_t, out):
            pe.matmul(out[:, 0:D], x_t, w_out[:, 0, :], start=True, stop=False)
            for i in range(3):
                mm = pe.matmul(out[:, 0:D], mem["sums"][:, h, i, :], w_out[:, 1 + i, :], start=False, stop=i == 2)
            return mm

        def use(dve, mem, blk, h, out):
            return add_and_measure(env, dve, mem, blk, h, out[:, 0:D], scale=attr)

        per_node_block(env, "tpout", True, prepare, apply, use, memory)
    normalize(env, "norm3", store_output(env, out))


def build(nc, inp, out):
    with ExitStack() as ctx:
        env = Env(nc, ctx)
        records = nc.dram_tensor("records", (SLOTS, REC), F32, kind="Internal").ap()
        x_table = nc.dram_tensor("x_table", (NPAD, D), F32, kind="Internal").ap()
        setup(env, inp)
        sort_edges(env, inp, records)
        load_sorted(env, records)
        relational_layer(env, inp, x_table)
        gcn_layer(env, inp, x_table)
        gat_layer(env, inp)
        tensor_layer(env, inp, records, out)


def kernel(**inputs):
    import numpy as _np
    import concourse.bacc as _bacc
    from concourse import mybir as _mybir
    from concourse.bass_utils import run_bass_kernel_spmd as _run

    nc = _bacc.Bacc("TRN2", target_bir_lowering=False, num_devices=1)
    arrays, inp = {}, {}
    for name, value in inputs.items():
        a = _np.ascontiguousarray(value)
        arrays[f"in_{name}_dram"] = a
        inp[name] = nc.dram_tensor(f"in_{name}_dram", a.shape, _mybir.dt.from_np(a.dtype), kind="ExternalInput").ap()
    out = nc.dram_tensor("out_0_dram", (N, D), F32, kind="ExternalOutput").ap()
    build(nc, inp, out)
    r = _run(nc, [arrays], core_ids=[0])
    return r.results[0]["out_0_dram"]
```

```python
from contextlib import ExitStack
import math

import concourse.bass as bass
from concourse import mybir

F32 = mybir.dt.float32
BF16 = mybir.dt.bfloat16
I32 = mybir.dt.int32
ALU = mybir.AluOpType
ACT = mybir.ActivationFunctionType
AX_X = mybir.AxisListType.X
DVE_ENGINE = mybir.EngineType.DVE

P = 128
N, E, D = 3750, 123750, 128
REL, BASES = 32, 8
HEADS, CH = 8, 16
MUL, HID, LEN = 32, 100, 10
BLKS = -(-N // P)
NPAD = BLKS * P
LAST = N - (BLKS - 1) * P
ACC = NPAD + P

SLOT_BUFS = 16
PHASES = 3
GRPS = -(-(N + E) // (P * SLOT_BUFS * PHASES)) * PHASES
TILES = SLOT_BUFS * GRPS
SLOTS = TILES * P

EP, EC = 125, 990
assert EP * EC == E
SB = 15
SBATCHES = EC // SB
REC = 20
R_SRC, R_TAB, R_DST, R_W, R_W1, R_START, R_EA, R_LEN = 0, 1, 2, 3, 4, 5, 6, 10
FIRSTS = -(-TILES // P)
AHEAD = 3
BIG = 1e30
EPS = 1e-5


class Signal:

    def __init__(self, sem):
        self.sem, self.base = sem, 0

    def at(self, n):
        return self.base + n

    def passed(self, n):
        self.base += n


class Env:

    def __init__(self, nc, ctx, till_last):
        self.nc, self.ctx, self.till_last, self.signals = nc, ctx, till_last, {}

    def sig(self, name):
        if name not in self.signals:
            self.signals[name] = Signal(self.ctx.enter_context(self.nc.semaphore(name)))
        return self.signals[name]

    def keep(self, name, shape, dt, ctx=None):
        t = (ctx or self.ctx).enter_context(self.nc.sbuf_tensor(name, shape, dt))
        return t


def stage_memory(nc, ctx, tag):
    def sb(name, shape, dt):
        return ctx.enter_context(nc.sbuf_tensor(f"{tag}_{name}", shape, dt))

    def ps(name, shape, dt):
        return ctx.enter_context(nc.psum_tensor(f"{tag}_{name}", shape, dt))

    return sb, ps


def over_columns(ap, count):
    return ap.unsqueeze(2).to_broadcast([ap.shape[0], ap.shape[1], count])


def over_rows(ap, count):
    return ap.unsqueeze(1).to_broadcast([ap.shape[0], count, ap.shape[1]])


def setup(env, inp):
    nc = env.nc
    env.ident = env.keep("ident", [P, P], F32)
    env.ident_bf = env.keep("ident_bf", [P, P], BF16)
    env.iota_bf = env.keep("iota_bf", [P, P], BF16)
    env.iota_row = env.keep("iota_row", [P, P], F32)
    env.above = env.keep("above", [P, P], F32)
    env.below = env.keep("below", [P, P], F32)
    env.ones = env.keep("ones", [P, P], F32)
    env.tile_mask = env.keep("tile_mask", [P, SLOT_BUFS], F32)
    env.head_mask = env.keep("head_mask", [P, HEADS], F32)
    env.head_sel = env.keep("head_sel", [P, HEADS], F32)
    env.head_sel_t = env.keep("head_sel_t", [HEADS, P], F32)
    env.head_rows = env.keep("head_rows", [P, P], F32)
    env.tile_sel = env.keep("tile_sel", [P, SLOT_BUFS], F32)
    env.other_tile = env.keep("other_tile", [P, SLOT_BUFS], F32)
    env.first_idx = env.keep("first_idx", [P, FIRSTS], I32)
    env.x = env.keep("x", [P, BLKS + 1, D], F32)
    env.stats = env.keep("stats", [P, BLKS, 6], F32)
    env.mean = env.keep("mean", [P, BLKS], F32)
    env.spread = env.keep("spread", [P, BLKS], F32)
    env.rstd = env.keep("rstd", [P, BLKS], F32)
    env.eps = env.keep("eps", [P, 1], F32)
    env.src_idx = env.keep("src_idx", [P, TILES + PHASES * SLOT_BUFS], I32)
    env.dst_rel = env.keep("dst_rel", [P, TILES + SLOT_BUFS], F32)
    env.win = env.keep("win", [1, 2 + TILES], I32)
    env.idx_stage = env.keep("idx_stage", [P, SLOT_BUFS], I32)
    env.tab_idx = env.keep("tab_idx", [P, TILES + SLOT_BUFS], I32, env.till_last)
    env.w = env.keep("w", [P, TILES + SLOT_BUFS], F32, env.till_last)
    env.w1 = env.keep("w1", [P, TILES + SLOT_BUFS], F32, env.till_last)
    env.start = env.keep("start", [P, TILES + SLOT_BUFS], F32, env.till_last)
    zeroed, consts, x_in = env.sig("x_zeroed"), env.sig("consts"), env.sig("x_loaded")
    sel_t, stepped = env.sig("sel_transposed"), env.sig("const_step")
    with ExitStack() as ctx:
        sb, ps = stage_memory(nc, ctx, "setup")
        pt = ps("pt", [P, 512], F32)
        block = ctx.enter_context(nc.Block())

        @block.gpsimd
        def _(pool):
            pool.memset(env.ident[:, :], 0.0)
            pool.memset(env.above[:, :], 1.0)
            pool.memset(env.below[:, :], 1.0)
            pool.memset(env.ones[:, :], 1.0)
            pool.memset(env.tile_mask[:, :], 1.0)
            pool.memset(env.head_mask[:, :], 1.0)
            pool.memset(env.eps[:, :], EPS)
            pool.iota(env.iota_row[:, :], pattern=[[1, P]], base=0, channel_multiplier=0,
                      allow_small_or_imprecise_dtypes=True).then_inc(stepped.sem, 1)
            pool.wait_ge(stepped.sem, 1)
            pool.affine_select(out=env.ident[:, :], in_=env.ident[:, :], compare_op=ALU.not_equal,
                               fill=1.0, base=0, pattern=[[-1, P]], channel_multiplier=1)
            pool.affine_select(out=env.above[:, :], in_=env.above[:, :], compare_op=ALU.is_gt,
                               fill=0.0, base=0, pattern=[[1, P]], channel_multiplier=-1)
            pool.affine_select(out=env.below[:, :], in_=env.below[:, :], compare_op=ALU.is_gt,
                               fill=0.0, base=0, pattern=[[-1, P]], channel_multiplier=1)
            for mask, width, count in ((env.tile_mask, HEADS, SLOT_BUFS), (env.head_mask, CH, HEADS)):
                pool.affine_select(out=mask[:, :], in_=mask[:, :], compare_op=ALU.is_ge, fill=0.0,
                                   base=0, pattern=[[-width, count]], channel_multiplier=1)
            pool.memset(env.win[:, 0:2], N)
            pool.memset(env.idx_stage[:, :], 0).then_inc(stepped.sem, 1)
            pool.wait_ge(stepped.sem, 2)
            for mask, width, count in ((env.tile_mask, HEADS, SLOT_BUFS), (env.head_mask, CH, HEADS)):
                pool.affine_select(out=mask[:, :], in_=mask[:, :], compare_op=ALU.is_ge, fill=0.0,
                                   base=width - 1, pattern=[[width, count]],
                                   channel_multiplier=-1).then_inc(consts.sem, 1)

        @block.vector
        def _(dve):
            dve.memset(env.x[:, BLKS - 1:, :], 0.0).then_inc(zeroed.sem, 1)
            for t, fill in ((env.src_idx, 0), (env.tab_idx, 0), (env.dst_rel, 200.0), (env.w, 0.0),
                            (env.w1, 0.0), (env.start, 0.0)):
                dve.memset(t[:, TILES:], fill)
            dve.wait_ge(consts.sem, 2)
            dve.tensor_copy(env.ident_bf[:, :], env.ident[:, :])
            dve.tensor_copy(env.iota_bf[:, :], env.iota_row[:, :])
            dve.tensor_scalar(env.other_tile[:, :], env.tile_mask[:, :], BIG, -BIG, ALU.mult, ALU.add)
            dve.tensor_reduce(env.tile_sel[:, :], env.ident[:, :].rearrange("p (c k) -> p k c", k=SLOT_BUFS),
                              AX_X, ALU.add)
            dve.tensor_reduce(env.head_sel[:, :], env.ident[:, :].rearrange("p (c h) -> p h c", h=HEADS),
                              AX_X, ALU.add).then_inc(consts.sem, 1)
            dve.wait_ge(sel_t.sem, 1)
            dve.tensor_copy(env.head_sel_t[:, :], pt[0:HEADS, 0:P])
            dve.tensor_copy(env.head_rows[:, :].rearrange("p (h c) -> p h c", c=CH), over_columns(env.head_sel[:, :], CH))

        @block.tensor
        def _(pe):
            pe.wait_ge(consts.sem, 3)
            pe.transpose(pt[0:HEADS, 0:P], env.head_sel[:, :], env.ident[:, :]).then_inc(sel_t.sem, 1)

        @block.sync
        def _(sp):
            sp.dma_start(env.x[:, 0:BLKS - 1, :],
                         inp["x"][0:(BLKS - 1) * P, :].rearrange("(b p) f -> p b f", p=P)).then_inc(x_in.sem, 16)
            sp.wait_ge(zeroed.sem, 1)
            sp.dma_start(env.x[0:LAST, BLKS - 1, :], inp["x"][(BLKS - 1) * P:N, :]).then_inc(x_in.sem, 16)
            sp.wait_ge(x_in.sem, 32)


def slot_rows(dve, rows_out, at, low, tile_no):
    dve.tensor_scalar(low, at, P - 1, None, ALU.bitwise_and)
    dve.tensor_scalar(tile_no, at, 7, None, ALU.arith_shift_right)
    dve.drain()
    return dve.scalar_tensor_tensor(rows_out, low, float(TILES), tile_no, ALU.mult, ALU.add)


def one_hot(dve, env, hot_lo, hot_hi, lo, hi, b, h, k):
    c = bass.ds(b * SB + k, 1)
    dve.tensor_scalar(hot_lo[:, h, k, :], env.iota_bf[0:EP, :], lo[:, c], None, ALU.is_equal)
    return dve.tensor_scalar(hot_hi[:, h, k, :], env.iota_bf[0:EP, 0:BLKS], hi[:, c], None, ALU.is_equal)


def sort_edges(env, inp, records):
    assert P == 128
    nc = env.nc
    with ExitStack() as ctx:
        sb, ps = stage_memory(nc, ctx, "sort")
        src_i = sb("src_i", [EP, EC], I32)
        dst_i = sb("dst_i", [EP, EC], I32)
        typ_i = sb("typ_i", [EP, EC], I32)
        tab_f = sb("tab_f", [EP, EC], F32)
        dst_f = sb("dst_f", [EP, EC], F32)
        lo_i = sb("lo_i", [EP, EC], I32)
        hi_i = sb("hi_i", [EP, EC], I32)
        lo = sb("lo", [EP, EC + SB], F32)
        hi = sb("hi", [EP, EC + SB], F32)
        w_in = sb("w_in", [EP, EC], F32)
        w1_in = sb("w1_in", [EP, EC], F32)
        ea_in = sb("ea_in", [EP, EC, 4], F32)
        len_in = sb("len_in", [EP, EC, LEN], F32)
        hot_lo = sb("hot_lo", [EP, 2, SB, P], BF16)
        hot_hi = sb("hot_hi", [EP, 2, SB, BLKS], BF16)
        zero_lo = sb("zero_lo", [EP, P], BF16)
        count1 = sb("count1", [P, BLKS], F32)
        totals = sb("totals", [P, BLKS], F32)
        cum = sb("cum", [P, BLKS], F32)
        zeros = sb("zeros", [P, BLKS], F32)
        first = sb("first", [P, BLKS], F32)
        next_slot = sb("next_slot", [P, BLKS], F32)
        node_i = sb("node_i", [P, BLKS, 3], I32)
        node_row = sb("node_row", [P, BLKS], I32)
        node_rec = sb("node_rec", [P, BLKS, REC], F32)
        pad_rec = sb("pad_rec", [P, TILES - (N + E) // P, REC], F32)
        recs = sb("recs", [EP, 2, SB, REC], F32)
        sigs = {n: env.sig(f"sort_{n}") for n in (
            "loaded", "prepared", "hot", "counted", "summed", "count1_ready", "node_rows", "node_recs",
            "self_written", "pads_written", "first_ready")}
        s = {n: v.sem for n, v in sigs.items()}

        with ExitStack() as inner:
            cnt = inner.enter_context(nc.psum_tensor("sort_cnt", [P, 512], F32))
            sums = inner.enter_context(nc.psum_tensor("sort_sums", [P, 512], F32))
            block = inner.enter_context(nc.Block())

            @block.sync
            def _(sp):
                for tile, name in ((dst_i, "dst"), (src_i, "src"), (typ_i, "edge_type_32"), (w_in, "edge_weight")):
                    sp.dma_start(tile[:, :], inp[name].rearrange("(p c) -> p c", c=EC)).then_inc(s["loaded"], 16)
                sp.dma_start(w1_in[:, :], inp["edge_weight1"].rearrange("(p c) o -> p (c o)", c=EC)).then_inc(s["loaded"], 16)
                sp.dma_start(ea_in[:, :, :], inp["edge_attr_4"].rearrange("(p c) k -> p c k", c=EC)).then_inc(s["loaded"], 16)
                sp.dma_start(len_in[:, :, :], inp["edge_attr_10"].rearrange("(p c) k -> p c k", c=EC)).then_inc(s["loaded"], 16)
                sp.wait_ge(s["loaded"], 7 * 16)
                sp.wait_ge(s["node_recs"], 2)
                lane, tile0 = (N + E) % P, (N + E) // P
                assert lane and tile0 + 1 < TILES
                rows = records.rearrange("(p q) k -> p q k", p=P)
                sp.dma_start(rows[:, tile0 + 1:TILES, :], pad_rec[:, 1:, :]).then_inc(s["pads_written"], 16)
                sp.dma_start(rows[lane:P, tile0, :], pad_rec[lane:P, 0, :]).then_inc(s["pads_written"], 16)
                sp.wait_ge(s["pads_written"], 32)

            @block.vector
            def _(dve):
                dve.memset(zero_lo[:, :], 0.0)
                dve.memset(zeros[:, :], 0.0)
                dve.memset(lo[:, EC:], 0.0)
                dve.memset(hi[:, EC:], 0.0)
                dve.memset(recs[:, :, :, :], 0.0)
                dve.wait_ge(s["loaded"], 7 * 16)
                dve.tensor_scalar(lo_i[:, :], dst_i[:, :], P - 1, None, ALU.bitwise_and)
                dve.tensor_scalar(hi_i[:, :], dst_i[:, :], 7, None, ALU.arith_shift_right)
                dve.drain()
                dve.tensor_copy(lo[:, 0:EC], lo_i[:, :])
                dve.tensor_copy(hi[:, 0:EC], hi_i[:, :])
                dve.tensor_copy(dst_f[:, :], dst_i[:, :])
                dve.tensor_copy(tab_f[:, :], typ_i[:, :])
                dve.drain()
                dve.scalar_tensor_tensor(tab_f[:, :], src_i[:, :], float(REL), tab_f[:, :], ALU.mult,
                                         ALU.add).then_inc(s["prepared"], 1)
                dve.drain()
                with dve.Fori(0, SBATCHES // 2) as i:
                    for h in range(2):
                        b = i * 2 + h
                        dve.wait_ge(s["counted"], b + 1)
                        for k in range(SB):
                            last = one_hot(dve, env, hot_lo, hot_hi, lo, hi, b, h, k)
                        last.then_inc(s["hot"], 1)
                dve.wait_ge(s["counted"], SBATCHES + 3)
                dve.tensor_scalar(count1[:, :], cnt[:, 0:BLKS], 1.0, None, ALU.add).then_inc(s["count1_ready"], 1)
                dve.wait_ge(s["summed"], 1)
                dve.tensor_copy(totals[:, :], sums[:, BLKS:2 * BLKS])
                dve.drain()
                dve.tensor_tensor_scan(cum[:, :], zeros[:, :], totals[:, :], 0.0, ALU.add, ALU.add)
                dve.drain()
                dve.tensor_tensor(cum[:, :], cum[:, :], totals[:, :], ALU.subtract)
                dve.drain()
                dve.tensor_tensor(first[:, :], cum[:, :], sums[:, 0:BLKS], ALU.add)
                dve.drain()
                dve.tensor_scalar(next_slot[:, :], first[:, :], 1.0, None, ALU.add)
                dve.tensor_copy(node_i[:, :, 0], first[:, :])
                dve.drain()
                slot_rows(dve, node_row[:, :], *(node_i[:, :, k] for k in range(3))).then_inc(s["node_rows"], 1)

            @block.tensor
            def _(pe):
                pe.wait_ge(s["prepared"], 1)
                pe.matmul(cnt[:, 0:BLKS], zero_lo[:, :], zero_lo[:, 0:BLKS], start=True, stop=True,
                          skip_group_check=True).then_inc(s["counted"], 2)
                with pe.Fori(0, SBATCHES // 2) as i:
                    for h in range(2):
                        pe.wait_ge(s["hot"], i * 2 + h + 1)
                        for k in range(SB):
                            mm = pe.matmul(cnt[:, 0:BLKS], hot_lo[:, h, k, :], hot_hi[:, h, k, :], start=False,
                                           stop=False, skip_group_check=True)
                        mm.then_inc(s["counted"], 1)
                pe.matmul(cnt[:, 0:BLKS], zero_lo[:, :], zero_lo[:, 0:BLKS], start=False, stop=True,
                          skip_group_check=True).then_inc(s["counted"], 1)
                pe.wait_ge(s["count1_ready"], 1)
                pe.matmul(sums[:, 0:BLKS], env.above[:, :], count1[:, :], start=True, stop=True)
                pe.matmul(sums[:, BLKS:2 * BLKS], env.ones[:, :], count1[:, :], start=True,
                          stop=True).then_inc(s["summed"], 1)

            @block.gpsimd
            def _(pool):
                pool.memset(node_rec[:, :, :], 0.0)
                pool.memset(pad_rec[:, :, :], 0.0).then_inc(s["node_recs"], 1)
                pool.wait_ge(s["node_recs"], 1)
                pool.memset(node_rec[:, :, R_START:R_START + 1], 1.0)
                for col, mult in ((R_SRC, 1), (R_DST, 1), (R_TAB, REL)):
                    pool.iota(node_rec[:, :, col], pattern=[[P * mult, BLKS]], base=0, channel_multiplier=mult,
                              allow_small_or_imprecise_dtypes=True)
                pool.memset(pad_rec[:, :, R_DST:R_DST + 1], float(N))
                pool.memset(pad_rec[:, :, R_START:R_START + 1], 1.0).then_inc(s["node_recs"], 1)
                pool.wait_ge(s["node_recs"], 2)
                pool.wait_ge(s["node_rows"], 1)
                for b in range(BLKS):
                    m = P if b < BLKS - 1 else LAST
                    pool.indirect_dma_start(records, bass.IndirectOffsetOnAxis(ap=node_row[0:m, b:b + 1], axis=0),
                                            node_rec[0:m, b, :], None).then_inc(s["self_written"], 16)
                pool.wait_ge(s["self_written"], 16 * BLKS)

        dst_now = sb("dst_now", [EP, 2, SB], F32)
        hot_lo_t = sb("hot_lo_t", [P, 2, EP], F32)
        heads = sb("heads", [P, 2, BLKS], F32)
        same = sb("same", [EP, 2, EP], F32)
        own_head = sb("own_head", [EP, BLKS], F32)
        in_column = sb("in_column", [EP, SB], F32)
        before = sb("before", [EP, SB], F32)
        slot_i = sb("slot_i", [EP, 3, SB], I32)
        rows = sb("rows", [EP, 2, SB], I32)
        taken = ps("taken", [P, 512], F32)
        hot_ps = [ps(f"hot_ps{j}", [P, 1024], BF16) for j in range(2)]
        dst_ps = [ps(f"dst_ps{j}", [EP, 512], F32) for j in range(2)]
        head_ps = [ps(f"head_ps{j}", [EP, 512], F32) for j in range(2)]
        s = {n: env.sig(f"rank_{n}").sem for n in (
            "hot", "dst_staged", "recs_staged", "turned", "copied", "dst_wide", "ranked", "heads_ready",
            "looked", "added", "rows_ready")}
        scattered = [env.sig(f"rank_scattered{h}").sem for h in range(2)]
        issued = env.sig("dma_turn").sem
        block = ctx.enter_context(nc.Block())
        half = SBATCHES // 2
        per_batch = 16 * SB

        @block.scalar
        def _(act):
            def batch(i, h):
                b = i * 2 + h
                cols = bass.ds(b * SB, SB)
                if not (isinstance(i, int) and i == 0):
                    act.wait_ge(scattered[h], i * per_batch)
                act.copy(dst_now[:, h, :], dst_f[:, cols]).then_inc(s["dst_staged"], 1)
                for k in range(SB):
                    j = (h * SB + k) % 2
                    act.wait_ge(s["turned"], b * SB + k + 1)
                    act.wait_ge(s["looked"], b * SB + k + 1)
                    act.copy(hot_lo_t[:, j, :], hot_ps[j][:, 0:EP]).then_inc(s["copied"], 1)
                act.copy(recs[:, h, :, R_SRC], src_i[:, cols])
                act.copy(recs[:, h, :, R_TAB], tab_f[:, cols])
                act.copy(recs[:, h, :, R_DST], dst_f[:, cols])
                act.copy(recs[:, h, :, R_W], w_in[:, cols])
                act.copy(recs[:, h, :, R_W1], w1_in[:, cols])
                act.copy(recs[:, h, :, R_EA:R_EA + 4], ea_in[:, cols, :])
                act.copy(recs[:, h, :, R_LEN:R_LEN + LEN], len_in[:, cols, :]).then_inc(s["recs_staged"], 1)

            for h in range(2):
                batch(0, h)
            with act.Fori(1, half) as i:
                for h in range(2):
                    batch(i, h)

        @block.vector
        def _(dve):
            dve.sem_inc(s["ranked"], 2)
            for k in range(SB):
                last = one_hot(dve, env, hot_lo, hot_hi, lo, hi, 0, 0, k)
            last.then_inc(s["hot"], 1)

            def batch(i, h):
                b = i * 2 + h
                for k in range(SB):
                    c, j = b * SB + k, (h * SB + k) % 2
                    dve.wait_ge(s["added"], c + 1)
                    dve.tensor_tensor(heads[:, j, :], taken[:, 0:BLKS], next_slot[:, :],
                                      ALU.add).then_inc(s["heads_ready"], 1)
                    ahead = one_hot(dve, env, hot_lo, hot_hi, lo, hi, b + 1, 1 - h, k)
                    dve.wait_ge(s["dst_wide"], c + 1)
                    dve.scalar_tensor_tensor(same[:, j, :], dst_ps[j][:, 0:EP], dst_now[:, h, k:k + 1],
                                             env.below[0:EP, 0:EP], ALU.is_equal, ALU.mult,
                                             accum_out=in_column[:, k:k + 1]).then_inc(s["ranked"], 1)
                    dve.wait_ge(s["looked"], c + 3)
                    dve.tensor_tensor_reduce(own_head[:, :], head_ps[j][:, 0:BLKS], hot_hi[:, h, k, :], 1.0, 0.0,
                                             ALU.mult, ALU.add, before[:, k:k + 1])
                ahead.then_inc(s["hot"], 1)
                dve.drain()
                if not (isinstance(i, int) and i == 0):
                    dve.wait_ge(scattered[h], i * per_batch)
                dve.tensor_tensor(slot_i[:, 0, :], in_column[:, :], before[:, :], ALU.add)
                dve.drain()
                slot_rows(dve, rows[:, h, :], *(slot_i[:, m, :] for m in range(3))).then_inc(s["rows_ready"], 1)

            for h in range(2):
                batch(0, h)
            with dve.Fori(1, half) as i:
                for h in range(2):
                    batch(i, h)

        @block.tensor
        def _(pe):
            pe.sem_inc(s["looked"], 2)
            pe.matmul(taken[:, 0:BLKS], zero_lo[:, :], zero_lo[:, 0:BLKS], start=True, stop=True,
                      skip_group_check=True).then_inc(s["added"], 1)

            def ahead(b, h, k):
                j = (h * SB + k) % 2
                pe.transpose(hot_ps[j][:, 0:EP], hot_lo[:, h, k, :], env.ident_bf[0:EP, 0:EP]).then_inc(s["turned"], 1)
                pe.wait_ge(s["ranked"], b * SB + k + 1)
                pe.matmul(dst_ps[j][:, 0:EP], dst_now[:, h, k:k + 1].to_broadcast([EP, EP]),
                          env.ident[0:EP, 0:EP], start=True, stop=True).then_inc(s["dst_wide"], 1)

            with pe.Fori(0, half) as i:
                for h in range(2):
                    b = i * 2 + h
                    pe.wait_ge(s["hot"], b + 1)
                    pe.wait_ge(s["dst_staged"], b + 1)
                    ahead(b, h, 0)
                    ahead(b, h, 1)
                    for k in range(SB):
                        c, j = b * SB + k, (h * SB + k) % 2
                        pe.wait_ge(s["copied"], c + 1)
                        pe.wait_ge(s["heads_ready"], c + 1)
                        pe.matmul(head_ps[j][:, 0:BLKS], hot_lo_t[:, j, :], heads[:, j, :], start=True,
                                  stop=True).then_inc(s["looked"], 1)
                        pe.matmul(taken[:, 0:BLKS], hot_lo[:, h, k, :], hot_hi[:, h, k, :], start=False, stop=True,
                                  skip_group_check=True).then_inc(s["added"], 1)
                        if k + 2 < SB:
                            ahead(b, h, k + 2)

        @block.gpsimd
        def _(pool):
            with pool.Fori(0, half) as i:
                for h in range(2):
                    pool.wait_ge(s["recs_staged"], i * 2 + (h + 1))
                    pool.wait_ge(s["rows_ready"], i * 2 + (h + 1))
                    pool.sem_inc(issued, 1)
                    for k in range(SB):
                        pool.indirect_dma_start(records, bass.IndirectOffsetOnAxis(ap=rows[:, h, k:k + 1], axis=0),
                                                recs[:, h, k, :], None).then_inc(scattered[h], 16)
            for h in range(2):
                pool.wait_ge(scattered[h], half * per_batch)


def load_sorted(env, records):
    nc = env.nc
    with ExitStack() as ctx:
        sb, ps = stage_memory(nc, ctx, "reload")
        rec = sb("rec", [P, TILES, REC], F32)
        dst = sb("dst", [P, FIRSTS * P], F32)
        base = ps("base", [P, 1024], F32)
        firsts = ps("firsts", [P, 512], F32)
        got, dst_ready, wide = (env.sig(f"reload_{n}").sem for n in ("got", "dst_ready", "wide"))
        block = ctx.enter_context(nc.Block())

        @block.sync
        def _(sp):
            sp.dma_start(rec[:, :, :], records.rearrange("(p q) k -> p q k", p=P)).then_inc(got, 16)

        @block.vector
        def _(dve):
            dve.memset(dst[:, TILES:], 0.0)
            dve.wait_ge(got, 16)
            dve.tensor_copy(dst[:, 0:TILES], rec[:, :, R_DST]).then_inc(dst_ready, 1)
            dve.tensor_copy(env.win[:, 2:], rec[0:1, :, R_DST])
            dve.tensor_copy(env.src_idx[:, 0:TILES], rec[:, :, R_SRC])
            dve.tensor_copy(env.tab_idx[:, 0:TILES], rec[:, :, R_TAB])
            dve.wait_ge(wide, 1)
            dve.tensor_tensor(env.dst_rel[:, 0:TILES], dst[:, 0:TILES], base[:, 0:TILES], ALU.subtract)
            dve.tensor_copy(env.first_idx[:, :], firsts[:, 0:FIRSTS])

        @block.scalar
        def _(act):
            act.wait_ge(got, 16)
            act.copy(env.w[:, 0:TILES], rec[:, :, R_W])
            act.copy(env.w1[:, 0:TILES], rec[:, :, R_W1])
            act.copy(env.start[:, 0:TILES], rec[:, :, R_START])

        @block.tensor
        def _(pe):
            pe.wait_ge(dst_ready, 1)
            assert FIRSTS * P == 1024
            for half in range(2):
                cols = slice(half * 512, half * 512 + 512)
                pe.matmul(base[:, cols], env.ones[0:1, :], dst[0:1, cols], start=True, stop=True)
            for j in range(FIRSTS):
                mm = pe.matmul(firsts[:, j:j + 1], dst[0:1, j * P:(j + 1) * P], env.ones[0:1, 0:1], start=True, stop=True)
            mm.then_inc(wide, 1)


def relation_weights(env, tag, basis, coeff, weights_dram, weights):
    nc = env.nc
    cols = 512
    chunks = D * D // cols
    with ExitStack() as ctx:
        sb, ps = stage_memory(nc, ctx, tag)
        basis_sb = sb("basis", [BASES, D * D], F32)
        coeff_t = sb("coeff_t", [BASES, P], F32)
        mixed = sb("mixed", [REL, 2, 4 * cols], F32)
        mix_ps = [ps(f"mix{j}", [P, cols], F32) for j in range(4)]
        sig = {n: env.sig(f"relw_{n}") for n in ("loaded", "zeroed", "mixed", "copied", "back")}
        stored = [env.sig(f"relw_stored{h}") for h in range(2)]
        groups = chunks // 4
        block = ctx.enter_context(nc.Block())

        def copy_out(eng, copy, parity):
            for c in range(parity, chunks, 2):
                group, k = c // 4, c % 4
                eng.wait_ge(sig["mixed"].sem, sig["mixed"].at(c + 1))
                if group >= 2 and k == parity:
                    eng.wait_ge(stored[group % 2].sem, stored[group % 2].at(16 * (group // 2)))
                copy(mixed[:, group % 2, k * cols:(k + 1) * cols], mix_ps[c % 4][0:REL, :]).then_inc(sig["copied"].sem, 1)

        @block.vector
        def _(dve):
            dve.memset(coeff_t[:, :], 0.0).then_inc(sig["zeroed"].sem, 1)
            copy_out(dve, dve.tensor_copy, 1)

        @block.scalar
        def _(act):
            copy_out(act, act.copy, 0)

        @block.tensor
        def _(pe):
            pe.wait_ge(sig["loaded"].sem, sig["loaded"].at(32))
            for c in range(chunks):
                if c >= 4 and c % 4 == 0:
                    pe.wait_ge(sig["copied"].sem, sig["copied"].at(c))
                pe.matmul(mix_ps[c % 4][:, :], coeff_t[:, :], basis_sb[:, c * cols:(c + 1) * cols], start=True,
                          stop=True).then_inc(sig["mixed"].sem, 1)

        @block.sync
        def _(sp):
            sp.dma_start(basis_sb[:, :], basis.rearrange("b d f -> b (d f)")).then_inc(sig["loaded"].sem, 16)
            sp.wait_ge(sig["zeroed"].sem, sig["zeroed"].at(1))
            sp.dma_start(coeff_t[:, 0:REL], coeff.rearrange("r b -> b r"),
                         allow_slow_non_contiguous=True).then_inc(sig["loaded"].sem, 16)
            for group in range(groups):
                sp.wait_ge(sig["copied"].sem, sig["copied"].at(4 * group + 4))
                sp.dma_start(weights_dram[:, group * 4 * cols:(group + 1) * 4 * cols],
                             mixed[:, group % 2, :]).then_inc(stored[group % 2].sem, 16)
            for h in range(2):
                sp.wait_ge(stored[h].sem, stored[h].at(16 * groups // 2))
            sp.dma_start(weights[:, :, :], weights_dram.rearrange("r (d f) -> d r f", d=D)).then_inc(sig["back"].sem, 16)
            sp.wait_ge(sig["back"].sem, sig["back"].at(16))

        for name, n in (("loaded", 32), ("zeroed", 1), ("mixed", chunks), ("copied", chunks), ("back", 16)):
            sig[name].passed(n)
        for h in range(2):
            stored[h].passed(16 * groups // 2)


def relation_table(env, tag, weights, table, hidden=None, bias=None):
    nc = env.nc
    cols = 512
    chunks = REL * D // cols
    with ExitStack() as ctx:
        sb, ps = stage_memory(nc, ctx, tag)
        x_now = sb("x_now", [P, 2, D], F32)
        h_t = sb("h_t", [P, 2, P], F32)
        row = sb("row", [P, 2, REL * D], F32)
        bias_sb = sb("bias", [P, 1], F32)
        turn_ps = ps("turn", [P, 512], F32)
        out_ps = [ps(f"out{j}", [P, cols], F32) for j in range(4)]
        names = ("bias_in", "x_staged", "turned", "ready", "made", "out_act", "out_dve")
        sig = {n: env.sig(f"reltab_{n}") for n in names}
        s = {n: v.sem for n, v in sig.items()}
        v = {n: v.at for n, v in sig.items()}
        stored = [env.sig(f"reltab_stored{h}") for h in range(2)]
        rows = table.rearrange("(n r) f -> n (r f)", r=REL)
        block = ctx.enter_context(nc.Block())

        @block.scalar
        def _(act):
            def produce(blk, h):
                act.wait_ge(s["made"], v["made"](blk * chunks + chunks))
                if hidden is None:
                    act.copy(x_now[:, h, :], env.x[:, bass.ds(blk, 1), :]).then_inc(s["x_staged"], 1)
                    act.wait_ge(s["turned"], v["turned"](blk + 1))
                    act.copy(h_t[:, h, :], turn_ps[:, 0:P]).then_inc(s["ready"], 1)
                else:
                    act.activation(h_t[:, h, :], hidden[:, bass.ds(blk * P, P)], ACT.Relu,
                                   bias=bias_sb[:, 0:1]).then_inc(s["ready"], 1)

            act.sem_inc(s["out_act"], 2)
            if hidden is not None:
                act.wait_ge(s["bias_in"], v["bias_in"](16))
            produce(0, 0)
            with act.Fori(0, BLKS // 2) as i:
                for h in range(2):
                    blk = i * 2 + h
                    produce(blk + 1, 1 - h)
                    act.wait_ge(stored[h].sem, (i * 16) + stored[h].at(16))
                    for c in range(0, chunks, 2):
                        act.wait_ge(s["made"], blk * chunks + v["made"](2 * chunks + c + 1))
                        act.copy(row[:, h, c * cols:(c + 1) * cols], out_ps[c % 4][:, :]).then_inc(s["out_act"], 1)

        @block.vector
        def _(dve):
            dve.sem_inc(s["out_dve"], 2)
            with dve.Fori(0, BLKS // 2) as i:
                for h in range(2):
                    blk = i * 2 + h
                    dve.wait_ge(stored[h].sem, (i * 16) + stored[h].at(16))
                    for c in range(1, chunks, 2):
                        dve.wait_ge(s["made"], blk * chunks + v["made"](2 * chunks + c + 1))
                        dve.tensor_copy(row[:, h, c * cols:(c + 1) * cols], out_ps[c % 4][:, :]).then_inc(s["out_dve"], 1)

        @block.tensor
        def _(pe):
            def turn(blk, h):
                pe.wait_ge(s["x_staged"], v["x_staged"](blk + 1))
                pe.transpose(turn_ps[:, 0:P], x_now[:, h, :], env.ident[:, :]).then_inc(s["turned"], 1)

            pe.sem_inc(s["made"], 2 * chunks)
            if hidden is None:
                turn(0, 0)
            with pe.Fori(0, BLKS // 2) as i:
                for h in range(2):
                    blk = i * 2 + h
                    pe.wait_ge(s["ready"], blk + v["ready"](1))
                    if hidden is None:
                        turn(blk + 1, 1 - h)
                    for c in range(chunks):
                        out_name = "out_act" if c % 2 == 0 else "out_dve"
                        pe.wait_ge(s[out_name], blk * (chunks // 2) + v[out_name](c // 2 + 1))
                        pe.matmul(out_ps[c % 4][:, :], h_t[:, h, :],
                                  weights[:, 4 * c:4 * c + 4, :].rearrange("d r f -> d (r f)"),
                                  start=True, stop=True).then_inc(s["made"], 1)

        @block.sync
        def _(sp):
            if hidden is not None:
                sp.dma_start(bias_sb[:, :], bias.rearrange("(f o) -> f o", o=1)).then_inc(s["bias_in"], 16)
            for h in range(2):
                sp.sem_inc(stored[h].sem, 16)
            with sp.Fori(0, BLKS // 2) as i:
                for h in range(2):
                    blk = i * 2 + h
                    sp.wait_ge(s["out_act"], blk * (chunks // 2) + v["out_act"](chunks // 2 + 2))
                    sp.wait_ge(s["out_dve"], blk * (chunks // 2) + v["out_dve"](chunks // 2 + 2))
                    sp.dma_start(rows[bass.ds(blk * P, P), :], row[:, h, :]).then_inc(stored[h].sem, 16)
            for h in range(2):
                sp.wait_ge(stored[h].sem, stored[h].at(16 * (BLKS // 2) + 16))

        turns = BLKS + 1 if hidden is None else 0
        counts = dict(bias_in=16 if hidden is not None else 0, x_staged=turns, turned=turns, ready=BLKS + 1,
                      made=chunks * BLKS + 2 * chunks, out_act=chunks // 2 * BLKS + 2, out_dve=chunks // 2 * BLKS + 2)
        for n in names:
            sig[n].passed(counts[n])
        for h in range(2):
            stored[h].passed(16 * (BLKS // 2) + 16)


def gather_program(pool, env, table, bufs, landed, free, free_at, staged, staged_at):
    with pool.Fori(0, GRPS) as g:
        for k in range(SLOT_BUFS):
            if k % 4 == 0:
                pool.wait_ge(staged, g * 4 + staged_at(k // 4 + 1))
                pool.wait_ge(free, g * SLOT_BUFS + free_at(k + 4))
                pool.sem_inc(env.sig("dma_turn").sem, 1)
            pool.indirect_dma_start(bufs[:, k, :], None, table,
                                    bass.IndirectOffsetOnAxis(ap=env.idx_stage[:, k:k + 1], axis=0)
                                    ).then_inc(landed[k].sem, 16)


def stage_indices(act, env, idx, g, turn, staged):
    cols = slice(4 * turn, 4 * turn + 4)
    act.copy(env.idx_stage[:, cols], idx[:, bass.ds(g * SLOT_BUFS + 4 * turn, 4)]).then_inc(staged, 1)


def window_starts(env, g, late=0):
    return env.nc.values_load_multi_w_load_instructions(
        env.win[0:1, bass.ds(g * SLOT_BUFS + (2 - late), SLOT_BUFS)], engines=[DVE_ENGINE], min_val=0, max_val=N,
        skip_runtime_bounds_check_because="sorted destinations are node numbers")[1]


def one_hots_on_act(act, env, tile, count, dist, hot, made, made_at, ready, ready_at):
    if ready_at is not None:
        act.wait_ge(ready, ready_at)
    for k in range(count):
        last = act.activation(dist[:, k, :], env.iota_row[:, :], ACT.Abs, scale=-1.0, bias=env.dst_rel[:, bass.ds(tile + k, 1)])
    last.then_inc(made, 1)
    act.wait_ge(made, made_at)
    act.activation(hot, dist[:, 0:count, :], ACT.Relu, scale=-1.0, bias=1.0).then_inc(ready, count)


def sum_over_slots(env, tag, idx, table, weight, acc, degree=False):
    nc = env.nc
    parts = 2 if degree else 1
    with ExitStack() as ctx:
        sb, ps = stage_memory(nc, ctx, tag)
        rows = sb("rows", [P, SLOT_BUFS, D], F32)
        hot = sb("hot", [P, 4, P], F32)
        sums = [ps(f"sums{j}", [P, 512], F32) for j in range(4)]
        landed = [env.sig(f"landed{k}") for k in range(SLOT_BUFS)]
        names = ("idx_staged", "hot_ready", "multiplied", "added")
        sig = {n: env.sig(f"sum_{n}") for n in names}
        s = {n: v.sem for n, v in sig.items()}
        v = {n: v.at for n, v in sig.items()}
        block = ctx.enter_context(nc.Block())

        @block.gpsimd
        def _(pool):
            gather_program(pool, env, table, rows, landed, s["multiplied"], v["multiplied"], s["idx_staged"],
                           v["idx_staged"])

        @block.scalar
        def _(act):
            for turn in range(4):
                stage_indices(act, env, idx, 0, turn, s["idx_staged"])
            with act.Fori(0, GRPS) as g:
                for turn in range(4):
                    act.wait_ge(s["multiplied"], g * SLOT_BUFS + v["multiplied"](SLOT_BUFS + 4 * turn + 4))
                    stage_indices(act, env, idx, g + 1, turn, s["idx_staged"])

        @block.vector
        def _(dve):
            def build(tile, j):
                c = bass.ds(tile, 1)
                dve.tensor_scalar(hot[:, j, :], env.iota_row[:, :], env.dst_rel[:, c], weight[:, c], ALU.is_equal,
                                  ALU.mult).then_inc(s["hot_ready"], 1)

            dve.memset(acc[:, :, :], 0.0)
            dve.drain().then_inc(s["added"], 4)
            for t in range(AHEAD):
                build(t, t)
            with dve.Fori(0, GRPS) as g:
                starts = window_starts(env, g)
                for k in range(SLOT_BUFS):
                    tile = g * SLOT_BUFS + k
                    build(tile + AHEAD, (k + AHEAD) % 4)
                    dve.wait_ge(s["multiplied"], g * SLOT_BUFS + v["multiplied"](SLOT_BUFS + k + 1))
                    dve.wait_ge(s["added"], g * SLOT_BUFS + v["added"](k + 4))
                    window = acc[:, :, bass.ds(starts[k], P)]
                    dve.tensor_tensor(window, window, sums[k % 4][:, 0:parts * P].rearrange("p (a n) -> p a n", a=parts),
                                      ALU.add).then_inc(s["added"], 1)

        @block.tensor
        def _(pe):
            pe.sem_inc(s["multiplied"], SLOT_BUFS)
            with pe.Fori(0, GRPS) as g:
                for k in range(SLOT_BUFS):
                    j = k % 4
                    pe.wait_ge(landed[k].sem, g * 16 + landed[k].at(16))
                    pe.wait_ge(s["hot_ready"], g * SLOT_BUFS + v["hot_ready"](k + 1))
                    pe.wait_ge(s["added"], g * SLOT_BUFS + v["added"](k + 1))
                    mm = pe.matmul(sums[j][:, 0:P], rows[:, k, :], hot[:, j, :], start=True, stop=True)
                    if degree:
                        mm = pe.matmul(sums[j][:, P:2 * P], env.ones[:, :], hot[:, j, :], start=True, stop=True)
                    mm.then_inc(s["multiplied"], 1)

        for n, count in (("idx_staged", 4 * GRPS + 4), ("hot_ready", TILES + AHEAD), ("multiplied", TILES + SLOT_BUFS),
                         ("added", TILES + 4)):
            sig[n].passed(count)
        for k in range(SLOT_BUFS):
            landed[k].passed(16 * GRPS)


def per_node_block(env, tag, from_x, prepare, apply, use, memory):
    nc = env.nc
    with ExitStack() as ctx:
        sb, ps = stage_memory(nc, ctx, tag)
        mem = memory(sb, ps)
        x_now = sb("x_now", [P, 2, D], F32)
        x_t = sb("x_t", [P, 2, P], F32)
        turn_ps = [ps(f"turn{h}", [P, 512], F32) for h in range(2)]
        out_ps = [ps(f"out{h}", [P, 512], F32) for h in range(2)]
        names = ("x_staged", "turned", "prepared", "applied", "used")
        sig = {n: env.sig(f"node_{n}") for n in names}
        s = {n: v.sem for n, v in sig.items()}
        v = {n: v.at for n, v in sig.items()}
        block = ctx.enter_context(nc.Block())

        @block.scalar
        def _(act):
            with act.Fori(0, BLKS // 2) as i:
                for h in range(2):
                    blk = i * 2 + h
                    act.wait_ge(s["applied"], blk + v["applied"](1))
                    if from_x:
                        act.copy(x_now[:, h, :], env.x[:, bass.ds(blk, 1), :]).then_inc(s["x_staged"], 1)
                    last = prepare(act, mem, blk, h)
                    if from_x:
                        act.wait_ge(s["turned"], blk + v["turned"](1))
                        last = act.copy(x_t[:, h, :], turn_ps[h][:, 0:P])
                    last.then_inc(s["prepared"], 1)

        @block.tensor
        def _(pe):
            pe.sem_inc(s["applied"], 2)
            with pe.Fori(0, BLKS // 2) as i:
                for h in range(2):
                    blk = i * 2 + h
                    if from_x:
                        pe.wait_ge(s["x_staged"], blk + v["x_staged"](1))
                        pe.transpose(turn_ps[h][:, 0:P], x_now[:, h, :], env.ident[:, :]).then_inc(s["turned"], 1)
                    pe.wait_ge(s["prepared"], blk + v["prepared"](1))
                    pe.wait_ge(s["used"], blk + v["used"](1))
                    apply(pe, mem, h, x_t[:, h, :], out_ps[h]).then_inc(s["applied"], 1)

        @block.vector
        def _(dve):
            dve.sem_inc(s["used"], 2)
            with dve.Fori(0, BLKS // 2) as i:
                for h in range(2):
                    blk = i * 2 + h
                    dve.wait_ge(s["applied"], blk + v["applied"](3))
                    use(dve, mem, blk, h, out_ps[h]).then_inc(s["used"], 1)

        turns = BLKS if from_x else 0
        for n, count in (("x_staged", turns), ("turned", turns), ("prepared", BLKS), ("applied", BLKS + 2),
                         ("used", BLKS + 2)):
            sig[n].passed(count)


def add_and_measure(env, dve, mem, blk, h, update, scale=None, bias_row=None):
    x_blk = env.x[:, bass.ds(blk, 1), :].rearrange("p o f -> p (o f)")
    if scale is None:
        dve.tensor_tensor(x_blk, x_blk, update, ALU.add)
    else:
        dve.scalar_tensor_tensor(x_blk, update, scale[:, bass.ds(blk, 1)], x_blk, ALU.mult, ALU.add)
    dve.drain()
    if bias_row is not None:
        dve.tensor_tensor(x_blk, x_blk, bias_row, ALU.add)
        dve.drain()
    return dve.bn_stats(env.stats[:, bass.ds(blk, 1), :].rearrange("p o t -> p (o t)"), x_blk)


def normalize(env, tag, store=None):
    nc = env.nc
    measured, rooted, normed, stored = (env.sig(f"norm_{n}") for n in ("measured", "rooted", "normed", "stored"))
    with nc.Block() as block:
        @block.scalar
        def _(act):
            act.wait_ge(measured.sem, measured.at(1))
            act.activation(env.rstd[:, :], env.rstd[:, :], ACT.Sqrt, bias=env.eps[:, 0:1]).then_inc(rooted.sem, 1)

        @block.vector
        def _(dve):
            (even_mean, even_m2), (odd_mean, odd_m2) = ((env.stats[:, :, k + 1], env.stats[:, :, k + 2]) for k in (0, 3))
            dve.tensor_tensor(env.mean[:, :], even_mean, odd_mean, ALU.add)
            dve.tensor_tensor(env.spread[:, :], even_mean, odd_mean, ALU.subtract)
            dve.tensor_tensor(env.rstd[:, :], even_m2, odd_m2, ALU.add)
            dve.drain()
            dve.tensor_scalar(env.mean[:, :], env.mean[:, :], 0.5, None, ALU.mult)
            dve.scalar_tensor_tensor(env.spread[:, :], env.spread[:, :], 0.25, env.spread[:, :], ALU.mult, ALU.mult)
            dve.drain()
            dve.scalar_tensor_tensor(env.rstd[:, :], env.rstd[:, :], 1.0 / D, env.spread[:, :], ALU.mult,
                                     ALU.add).then_inc(measured.sem, 1)
            dve.wait_ge(rooted.sem, rooted.at(1))
            dve.reciprocal(env.rstd[:, :], env.rstd[:, :])
            dve.drain()
            with dve.Fori(0, BLKS // 2) as i:
                for h in range(2):
                    blk = bass.ds(i * 2 + h, 1)
                    x_blk = env.x[:, blk, :].rearrange("p o f -> p (o f)")
                    dve.tensor_scalar(x_blk, x_blk, env.mean[:, blk], env.rstd[:, blk], ALU.subtract,
                                      ALU.mult).then_inc(normed.sem, 1)

        if store is not None:
            @block.sync
            def _(sp):
                sp.wait_ge(normed.sem, normed.at(BLKS))
                count = store(sp, stored.sem)
                sp.wait_ge(stored.sem, stored.at(16 * count))
                stored.passed(16 * count)

    measured.passed(1)
    rooted.passed(1)
    normed.passed(BLKS)


def store_x(env, table):
    def store(sp, stored):
        sp.dma_start(table.rearrange("(b p) f -> p b f", p=P), env.x[:, 0:BLKS, :]).then_inc(stored, 16)
        return 1
    return store


def store_output(env, out):
    def store(sp, stored):
        sp.dma_start(out[0:(BLKS - 1) * P, :].rearrange("(b p) f -> p b f", p=P), env.x[:, 0:BLKS - 1, :]).then_inc(stored, 16)
        sp.dma_start(out[(BLKS - 1) * P:N, :], env.x[0:LAST, BLKS - 1, :]).then_inc(stored, 16)
        return 2
    return store


def relational_layer(env, inp, x_table):
    nc = env.nc
    table = nc.dram_tensor("relation_table", (NPAD * REL, D), F32, kind="Internal").ap()
    weights_dram = nc.dram_tensor("relation_weights", (REL, D * D), F32, kind="Internal").ap()
    with ExitStack() as ctx:
        acc = ctx.enter_context(nc.sbuf_tensor("rel_acc", [P, 1, ACC], F32))
        weights = ctx.enter_context(nc.sbuf_tensor("rel_weights", [P, REL, D], F32))
        relation_weights(env, "relw1", inp["L0_gnn_basis1"], inp["L0_gnn_coeff1"], weights_dram, weights)
        relation_table(env, "reltab1", weights, table)
        relation_weights(env, "relw2", inp["L0_gnn_basis2"], inp["L0_gnn_coeff2"], weights_dram, weights)
        sum_over_slots(env, "relsum1", env.tab_idx, table, env.w1, acc)
        relation_table(env, "reltab2", weights, table, hidden=acc[:, 0, :], bias=inp["L0_gnn_bias1"])
        sum_over_slots(env, "relsum2", env.tab_idx, table, env.w1, acc)
        add_rows(env, "relout", acc, inp["L0_gnn_bias2"])
    normalize(env, "norm0", store_x(env, x_table))


def load_columns(env, tag, pairs):
    sig = env.sig("small_loaded")
    with env.nc.Block() as block:
        @block.sync
        def _(sp):
            for to, frm in pairs:
                sp.dma_start(to, frm, allow_slow_non_contiguous=True).then_inc(sig.sem, 16)
            sp.wait_ge(sig.sem, sig.at(16 * len(pairs)))
    sig.passed(16 * len(pairs))


def add_rows(env, tag, acc, bias):
    with ExitStack() as ctx:
        bias_sb = ctx.enter_context(env.nc.sbuf_tensor(f"{tag}_bias", [P, 1], F32))
        load_columns(env, tag, [(bias_sb[:, :], bias.rearrange("(f o) -> f o", o=1))])

        def memory(sb, ps):
            return {"val": sb("val", [P, 2, P], F32)}

        def prepare(act, mem, blk, h):
            return act.activation(mem["val"][:, h, :], acc[:, 0, bass.ds(blk * P, P)], ACT.Identity, bias=bias_sb[:, 0:1])

        def apply(pe, mem, h, x_t, out):
            return pe.transpose(out[:, 0:P], mem["val"][:, h, :], env.ident[:, :])

        def use(dve, mem, blk, h, out):
            return add_and_measure(env, dve, mem, blk, h, out[:, 0:P])

        per_node_block(env, tag, False, prepare, apply, use, memory)


def gcn_layer(env, inp, x_in):
    nc = env.nc
    with ExitStack() as ctx:
        acc = ctx.enter_context(nc.sbuf_tensor("gcn_acc", [P, 2, ACC], F32))
        weight = ctx.enter_context(nc.sbuf_tensor("gcn_weight", [P, D], F32))
        bias_row = ctx.enter_context(nc.sbuf_tensor("gcn_bias", [P, D], F32))
        dinv = ctx.enter_context(nc.sbuf_tensor("gcn_dinv", [P, BLKS], F32))
        load_columns(env, "gcn", [(weight[:, :], inp["L1_gnn_weight"]),
                                  (bias_row[:, :], inp["L1_gnn_bias"].partition_broadcast(P))])
        sum_over_slots(env, "gcnsum", env.src_idx, x_in, env.w, acc, degree=True)
        with ExitStack() as inner:
            deg_ps = inner.enter_context(nc.psum_tensor("gcn_deg", [P, 512], F32))
            turned, floored, rooted = (env.sig(f"gcn_{n}").sem for n in ("deg_turned", "deg_floored", "deg_rooted"))
            block = inner.enter_context(nc.Block())

            @block.tensor
            def _(pe):
                for b in range(BLKS):
                    mm = pe.matmul(deg_ps[:, b:b + 1], acc[0:1, 1, b * P:(b + 1) * P], env.ones[0:1, 0:1], start=True,
                                   stop=True)
                mm.then_inc(turned, 1)

            @block.vector
            def _(dve):
                dve.wait_ge(turned, 1)
                dve.tensor_scalar(dinv[:, :], deg_ps[:, 0:BLKS], 1.0, None, ALU.max).then_inc(floored, 1)
                dve.wait_ge(rooted, 1)
                dve.reciprocal(dinv[:, :], dinv[:, :])

            @block.scalar
            def _(act):
                act.wait_ge(floored, 1)
                act.activation(dinv[:, :], dinv[:, :], ACT.Sqrt).then_inc(rooted, 1)

        def memory(sb, ps):
            return {"agg": sb("agg", [P, 2, P], F32)}

        def prepare(act, mem, blk, h):
            return act.copy(mem["agg"][:, h, :], acc[:, 0, bass.ds(blk * P, P)])

        def apply(pe, mem, h, x_t, out):
            pe.matmul(out[:, 0:D], x_t, weight[:, :], start=True, stop=False)
            return pe.matmul(out[:, 0:D], mem["agg"][:, h, :], weight[:, :], start=False, stop=True)

        def use(dve, mem, blk, h, out):
            return add_and_measure(env, dve, mem, blk, h, out[:, 0:D], scale=dinv, bias_row=bias_row[:, :])

        per_node_block(env, "gcnout", True, prepare, apply, use, memory)
    normalize(env, "norm1")


def project_nodes(env, tag, from_x, prepare, weights, width, table, scale=None):
    nc = env.nc
    with ExitStack() as ctx:
        rows = ctx.enter_context(nc.sbuf_tensor(f"{tag}_rows", [P, BLKS, width], F32))

        def memory(sb, ps):
            return {"own": None if from_x else sb("own", [P, 2, P], F32)}

        def ready(act, mem, blk, h):
            return None if from_x else prepare(act, mem, blk, h)

        def apply(pe, mem, h, x_t, out):
            return pe.matmul(out[:, 0:width], x_t if from_x else mem["own"][:, h, :], weights[:, 0:width], start=True,
                             stop=True)

        def use(dve, mem, blk, h, out):
            to = rows[:, bass.ds(blk, 1), :].rearrange("p o f -> p (o f)")
            if scale is None:
                return dve.tensor_copy(to, out[:, 0:width])
            return dve.tensor_scalar(to, out[:, 0:width], scale[:, bass.ds(blk, 1)], None, ALU.mult)

        per_node_block(env, tag, from_x, ready, apply, use, memory)
        sig = env.sig("table_stored")
        with nc.Block() as block:
            @block.sync
            def _(sp):
                sp.dma_start(table.rearrange("(b p) f -> p b f", p=P), rows[:, :, :]).then_inc(sig.sem, 16)
                sp.wait_ge(sig.sem, sig.at(16))
        sig.passed(16)


def attention_weights(env, tag, w_in, att_src, att_dst, combined):
    nc = env.nc
    with ExitStack() as ctx:
        sb, ps = stage_memory(nc, ctx, tag)
        att = sb("att", [P, 2], F32)
        load_columns(env, tag, [(combined[:, 0:D], w_in), (att[:, 0:1], att_src.rearrange("h (c o) -> (h c) o", o=1)),
                                (att[:, 1:2], att_dst.rearrange("h (c o) -> (h c) o", o=1))])
        per_head = sb("per_head", [P, 2 * HEADS], F32)
        w_t = sb("w_t", [P, P], F32)
        turn_ps, score_ps = ps("turn", [P, 512], F32), ps("score", [P, 512], F32)
        sig = {n: env.sig(f"att_{n}") for n in ("turned", "copied", "scored")}
        block = ctx.enter_context(nc.Block())

        @block.tensor
        def _(pe):
            pe.transpose(turn_ps[:, 0:P], combined[:, 0:D], env.ident[:, :]).then_inc(sig["turned"].sem, 1)
            pe.wait_ge(sig["copied"].sem, sig["copied"].at(1))
            pe.matmul(score_ps[:, 0:2 * HEADS], w_t[:, :], per_head[:, :], start=True, stop=True).then_inc(sig["scored"].sem, 1)

        @block.vector
        def _(dve):
            for k in range(2):
                dve.tensor_scalar(per_head[:, k * HEADS:(k + 1) * HEADS], env.head_mask[:, :], att[:, k:k + 1], None, ALU.mult)
            dve.wait_ge(sig["turned"].sem, sig["turned"].at(1))
            dve.tensor_copy(w_t[:, :], turn_ps[:, 0:P]).then_inc(sig["copied"].sem, 1)
            dve.wait_ge(sig["scored"].sem, sig["scored"].at(1))
            dve.tensor_copy(combined[:, D:D + 2 * HEADS], score_ps[:, 0:2 * HEADS])

        for n in sig:
            sig[n].passed(1)


def segment_flags(env, flags):
    nc = env.nc
    with ExitStack() as ctx:
        sb, ps = stage_memory(nc, ctx, "flags")
        wide = sb("wide", [P, 2, SLOT_BUFS, HEADS], F32)
        row_crossed = sb("row_crossed", [P, GRPS], F32)
        by_tile = sb("by_tile", [P, 1024], F32)
        turn_ps = [ps(f"turn{h}", [P, 512], F32) for h in range(2)]
        fold_ps = ps("fold", [P, 1024], F32)
        s = {n: env.sig(f"flags_{n}").sem for n in ("wide", "turned", "kept", "by_tile", "folded")}
        pairs = GRPS // 2
        block = ctx.enter_context(nc.Block())

        @block.scalar
        def _(act):
            def widen(g, h):
                act.wait_ge(s["turned"], g + 1)
                act.copy(wide[:, h, :, :], over_columns(env.start[:, bass.ds(g * SLOT_BUFS, SLOT_BUFS)], HEADS)).then_inc(s["wide"], 1)

            with act.Fori(0, pairs) as i:
                for h in range(2):
                    widen(i * 2 + h, h)
            widen(GRPS - 1, 0)

        @block.tensor
        def _(pe):
            def turn(g, h):
                pe.wait_ge(s["wide"], g + 1)
                pe.wait_ge(s["kept"], g + 1)
                pe.transpose(turn_ps[h][:, 0:P], wide[:, h, :, :].rearrange("p c h -> p (c h)"),
                             env.ident[:, :]).then_inc(s["turned"], 1)

            pe.sem_inc(s["turned"], 2)
            with pe.Fori(0, pairs) as i:
                for h in range(2):
                    turn(i * 2 + h, h)
            turn(GRPS - 1, 0)
            pe.wait_ge(s["by_tile"], 1)
            for half in range(2):
                mm = pe.matmul(fold_ps[0:HEADS, half * 512:half * 512 + 512], env.head_sel[:, :],
                               by_tile[:, half * 512:half * 512 + 512], start=True, stop=True)
            mm.then_inc(s["folded"], 1)

        @block.vector
        def _(dve):
            def firsts(t):
                return t[:, 0:(GRPS + 1) * P].rearrange("p (g e) -> p g e", e=P)[:, :, 0:1]

            def keep(g, h):
                cols = bass.ds(g * P + 1, P - 1)
                dve.wait_ge(s["turned"], g + 3)
                starts = turn_ps[h][:, 1:P]
                dve.tensor_scalar(flags["goes_on"][:, cols], starts, -1.0, 1.0, ALU.mult, ALU.add)
                dve.tensor_scalar(flags["reset"][:, cols], starts, -BIG, None, ALU.mult)
                dve.tensor_scalar(flags["entered"][:, bass.ds(g, 1)], turn_ps[h][:, 0:1], -BIG, None,
                                  ALU.mult).then_inc(s["kept"], 1)
                dve.drain()
                dve.tensor_tensor_scan(flags["lead"][:, cols], flags["reset"][:, cols], flags["reset"][:, cols], 0.0,
                                       ALU.min, ALU.min)

            dve.sem_inc(s["kept"], 2)
            last = slice(GRPS * P, None)
            for name, fill in (("goes_on", 0.0), ("reset", -BIG), ("lead", 0.0)):
                dve.memset(flags[name][:, last], fill)
                dve.memset(firsts(flags[name])[:, 0:GRPS, :], fill)
            dve.memset(flags["entered"][:, GRPS:], -BIG)
            dve.memset(flags["crossed"][:, :], -BIG)
            dve.memset(by_tile[:, TILES:], 0.0)
            dve.drain()
            with dve.Fori(0, pairs) as i:
                for h in range(2):
                    keep(i * 2 + h, h)
            keep(GRPS - 1, 0)
            dve.drain()
            ends = flags["lead"][:, 0:GRPS * P].rearrange("p (g e) -> p g e", e=P)[:, :, P - 1:P]
            dve.tensor_tensor(row_crossed[:, :].unsqueeze(2), ends, flags["entered"][:, 0:GRPS].unsqueeze(2), ALU.min)
            dve.drain()
            dve.tensor_tensor(by_tile[:, 0:TILES].rearrange("p (g k) -> p g k", k=SLOT_BUFS),
                              over_columns(row_crossed[:, :], SLOT_BUFS), over_rows(env.tile_mask[:, :], GRPS),
                              ALU.mult).then_inc(s["by_tile"], 1)
            dve.wait_ge(s["folded"], 1)
            dve.tensor_copy(flags["crossed"][:, 0:TILES], fold_ps[0:HEADS, 0:TILES])


def first_scores(env, tag, table, first_dst):
    nc = env.nc
    width = D + 2 * HEADS
    with ExitStack() as ctx:
        sb, ps = stage_memory(nc, ctx, tag)
        rows = sb("rows", [P, FIRSTS, width], F32)
        spread = sb("spread", [P, FIRSTS, SLOT_BUFS, HEADS], F32)
        out_ps = ps("out", [P, 512], F32)
        sig = {n: env.sig(f"first_{n}") for n in ("gathered", "spread", "turned")}
        block = ctx.enter_context(nc.Block())

        @block.gpsimd
        def _(pool):
            for j in range(FIRSTS):
                pool.indirect_dma_start(rows[:, j, :], None, table,
                                        bass.IndirectOffsetOnAxis(ap=env.first_idx[:, j:j + 1], axis=0)
                                        ).then_inc(sig["gathered"].sem, 16)

        @block.vector
        def _(dve):
            dve.wait_ge(sig["gathered"].sem, sig["gathered"].at(16 * FIRSTS))
            for j in range(FIRSTS):
                last = dve.tensor_tensor(spread[:, j, :, :], over_rows(rows[:, j, D + HEADS:width], SLOT_BUFS),
                                         over_columns(env.tile_sel[:, :], HEADS), ALU.mult)
            last.then_inc(sig["spread"].sem, 1)
            dve.wait_ge(sig["turned"].sem, sig["turned"].at(1))
            dve.tensor_scalar(first_dst[:, :], out_ps[:, 0:HEADS * FIRSTS], -1.0, None, ALU.mult)

        @block.tensor
        def _(pe):
            pe.wait_ge(sig["spread"].sem, sig["spread"].at(1))
            for j in range(FIRSTS):
                mm = pe.matmul(out_ps[:, j * HEADS:(j + 1) * HEADS], spread[:, j, :, :].rearrange("p k h -> p (k h)"),
                               env.head_mask[:, :], start=True, stop=True)
            mm.then_inc(sig["turned"].sem, 1)

        for n, count in (("gathered", 16 * FIRSTS), ("spread", 1), ("turned", 1)):
            sig[n].passed(count)


def attend(env, tag, table, flags, first_dst, acc):
    nc = env.nc
    width = D + 2 * HEADS
    with ExitStack() as ctx:
        sb, ps = stage_memory(nc, ctx, tag)
        rows = sb("rows", [P, PHASES * SLOT_BUFS, width], F32)
        scores = sb("scores", [P, PHASES, 2, SLOT_BUFS, HEADS], F32)
        score = sb("score", [P, P], F32)
        own_dst = sb("own_dst", [P, P], F32)
        neg_dst = sb("neg_dst", [P, P], F32)
        so_far = sb("so_far", [P, P], F32)
        next_reset = sb("next_reset", [P, P], BF16)
        largest = sb("largest", [P, P], F32)
        numer = sb("numer", [P, PHASES, P], F32)
        ends = sb("ends", [P, SLOT_BUFS], F32)
        chain = sb("chain", [HEADS, SLOT_BUFS + 1], F32)
        picked = sb("picked", [P, SLOT_BUFS], F32)
        came_in = sb("came_in", [P, 1], F32)
        first_max = sb("first_max", [P, 1], F32)
        drop = sb("drop", [P, SLOT_BUFS], F32)
        factor_row = sb("factor_row", [P, SLOT_BUFS], F32)
        p_col = sb("p_col", [P, P], F32)
        p_wide = sb("p_wide", [P, PHASES, SLOT_BUFS, D], F32)
        factor = sb("factor", [P, PHASES, SLOT_BUFS], F32)
        scaled = sb("scaled", [P, 4, HEADS, CH], F32)
        hot = sb("hot", [P, SLOT_BUFS, P], F32)
        dist = sb("dist", [P, 4, P], F32)
        turn_ps = ps("turn", [P, 2, 256], F32)
        p_ps = [ps(f"p{f}", [P, 512], F32) for f in range(PHASES)]
        small_ps = ps("small", [P, 512], F32)
        fold_ps, spread_ps, factor_ps = (small_ps[:, k * SLOT_BUFS:(k + 1) * SLOT_BUFS] for k in range(3))
        sums = [ps(f"sums{j}", [P, 2, 256], F32) for j in range(3)]
        landed = [env.sig(f"landed{k}") for k in range(SLOT_BUFS)]
        names = ("idx_staged", "arrived", "scores_staged", "turned", "kept", "ends_ready", "folded", "chained", "spread", "shifted",
                 "exped", "p_turned", "p_ready", "wide_ready", "dist_ready", "hot_ready", "scaled_ready", "multiplied", "added")
        sig = {n: env.sig(f"attend_{n}") for n in names}
        s = {n: x.sem for n, x in sig.items()}
        v = {n: x.at for n, x in sig.items()}
        held = PHASES * SLOT_BUFS
        block = ctx.enter_context(nc.Block())

        @block.gpsimd
        def _(pool):
            with pool.Fori(0, GRPS // PHASES) as i:
                for f in range(PHASES):
                    for k in range(SLOT_BUFS):
                        if k % 4 == 0:
                            g = i * PHASES + f
                            pool.wait_ge(s["idx_staged"], g * 4 + v["idx_staged"](k // 4 + 1))
                            pool.wait_ge(s["multiplied"], g * SLOT_BUFS + v["multiplied"](k + 4))
                            pool.sem_inc(env.sig("dma_turn").sem, 1)
                        pool.indirect_dma_start(rows[:, f * SLOT_BUFS + k, :], None, table,
                                                bass.IndirectOffsetOnAxis(ap=env.idx_stage[:, k:k + 1], axis=0)
                                                ).then_inc(landed[k].sem, 16)

        @block.sync
        def _(sp):
            with sp.Fori(0, GRPS) as g:
                for k in range(SLOT_BUFS):
                    sp.wait_ge(landed[k].sem, g * 16 + landed[k].at(16))
                    sp.sem_inc(s["arrived"], 1)
            sp.sem_inc(s["arrived"], 2 * SLOT_BUFS)

        @block.scalar
        def _(act):
            def take_scores(g, f, turn):
                four = slice(4 * turn, 4 * turn + 4)
                bufs = slice(f * SLOT_BUFS + 4 * turn, f * SLOT_BUFS + 4 * turn + 4)
                if turn == 0:
                    act.wait_ge(s["turned"], g + v["turned"](1))
                act.wait_ge(s["arrived"], g * SLOT_BUFS + v["arrived"](4 * turn + 4))
                act.copy(scores[:, f, 0, four, :], rows[:, bufs, D:D + HEADS])
                act.copy(scores[:, f, 1, four, :], rows[:, bufs, D + HEADS:width]).then_inc(s["scores_staged"], 1)
                stage_indices(act, env, env.src_idx, g + 1, turn, s["idx_staged"])

            def exponentials(g, f):
                act.wait_ge(s["shifted"], g + v["shifted"](1))
                act.activation(numer[:, f, :], score[:, :], ACT.Exp)
                act.activation(factor_row[:, :], drop[:, :], ACT.Exp).then_inc(s["exped"], 1)

            def keep_numerators(g, f):
                act.wait_ge(s["p_turned"], g + v["p_turned"](1))
                act.copy(p_col[:, :], p_ps[f][:, 0:P])
                act.copy(factor[:, f, :], factor_ps).then_inc(s["p_ready"], 1)
                act.wait_ge(s["p_ready"], g + v["p_ready"](1))
                for turn in range(4):
                    act.copy(p_wide[:, f, 4 * turn:4 * turn + 4, :].rearrange("p k (h c) -> p (k h) c", c=CH),
                             over_columns(p_col[:, 4 * turn * HEADS:4 * (turn + 1) * HEADS], CH)).then_inc(s["wide_ready"], 1)

            def build(g, turn):
                act.wait_ge(s["multiplied"], g * SLOT_BUFS + v["multiplied"](held - SLOT_BUFS + 4 * turn + 4))
                to = slice(turn % 4 * 4, turn % 4 * 4 + 4)
                one_hots_on_act(act, env, g * SLOT_BUFS + 4 * turn, 4, dist, hot[:, to, :], s["dist_ready"],
                                g * 4 + v["dist_ready"](turn + 1), s["hot_ready"],
                                None if turn == 0 else g * SLOT_BUFS + v["hot_ready"](4 * turn))

            for turn in range(4):
                stage_indices(act, env, env.src_idx, 0, turn, s["idx_staged"])
            for turn in range(2):
                build(0, turn)
            for g in range(2):
                for turn in range(4):
                    take_scores(g, g, turn)
            exponentials(0, 0)
            keep_numerators(0, 0)
            with act.Fori(0, GRPS // PHASES) as i:
                for f in range(PHASES):
                    g = i * PHASES + f
                    ahead, next_f = (f + 2) % PHASES, (f + 1) % PHASES
                    build(g, 2)
                    take_scores(g + 2, ahead, 0)
                    take_scores(g + 2, ahead, 1)
                    build(g, 3)
                    take_scores(g + 2, ahead, 2)
                    take_scores(g + 2, ahead, 3)
                    build(g, 4)
                    exponentials(g + 1, next_f)
                    keep_numerators(g + 1, next_f)
                    build(g, 5)

        @block.vector
        def _(dve):
            def softmax_step(g, step):
                cols, late = bass.ds(g * P, P), bass.ds(g * P + 1, P)
                source, dest = turn_ps[:, 0, 0:P], turn_ps[:, 1, 0:P]
                if step == 1:
                    dve.wait_ge(s["turned"], g + v["turned"](PHASES + 1))
                    dve.scalar_tensor_tensor(own_dst[:, 1:P], flags["goes_on"][:, bass.ds(g * P + 1, P - 1)], 1.0,
                                             dest[:, 1:P], ALU.subtract, ALU.mult)
                    dve.tensor_copy(own_dst[:, 0:1], first_dst[:, bass.ds(g, 1)])
                    dve.drain()
                    dve.tensor_tensor_scan(neg_dst[:, :], flags["goes_on"][:, cols], own_dst[:, :], 0.0, ALU.mult, ALU.add)
                elif step == 2:
                    dve.drain()
                    dve.tensor_tensor(score[:, :], source, neg_dst[:, :], ALU.subtract).then_inc(s["kept"], 1)
                elif step == 3:
                    dve.drain()
                    dve.scalar_tensor_tensor(score[:, :], score[:, :], 0.2, score[:, :], ALU.mult, ALU.max)
                elif step == 4:
                    dve.drain()
                    dve.tensor_copy(next_reset[:, :], flags["reset"][:, late])
                    dve.tensor_tensor_scan(so_far[:, :], flags["reset"][:, cols], score[:, :], -BIG, ALU.add, ALU.max)
                elif step == 5:
                    dve.drain()
                    dve.tensor_scalar(ends[:, :], env.tile_mask[:, :], so_far[:, P - 1:P], None, ALU.mult).then_inc(s["ends_ready"], 1)
                    dve.tensor_tensor_scan(largest[:, ::-1], next_reset[:, ::-1], so_far[:, ::-1], -BIG, ALU.add,
                                           ALU.max)
                elif step == 7:
                    dve.tensor_copy(chain[:, 0:1], chain[:, SLOT_BUFS:])
                    dve.drain()
                    dve.wait_ge(s["folded"], g + v["folded"](1))
                    dve.tensor_tensor_scan(chain[:, 1:], flags["crossed"][:, bass.ds(g * SLOT_BUFS, SLOT_BUFS)],
                                           fold_ps[0:HEADS, :], chain[:, 0:1], ALU.add, ALU.max).then_inc(s["chained"], 1)
                elif step == 9:
                    dve.wait_ge(s["spread"], g + v["spread"](1))
                    dve.tensor_tensor_reduce(picked[:, :], spread_ps, env.tile_mask[:, :], 1.0, 0.0, ALU.mult, ALU.add,
                                             came_in[:, 0:1])
                elif step == 10:
                    dve.drain()
                    dve.tensor_tensor(first_max[:, :], came_in[:, 0:1], largest[:, 0:1], ALU.max)
                    dve.drain()
                    dve.tensor_scalar(drop[:, :], env.other_tile[:, :], came_in[:, 0:1], first_max[:, 0:1], ALU.add, ALU.subtract)
                    dve.scalar_tensor_tensor(largest[:, :], flags["lead"][:, cols], first_max[:, 0:1], largest[:, :], ALU.add,
                                             ALU.max)
                elif step == 11:
                    dve.drain()
                    dve.tensor_tensor(score[:, :], score[:, :], largest[:, :], ALU.subtract).then_inc(s["shifted"], 1)

            dve.memset(acc[:, :, :], 0.0)
            dve.memset(factor[:, PHASES - 1, :], 0.0)
            dve.memset(chain[:, :], -BIG)
            for j in range(3):
                dve.memset(sums[j][:, :, :], 0.0)
            dve.sem_inc(s["kept"], 1)
            dve.drain().then_inc(s["added"], 1)
            for step in range(12):
                softmax_step(0, step)
            with dve.Fori(0, GRPS // PHASES) as i:
                for f in range(PHASES):
                    g = i * PHASES + f
                    starts = window_starts(env, g, late=2)
                    dve.wait_ge(s["p_ready"], g + v["p_ready"](1))
                    for k in range(SLOT_BUFS):
                        tile, j, buf = g * SLOT_BUFS + k, k % 4, f * SLOT_BUFS + k
                        dve.tensor_tensor(scaled[:, j, :, :], rows[:, buf, 0:D].rearrange("p (h c) -> p h c", h=HEADS),
                                          over_columns(p_ps[f][:, k * HEADS:(k + 1) * HEADS], CH),
                                          ALU.mult).then_inc(s["scaled_ready"], 1)
                        softmax_step(g + 1, k)
                        dve.wait_ge(s["multiplied"], tile + v["multiplied"](held - 1))
                        dve.wait_ge(s["added"], tile + v["added"](1))
                        before, bank = (buf - 2) % held, sums[(buf - 2) % 3]
                        first = acc[:, :, bass.ds(starts[k], 1)]
                        dve.scalar_tensor_tensor(first, first, factor[:, before // SLOT_BUFS, before % SLOT_BUFS:before % SLOT_BUFS + 1],
                                                 bank[:, :, 0:1], ALU.mult, ALU.add)
                        others = acc[:, :, bass.ds(starts[k] + 1, P - 1)]
                        dve.tensor_tensor(others, others, bank[:, :, 1:P], ALU.add).then_inc(s["added"], 1)
            assert SLOTS - (N + E) >= 2 * P

        @block.tensor
        def _(pe):
            def turn_scores(g, f):
                pe.wait_ge(s["scores_staged"], g * 4 + v["scores_staged"](4))
                pe.wait_ge(s["kept"], g + v["kept"](1))
                for k in range(2):
                    mm = pe.transpose(turn_ps[:, k, 0:P], scores[:, f, k, :, :].rearrange("p k h -> p (k h)"), env.ident[:, :])
                mm.then_inc(s["turned"], 1)

            def fold_ends(g):
                pe.wait_ge(s["ends_ready"], g + v["ends_ready"](1))
                pe.matmul(fold_ps[0:HEADS, :], env.head_sel[:, :], ends[:, :], start=True, stop=True).then_inc(s["folded"], 1)

            def spread_chain(g):
                pe.wait_ge(s["chained"], g + v["chained"](1))
                pe.matmul(spread_ps, env.ident[:, :], flags["entered"][:, bass.ds(g, 1)].to_broadcast([P, SLOT_BUFS]),
                          start=True, stop=False)
                pe.matmul(spread_ps, env.head_sel_t[:, :], chain[:, 0:SLOT_BUFS], start=False, stop=True).then_inc(s["spread"], 1)

            def turn_numerators(g, f):
                pe.wait_ge(s["exped"], g + v["exped"](1))
                pe.transpose(p_ps[f][:, 0:P], numer[:, f, :], env.ident[:, :])
                pe.matmul(factor_ps, env.head_rows[:, :], factor_row[:, :], start=True, stop=True).then_inc(s["p_turned"], 1)

            pe.sem_inc(s["multiplied"], held)
            pe.sem_inc(s["turned"], PHASES)
            turn_scores(0, 0)
            fold_ends(0)
            spread_chain(0)
            turn_numerators(0, 0)
            with pe.Fori(0, GRPS // PHASES) as i:
                for f in range(PHASES):
                    g, next_f = i * PHASES + f, (f + 1) % PHASES
                    pe.wait_ge(s["p_ready"], g + v["p_ready"](1))
                    for k in range(SLOT_BUFS):
                        tile, j, bank = g * SLOT_BUFS + k, k % 4, sums[(f * SLOT_BUFS + k) % 3]
                        if k == 0:
                            turn_scores(g + 1, next_f)
                        elif k == 6:
                            fold_ends(g + 1)
                        elif k == 8:
                            spread_chain(g + 1)
                        elif k == 12:
                            turn_numerators(g + 1, next_f)
                        if k % 4 == 0:
                            pe.wait_ge(s["wide_ready"], g * 4 + v["wide_ready"](k // 4 + 1))
                        pe.wait_ge(s["scaled_ready"], tile + v["scaled_ready"](1))
                        pe.wait_ge(s["hot_ready"], tile + v["hot_ready"](1))
                        pe.wait_ge(s["added"], tile + v["added"](1))
                        pe.matmul(bank[:, 0, 0:P], scaled[:, j, :, :].rearrange("p h c -> p (h c)"), hot[:, k, :], start=True,
                                  stop=True)
                        pe.matmul(bank[:, 1, 0:P], p_wide[:, f, k, :], hot[:, k, :], start=True,
                                  stop=True).then_inc(s["multiplied"], 1)

        for n, count in (("idx_staged", 4 * GRPS + 12), ("arrived", TILES + 2 * SLOT_BUFS), ("scores_staged", 4 * GRPS + 8), ("turned", GRPS + 1 + PHASES),
                         ("kept", GRPS + 2), ("ends_ready", GRPS + 1), ("folded", GRPS + 1), ("chained", GRPS + 1),
                         ("spread", GRPS + 1), ("shifted", GRPS + 1), ("exped", GRPS + 1), ("p_turned", GRPS + 1),
                         ("p_ready", GRPS + 1), ("wide_ready", 4 * GRPS + 4), ("dist_ready", 4 * GRPS + 2), ("hot_ready", TILES + 8), ("scaled_ready", TILES),
                         ("multiplied", TILES + held), ("added", TILES + 1)):
            sig[n].passed(count)
        for k in range(SLOT_BUFS):
            landed[k].passed(16 * GRPS)


def divide_sums(env, acc):
    with env.nc.Block() as block:
        @block.vector
        def _(dve):
            dve.tensor_scalar(acc[:, 1, 0:NPAD], acc[:, 1, 0:NPAD], 1e-30, None, ALU.max)
            dve.drain()
            dve.reciprocal(acc[:, 1, 0:NPAD], acc[:, 1, 0:NPAD])
            dve.drain()
            dve.tensor_tensor(acc[:, 0, 0:NPAD], acc[:, 0, 0:NPAD], acc[:, 1, 0:NPAD], ALU.mult)


def gat_layer(env, inp):
    nc = env.nc
    width = D + 2 * HEADS
    table = nc.dram_tensor("gat_table", (NPAD, width), F32, kind="Internal").ap()
    slots = (GRPS + 1) * P
    with ExitStack() as ctx:
        def sb(name, shape, dt=F32):
            return ctx.enter_context(nc.sbuf_tensor(f"gat_{name}", shape, dt))

        flags = {"goes_on": sb("goes_on", [P, slots], BF16), "reset": sb("reset", [P, slots + 1], BF16),
                 "lead": sb("lead", [P, slots], BF16), "entered": sb("entered", [P, GRPS + 1]),
                 "crossed": sb("crossed", [HEADS, TILES + SLOT_BUFS])}
        first_dst = sb("first_dst", [P, HEADS * FIRSTS])
        combined = sb("combined", [P, width])
        bias = sb("bias", [P, 1])
        acc = sb("acc", [P, 2, ACC])
        segment_flags(env, flags)
        attention_weights(env, "gat1w", inp["L2_gnn_W1"], inp["L2_gnn_as1"], inp["L2_gnn_ad1"], combined)
        project_nodes(env, "gat1tab", True, None, combined, width, table)
        first_scores(env, "gat1first", table, first_dst)
        attend(env, "gat1sum", table, flags, first_dst, acc)
        divide_sums(env, acc)
        load_columns(env, "gat1bias", [(bias[:, :], inp["L2_gnn_b1"].rearrange("(f o) -> f o", o=1))])
        attention_weights(env, "gat2w", inp["L2_gnn_W2"], inp["L2_gnn_as2"], inp["L2_gnn_ad2"], combined)

        def hidden(act, mem, blk, h):
            return act.activation(mem["own"][:, h, :], acc[:, 0, bass.ds(blk * P, P)], ACT.Relu, bias=bias[:, 0:1])

        project_nodes(env, "gat2tab", False, hidden, combined, width, table)
        first_scores(env, "gat2first", table, first_dst)
        attend(env, "gat2sum", table, flags, first_dst, acc)
        divide_sums(env, acc)
        add_rows(env, "gatout", acc, inp["L2_gnn_b2"])
    normalize(env, "norm2")


def tensor_weights(env, inp, wy, w_out, fc1, w2):
    nc = env.nc
    mix, keep = math.cos(math.pi / 8.0), math.sin(math.pi / 8.0)
    fan, fan_two, neighbors = math.sqrt(MUL), math.sqrt(2 * MUL), math.sqrt(16.0)
    edge_part = mix / (fan_two * neighbors)
    scales = (keep / fan, edge_part, edge_part, edge_part / math.sqrt(3.0))
    with ExitStack() as ctx:
        sb, ps = stage_memory(nc, ctx, "tpw")
        wy_in = sb("wy_in", [P, D], F32)
        w_in = sb("w_in", [P, 4, 4, MUL], F32)
        fc2_in = sb("fc2_in", [HID, 4 * MUL], F32)
        zeroed, loaded = env.sig("tpw_zeroed").sem, env.sig("tpw_loaded").sem
        block = ctx.enter_context(nc.Block())

        @block.sync
        def _(sp):
            def vectors(m):
                return slice(MUL + m, D, 3)

            l20, l21 = inp["L3_gnn_W_l20"], inp["L3_gnn_W_l21"]
            loads = [(wy_in[0:MUL, 0:MUL], inp["L3_gnn_W_l10"]), (w_in[0:MUL, 0, 0, :], inp["L3_gnn_W_sc0"]),
                     (w_in[0:MUL, 1, 0, :], l20[0:MUL, :]), (fc2_in[:, :], inp["L3_gnn_W_fc2"])]
            for m in range(3):
                lo = MUL + MUL * m
                loads += [(wy_in[vectors(m), lo:lo + MUL], inp["L3_gnn_W_l11"]),
                          (w_in[vectors(m), 0, 1 + m, :], inp["L3_gnn_W_sc1"]),
                          (w_in[lo:lo + MUL, 1, 1 + m, :], l21[MUL:2 * MUL, :]),
                          (w_in[MUL * m:MUL * (m + 1), 2, 1 + m, :], l21[0:MUL, :]),
                          (w_in[MUL * m:MUL * (m + 1), 3, 0, :], l20[MUL:2 * MUL, :])]
            for i in range(8):
                loads.append((fc1[LEN * i:LEN * (i + 1), i, :], inp["L3_gnn_W_fc1"]))
            sp.wait_ge(zeroed, 1)
            for to, frm in loads:
                sp.dma_start(to, frm).then_inc(loaded, 16)
            sp.wait_ge(loaded, 16 * len(loads))
            sp.sem_inc(zeroed, 1)

        @block.vector
        def _(dve):
            dve.memset(wy_in[:, :], 0.0)
            dve.memset(w_in[:, :, :, :], 0.0)
            dve.memset(fc1[:, :, :], 0.0)
            dve.drain().then_inc(zeroed, 1)
            dve.wait_ge(zeroed, 2)
            dve.tensor_scalar(wy[:, :], wy_in[:, :], 1.0 / fan, None, ALU.mult)
            for i, scale in enumerate(scales):
                dve.tensor_scalar(w_out[:, i, 0:MUL], w_in[:, i, 0, :], scale, None, ALU.mult)
                dve.tensor_scalar(w_out[:, i, MUL:D].rearrange("p (w m) -> p m w", m=3), w_in[:, i, 1:4, :], scale, None,
                                  ALU.mult)
            norm = 1.0 / math.sqrt(HID)
            for to, frm in ((0, 0), (1, 2), (2, 2), (3, 2), (4, 1), (5, 3)):
                dve.tensor_scalar(w2[:, to * MUL:(to + 1) * MUL], fc2_in[:, frm * MUL:(frm + 1) * MUL], norm, None, ALU.mult)


def convolve(env, tag, table, records, fc1, w2, acc):
    nc = env.nc
    vec = 3 * MUL
    octets, turns = 2 * GRPS, 4 * GRPS
    with ExitStack() as ctx:
        sb, ps = stage_memory(nc, ctx, tag)
        rec = sb("rec", [P, TILES + SLOT_BUFS, REC], F32)
        rows = sb("rows", [P, SLOT_BUFS, D], F32)
        hot = sb("hot", [P, 8, P], F32)
        dist = sb("dist", [P, 4, P], F32)
        message = sb("message", [P, 4, D + 2 * vec], F32)
        rows_attr = sb("rows_attr", [P, 8, 3, 2 * MUL], F32)
        lens = sb("lens", [P, 2, 8, LEN], F32)
        lens_t = sb("lens_t", [8 * LEN, 2, P], F32)
        hidden = sb("hidden", [HID, 2, 4, P], F32)
        lens_ps = ps("lens_ps", [P, 512], F32)
        hidden_ps = ps("hidden_ps", [P, 512], F32)
        w_ps = [ps(f"w{j}", [P, 2, 256], F32) for j in range(2)]
        sums = [ps(f"sums{j}", [P, 512], F32) for j in range(4)]
        landed = [env.sig(f"landed{k}") for k in range(SLOT_BUFS)]
        names = ("loaded", "arrived", "tail_zeroed", "idx_staged", "lens_staged", "lens_turned", "lens_ready", "hidden_made",
                 "hidden_ready", "w_made", "dist_ready", "hot_ready", "hot_dve", "rows_ready", "message_ready", "multiplied", "added")
        s = {n: env.sig(f"conv_{n}").sem for n in names}
        block = ctx.enter_context(nc.Block())

        def attr(tile, m):
            return rec[:, bass.ds(tile, 1), R_EA + m:R_EA + m + 1].rearrange("p o k -> p (o k)")

        @block.sync
        def _(sp):
            sp.dma_start(rec[:, 0:TILES, :], records.rearrange("(p q) k -> p q k", p=P)).then_inc(s["loaded"], 16)
            with sp.Fori(0, GRPS) as g:
                for k in range(SLOT_BUFS):
                    sp.wait_ge(landed[k].sem, g * 16 + landed[k].at(16))
                    sp.sem_inc(s["arrived"], 1)
            sp.sem_inc(s["arrived"], 4)

        @block.gpsimd
        def _(pool):
            gather_program(pool, env, table, rows, landed, s["multiplied"], lambda n: n, s["idx_staged"], lambda n: n)

        @block.scalar
        def _(act):
            def stage_lens(octet, u):
                act.copy(lens[:, u, :, :], rec[:, bass.ds(octet * 8, 8), R_LEN:REC]).then_inc(s["lens_staged"], 1)

            def keep_lens(octet, u):
                act.wait_ge(s["lens_turned"], octet + 1)
                act.copy(lens_t[:, u, :], lens_ps[0:8 * LEN, u * P:(u + 1) * P]).then_inc(s["lens_ready"], 1)

            def activate(turn, h):
                act.wait_ge(s["hidden_made"], turn + 1)
                act.activation(hidden[:, h, :, :].rearrange("p k e -> p (k e)"), hidden_ps[0:HID, :], ACT.Silu,
                               scale=1.0 / math.sqrt(LEN)).then_inc(s["hidden_ready"], 1)

            def build(g, turn):
                act.wait_ge(s["multiplied"], g * SLOT_BUFS + (SLOT_BUFS - 8 + 4 * turn + 4))
                to = slice(turn % 2 * 4, turn % 2 * 4 + 2)
                one_hots_on_act(act, env, g * SLOT_BUFS + 4 * turn, 2, dist, hot[:, to, :], s["dist_ready"], g * 4 + (turn + 1),
                                s["hot_ready"], None if turn == 0 else g * 8 + 2 * turn)
                for k in range(4 * turn, 4 * turn + 4):
                    j, tile = k % SLOT_BUFS, g * SLOT_BUFS + k
                    act.wait_ge(s["arrived"], tile + 1)
                    by_block = rows[:, j, :].rearrange("p (b u) -> p b u", b=4)
                    for m in range(3):
                        last = act.activation(rows_attr[:, k % 8, m, :].rearrange("p (i u) -> p i u", i=2),
                                              by_block[:, 0:m + 2:m + 1, :], ACT.Identity, scale=attr(tile, 1 + m))
                    last.then_inc(s["rows_ready"], 1)

            for turn in range(4):
                stage_indices(act, env, env.src_idx, 0, turn, s["idx_staged"])
            act.wait_ge(s["loaded"], 16)
            act.wait_ge(s["tail_zeroed"], 1)
            stage_lens(0, 0)
            stage_lens(1, 1)
            keep_lens(0, 0)
            activate(0, 0)
            build(0, 0)
            with act.Fori(0, GRPS) as g:
                for t in range(4):
                    if t % 2 == 0:
                        octet, u = g * 2 + t // 2, t // 2
                        keep_lens(octet + 1, 1 - u)
                        stage_lens(octet + 2, u)
                    act.wait_ge(s["w_made"], g * (SLOT_BUFS // 2) + (2 * t + 2))
                    activate(g * 4 + (t + 1), (t + 1) % 2)
                    build(g, t + 1)
                    act.wait_ge(s["multiplied"], g * SLOT_BUFS + (SLOT_BUFS + 4 * t + 4))
                    stage_indices(act, env, env.src_idx, g + 1, t, s["idx_staged"])

        @block.vector
        def _(dve):
            def build(tile, j):
                dve.tensor_scalar(hot[:, j, :], env.iota_row[:, :], env.dst_rel[:, bass.ds(tile, 1)], None,
                                  ALU.is_equal).then_inc(s["hot_dve"], 1)

            build(2, 2)
            build(3, 3)
            dve.memset(rec[:, TILES:, :], 0.0).then_inc(s["tail_zeroed"], 1)
            dve.memset(acc[:, :, :], 0.0)
            for j in range(4):
                dve.memset(sums[j][:, :], 0.0)
            dve.drain().then_inc(s["added"], 2)
            dve.wait_ge(s["loaded"], 16)
            with dve.Fori(0, GRPS) as g:
                starts = window_starts(env, g, late=2)
                for k in range(SLOT_BUFS):
                    tile, j = g * SLOT_BUFS + k, k % 4
                    dve.wait_ge(s["rows_ready"], tile + 1)
                    dve.wait_ge(s["w_made"], g * (SLOT_BUFS // 2) + (k // 2 + 3))
                    w = w_ps[k // 2 % 2][:, k % 2, :]
                    dve.scalar_tensor_tensor(message[:, j, 0:D], w[:, 0:D], attr(tile, 0), rows[:, k, :], ALU.mult, ALU.mult)
                    w_parts = over_rows(w[:, D:D + 2 * MUL], 3).rearrange("p m (i u) -> p m i u", i=2)
                    dve.tensor_tensor(message[:, j, D:].rearrange("p (i m u) -> p m i u", i=2, m=3),
                                      rows_attr[:, k % 8, :, :].rearrange("p m (i u) -> p m i u", i=2), w_parts,
                                      ALU.mult).then_inc(s["message_ready"], 1)
                    if k % 4 >= 2:
                        build(tile + 4, (k + 4) % 8)
                    dve.wait_ge(s["multiplied"], tile + (SLOT_BUFS - 1))
                    dve.wait_ge(s["added"], tile + 2)
                    window = acc[:, :, bass.ds(starts[k], P)]
                    dve.tensor_tensor(window, window, sums[(k - 2) % 4][:, 0:3 * P].rearrange("p (a n) -> p a n", a=3),
                                      ALU.add).then_inc(s["added"], 1)
            assert SLOTS - (N + E) >= 2 * P

        @block.tensor
        def _(pe):
            def turn_lens(octet, u):
                pe.wait_ge(s["lens_staged"], octet + 1)
                pe.transpose(lens_ps[0:8 * LEN, u * P:(u + 1) * P], lens[:, u, :, :].rearrange("p k l -> p (k l)"),
                             env.ident[:, :]).then_inc(s["lens_turned"], 1)

            def make_hidden(octet, u, half):
                pe.wait_ge(s["lens_ready"], octet + 1)
                for i in range(4):
                    mm = pe.matmul(hidden_ps[0:HID, i * P:(i + 1) * P], fc1[:, 4 * half + i, :], lens_t[:, u, :], start=True,
                                   stop=True)
                mm.then_inc(s["hidden_made"], 1)

            def make_w(first):
                for k in (first, first + 1):
                    mm = pe.matmul(w_ps[k // 2 % 2][:, k % 2, 0:D + 2 * MUL], hidden[:, k // 4 % 2, k % 4, :], w2[:, :],
                                   start=True, stop=True)
                mm.then_inc(s["w_made"], 1)

            pe.sem_inc(s["multiplied"], SLOT_BUFS)
            pe.sem_inc(s["w_made"], 2)
            turn_lens(0, 0)
            make_hidden(0, 0, 0)
            pe.wait_ge(s["hidden_ready"], 1)
            make_w(0)
            with pe.Fori(0, GRPS) as g:
                for k in range(SLOT_BUFS):
                    t, j, tile = k // 4, k % 4, g * SLOT_BUFS + k
                    octet, u = g * 2 + t // 2, t // 2
                    if k % 8 == 0:
                        turn_lens(octet + 1, 1 - u)
                    if k % 4 == 0:
                        if t % 2 == 0:
                            make_hidden(octet, u, 1)
                        else:
                            make_hidden(octet + 1, 1 - u, 0)
                    if k % 4 == 2:
                        pe.wait_ge(s["hidden_ready"], g * 4 + (t + 2))
                    if k % 2 == 0:
                        make_w(k + 2)
                    if j < 2:
                        pe.wait_ge(s["hot_ready"], g * 8 + (2 * t + j + 1))
                    else:
                        pe.wait_ge(s["hot_dve"], g * 8 + (2 * t + j - 1))
                    pe.wait_ge(s["message_ready"], tile + 1)
                    pe.wait_ge(s["added"], tile + 1)
                    pe.matmul(sums[j][:, 0:P], message[:, j, 0:D], hot[:, k % 8, :], start=True, stop=True)
                    for i in range(2):
                        mm = pe.matmul(sums[j][0:vec, (i + 1) * P:(i + 2) * P], message[:, j, D + i * vec:D + (i + 1) * vec],
                                       hot[:, k % 8, :], start=True, stop=True)
                    mm.then_inc(s["multiplied"], 1)

        for k in range(SLOT_BUFS):
            landed[k].passed(16 * GRPS)


def tensor_layer(env, inp, records, out):
    nc = env.nc
    table = nc.dram_tensor("tensor_table", (NPAD, D), F32, kind="Internal").ap()
    with ExitStack() as ctx:
        def sb(name, shape):
            return ctx.enter_context(nc.sbuf_tensor(f"tp_{name}", shape, F32))

        attr = sb("attr", [P, BLKS])
        wy, w_out = sb("wy", [P, D]), sb("w_out", [P, 4, D])
        fc1, w2 = sb("fc1", [8 * LEN, 8, HID]), sb("w2", [HID, D + 2 * MUL])
        tensor_weights(env, inp, wy, w_out, fc1, w2)
        with nc.Block() as block:
            @block.vector
            def _(dve):
                dve.memset(attr[:, :], 0.0)
        whole = (BLKS - 1) * P
        load_columns(env, "attr", [(attr[:, 0:BLKS - 1], inp["node_vec1"][0:whole, :].rearrange("(b p) o -> p (b o)", p=P)),
                                   (attr[0:LAST, BLKS - 1:BLKS], inp["node_vec1"][whole:N, :])])
        project_nodes(env, "tptab", True, None, wy, D, table, scale=attr)
        acc = ctx.enter_context(nc.sbuf_tensor("tp_acc", [P, 3, ACC], F32))
        convolve(env, "conv", table, records, fc1, w2, acc)

        def memory(sb, ps):
            return {"sums": sb("sums", [P, 2, 3, P], F32)}

        def prepare(act, mem, blk, h):
            return act.copy(mem["sums"][:, h, :, :], acc[:, :, bass.ds(blk * P, P)])

        def apply(pe, mem, h, x_t, out):
            pe.matmul(out[:, 0:D], x_t, w_out[:, 0, :], start=True, stop=False)
            for i in range(3):
                mm = pe.matmul(out[:, 0:D], mem["sums"][:, h, i, :], w_out[:, 1 + i, :], start=False, stop=i == 2)
            return mm

        def use(dve, mem, blk, h, out):
            return add_and_measure(env, dve, mem, blk, h, out[:, 0:D], scale=attr)

        per_node_block(env, "tpout", True, prepare, apply, use, memory)
    normalize(env, "norm3", store_output(env, out))


def build(nc, inp, out):
    with ExitStack() as ctx:
        till_last = ctx.enter_context(ExitStack())
        env = Env(nc, ctx, till_last)
        records = nc.dram_tensor("records", (SLOTS, REC), F32, kind="Internal").ap()
        x_table = nc.dram_tensor("x_table", (NPAD, D), F32, kind="Internal").ap()
        setup(env, inp)
        sort_edges(env, inp, records)
        load_sorted(env, records)
        relational_layer(env, inp, x_table)
        gcn_layer(env, inp, x_table)
        gat_layer(env, inp)
        till_last.close()
        tensor_layer(env, inp, records, out)


def kernel(**inputs):
    import numpy as _np
    import concourse.bacc as _bacc
    from concourse import mybir as _mybir
    from concourse.bass_utils import run_bass_kernel_spmd as _run

    nc = _bacc.Bacc("TRN2", target_bir_lowering=False, num_devices=1)
    arrays, inp = {}, {}
    for name, value in inputs.items():
        a = _np.ascontiguousarray(value)
        arrays[f"in_{name}_dram"] = a
        inp[name] = nc.dram_tensor(f"in_{name}_dram", a.shape, _mybir.dt.from_np(a.dtype), kind="ExternalInput").ap()
    out = nc.dram_tensor("out_0_dram", (N, D), F32, kind="ExternalOutput").ap()
    build(nc, inp, out)
    r = _run(nc, [arrays], core_ids=[0])
    return r.results[0]["out_0_dram"]
```

```python
from contextlib import ExitStack
import math

import concourse.bass as bass
from concourse import mybir

F32 = mybir.dt.float32
BF16 = mybir.dt.bfloat16
I32 = mybir.dt.int32
ALU = mybir.AluOpType
ACT = mybir.ActivationFunctionType
AX_X = mybir.AxisListType.X
DVE_ENGINE = mybir.EngineType.DVE

P = 128
N, E, D = 3750, 123750, 128
REL, BASES = 32, 8
HEADS, CH = 8, 16
MUL, HID, LEN = 32, 100, 10
BLKS = -(-N // P)
NPAD = BLKS * P
LAST = N - (BLKS - 1) * P
ACC = NPAD + P

SLOT_BUFS = 16
PHASES = 3
GRPS = -(-(N + E) // (P * SLOT_BUFS * PHASES)) * PHASES
TILES = SLOT_BUFS * GRPS
SLOTS = TILES * P

EP, EC = 125, 990
assert EP * EC == E
SB = 15
SBATCHES = EC // SB
REC = 20
R_SRC, R_TAB, R_DST, R_W, R_W1, R_START, R_EA, R_LEN = 0, 1, 2, 3, 4, 5, 6, 10
FIRSTS = -(-TILES // P)
AHEAD = 3
BIG = 1e30
EPS = 1e-5


class Signal:

    def __init__(self, sem):
        self.sem, self.base = sem, 0

    def at(self, n):
        return self.base + n

    def passed(self, n):
        self.base += n


class Env:

    def __init__(self, nc, ctx, till_last):
        self.nc, self.ctx, self.till_last, self.signals = nc, ctx, till_last, {}

    def sig(self, name):
        if name not in self.signals:
            self.signals[name] = Signal(self.ctx.enter_context(self.nc.semaphore(name)))
        return self.signals[name]

    def keep(self, name, shape, dt, ctx=None):
        t = (ctx or self.ctx).enter_context(self.nc.sbuf_tensor(name, shape, dt))
        return t


def stage_memory(nc, ctx, tag):
    def sb(name, shape, dt):
        return ctx.enter_context(nc.sbuf_tensor(f"{tag}_{name}", shape, dt))

    def ps(name, shape, dt):
        return ctx.enter_context(nc.psum_tensor(f"{tag}_{name}", shape, dt))

    return sb, ps


def over_columns(ap, count):
    return ap.unsqueeze(2).to_broadcast([ap.shape[0], ap.shape[1], count])


def over_rows(ap, count):
    return ap.unsqueeze(1).to_broadcast([ap.shape[0], count, ap.shape[1]])


def setup(env, inp):
    nc = env.nc
    env.ident = env.keep("ident", [P, P], F32)
    env.ident_bf = env.keep("ident_bf", [P, P], BF16)
    env.iota_bf = env.keep("iota_bf", [P, P], BF16)
    env.iota_row = env.keep("iota_row", [P, P], F32)
    env.above = env.keep("above", [P, P], F32)
    env.below = env.keep("below", [P, P], F32)
    env.ones = env.keep("ones", [P, P], F32)
    env.tile_mask = env.keep("tile_mask", [P, SLOT_BUFS], F32)
    env.head_mask = env.keep("head_mask", [P, HEADS], F32)
    env.head_sel = env.keep("head_sel", [P, HEADS], F32)
    env.head_sel_t = env.keep("head_sel_t", [HEADS, P], F32)
    env.head_rows = env.keep("head_rows", [P, P], F32)
    env.tile_sel = env.keep("tile_sel", [P, SLOT_BUFS], F32)
    env.other_tile = env.keep("other_tile", [P, SLOT_BUFS], F32)
    env.first_idx = env.keep("first_idx", [P, FIRSTS], I32)
    env.x = env.keep("x", [P, BLKS + 1, D], F32)
    env.stats = env.keep("stats", [P, BLKS, 6], F32)
    env.mean = env.keep("mean", [P, BLKS], F32)
    env.spread = env.keep("spread", [P, BLKS], F32)
    env.rstd = env.keep("rstd", [P, BLKS], F32)
    env.eps = env.keep("eps", [P, 1], F32)
    env.src_idx = env.keep("src_idx", [P, TILES + PHASES * SLOT_BUFS], I32)
    env.dst_rel = env.keep("dst_rel", [P, TILES + SLOT_BUFS], F32)
    env.win = env.keep("win", [1, 2 + TILES], I32)
    env.idx_stage = env.keep("idx_stage", [P, SLOT_BUFS], I32)
    env.tab_idx = env.keep("tab_idx", [P, TILES + SLOT_BUFS], I32, env.till_last)
    env.w = env.keep("w", [P, TILES + SLOT_BUFS], F32, env.till_last)
    env.w1 = env.keep("w1", [P, TILES + SLOT_BUFS], F32, env.till_last)
    env.start = env.keep("start", [P, TILES + SLOT_BUFS], F32, env.till_last)
    zeroed, consts, x_in = env.sig("x_zeroed"), env.sig("consts"), env.sig("x_loaded")
    sel_t, stepped = env.sig("sel_transposed"), env.sig("const_step")
    with ExitStack() as ctx:
        sb, ps = stage_memory(nc, ctx, "setup")
        pt = ps("pt", [P, 512], F32)
        block = ctx.enter_context(nc.Block())

        @block.gpsimd
        def _(pool):
            pool.memset(env.ident[:, :], 0.0)
            pool.memset(env.above[:, :], 1.0)
            pool.memset(env.below[:, :], 1.0)
            pool.memset(env.ones[:, :], 1.0)
            pool.memset(env.tile_mask[:, :], 1.0)
            pool.memset(env.head_mask[:, :], 1.0)
            pool.memset(env.eps[:, :], EPS)
            pool.iota(env.iota_row[:, :], pattern=[[1, P]], base=0, channel_multiplier=0,
                      allow_small_or_imprecise_dtypes=True).then_inc(stepped.sem, 1)
            pool.wait_ge(stepped.sem, 1)
            pool.affine_select(out=env.ident[:, :], in_=env.ident[:, :], compare_op=ALU.not_equal,
                               fill=1.0, base=0, pattern=[[-1, P]], channel_multiplier=1)
            pool.affine_select(out=env.above[:, :], in_=env.above[:, :], compare_op=ALU.is_gt,
                               fill=0.0, base=0, pattern=[[1, P]], channel_multiplier=-1)
            pool.affine_select(out=env.below[:, :], in_=env.below[:, :], compare_op=ALU.is_gt,
                               fill=0.0, base=0, pattern=[[-1, P]], channel_multiplier=1)
            for mask, width, count in ((env.tile_mask, HEADS, SLOT_BUFS), (env.head_mask, CH, HEADS)):
                pool.affine_select(out=mask[:, :], in_=mask[:, :], compare_op=ALU.is_ge, fill=0.0,
                                   base=0, pattern=[[-width, count]], channel_multiplier=1)
            pool.memset(env.win[:, 0:2], N)
            pool.memset(env.idx_stage[:, :], 0).then_inc(stepped.sem, 1)
            pool.wait_ge(stepped.sem, 2)
            for mask, width, count in ((env.tile_mask, HEADS, SLOT_BUFS), (env.head_mask, CH, HEADS)):
                pool.affine_select(out=mask[:, :], in_=mask[:, :], compare_op=ALU.is_ge, fill=0.0,
                                   base=width - 1, pattern=[[width, count]],
                                   channel_multiplier=-1).then_inc(consts.sem, 1)

        @block.vector
        def _(dve):
            dve.memset(env.x[:, BLKS - 1:, :], 0.0).then_inc(zeroed.sem, 1)
            for t, fill in ((env.src_idx, 0), (env.tab_idx, 0), (env.dst_rel, 200.0), (env.w, 0.0),
                            (env.w1, 0.0), (env.start, 0.0)):
                dve.memset(t[:, TILES:], fill)
            dve.wait_ge(consts.sem, 2)
            dve.tensor_copy(env.ident_bf[:, :], env.ident[:, :])
            dve.tensor_copy(env.iota_bf[:, :], env.iota_row[:, :])
            dve.tensor_scalar(env.other_tile[:, :], env.tile_mask[:, :], BIG, -BIG, ALU.mult, ALU.add)
            dve.tensor_reduce(env.tile_sel[:, :], env.ident[:, :].rearrange("p (c k) -> p k c", k=SLOT_BUFS),
                              AX_X, ALU.add)
            dve.tensor_reduce(env.head_sel[:, :], env.ident[:, :].rearrange("p (c h) -> p h c", h=HEADS),
                              AX_X, ALU.add).then_inc(consts.sem, 1)
            dve.wait_ge(sel_t.sem, 1)
            dve.tensor_copy(env.head_sel_t[:, :], pt[0:HEADS, 0:P])
            dve.tensor_copy(env.head_rows[:, :].rearrange("p (h c) -> p h c", c=CH), over_columns(env.head_sel[:, :], CH))

        @block.tensor
        def _(pe):
            pe.wait_ge(consts.sem, 3)
            pe.transpose(pt[0:HEADS, 0:P], env.head_sel[:, :], env.ident[:, :]).then_inc(sel_t.sem, 1)

        @block.sync
        def _(sp):
            sp.dma_start(env.x[:, 0:BLKS - 1, :],
                         inp["x"][0:(BLKS - 1) * P, :].rearrange("(b p) f -> p b f", p=P)).then_inc(x_in.sem, 16)
            sp.wait_ge(zeroed.sem, 1)
            sp.dma_start(env.x[0:LAST, BLKS - 1, :], inp["x"][(BLKS - 1) * P:N, :]).then_inc(x_in.sem, 16)
            sp.wait_ge(x_in.sem, 32)


def slot_rows(dve, rows_out, at, low, tile_no):
    dve.tensor_scalar(low, at, P - 1, None, ALU.bitwise_and)
    dve.tensor_scalar(tile_no, at, 7, None, ALU.arith_shift_right)
    dve.drain()
    return dve.scalar_tensor_tensor(rows_out, low, float(TILES), tile_no, ALU.mult, ALU.add)


def one_hot_lo(dve, env, hot_lo, lo, b, h, k):
    return dve.tensor_scalar(hot_lo[:, h, k, :], env.iota_bf[0:EP, :], lo[:, bass.ds(b * SB + k, 1)], None, ALU.is_equal)


def one_hots_hi(dve, env, hot_hi, hi, b, h):
    return dve.tensor_tensor(hot_hi[:, h, :, :], over_rows(env.iota_bf[0:EP, 0:BLKS], SB),
                             over_columns(hi[:, bass.ds(b * SB, SB)], BLKS), ALU.is_equal)


def sort_edges(env, inp, records, relation_layers, weights_dram, table):
    assert P == 128
    nc = env.nc
    with ExitStack() as ctx:
        sb, ps = stage_memory(nc, ctx, "sort")
        src_i = sb("src_i", [EP, EC], I32)
        dst_i = sb("dst_i", [EP, EC], I32)
        typ_i = sb("typ_i", [EP, EC], I32)
        tab_f = sb("tab_f", [EP, EC], F32)
        dst_f = sb("dst_f", [EP, EC], F32)
        lo_i = sb("lo_i", [EP, EC], I32)
        hi_i = sb("hi_i", [EP, EC], I32)
        lo = sb("lo", [EP, EC + SB], F32)
        hi = sb("hi", [EP, EC + SB], BF16)
        w_in = sb("w_in", [EP, EC], F32)
        w1_in = sb("w1_in", [EP, EC], F32)
        hot_lo = sb("hot_lo", [EP, 2, SB, P], BF16)
        hot_hi = sb("hot_hi", [EP, 2, SB, BLKS], BF16)
        zero_lo = sb("zero_lo", [EP, P], BF16)
        count1 = sb("count1", [P, BLKS], F32)
        totals = sb("totals", [P, BLKS], F32)
        cum = sb("cum", [P, BLKS], F32)
        zeros = sb("zeros", [P, BLKS], F32)
        first = sb("first", [P, BLKS], F32)
        next_slot = sb("next_slot", [P, BLKS], F32)
        node_i = sb("node_i", [P, BLKS, 3], I32)
        node_row = sb("node_row", [P, BLKS], I32)
        node_rec = sb("node_rec", [P, BLKS, REC], F32)
        pad_rec = sb("pad_rec", [P, TILES - (N + E) // P, REC], F32)
        recs = sb("recs", [EP, 2, SB, REC], F32)
        sigs = {n: env.sig(f"sort_{n}") for n in (
            "loaded", "prepared", "hot", "counted", "summed", "count1_ready", "node_rows", "node_recs",
            "self_written", "pads_written", "first_ready")}
        s = {n: v.sem for n, v in sigs.items()}

        def load_edges(sp):
            for tile, name in ((dst_i, "dst"), (src_i, "src"), (typ_i, "edge_type_32"), (w_in, "edge_weight")):
                sp.dma_start(tile[:, :], inp[name].rearrange("(p c) -> p c", c=EC)).then_inc(s["loaded"], 16)
            sp.dma_start(w1_in[:, :], inp["edge_weight1"].rearrange("(p c) o -> p (c o)", c=EC)).then_inc(s["loaded"], 16)

        relation_weights(env, relation_layers, weights_dram, load_edges)
        with ExitStack() as inner:
            cnt = inner.enter_context(nc.psum_tensor("sort_cnt", [P, 512], F32))
            sums = inner.enter_context(nc.psum_tensor("sort_sums", [P, 512], F32))
            load_table, store_table, table_on_act, start_table, half_table = first_table(
                env, *stage_memory(nc, inner, "count"), weights_dram[0:REL, :], table)
            block = inner.enter_context(nc.Block())

            @block.sync
            def _(sp):
                load_table(sp)
                sp.wait_ge(s["node_recs"], 2)
                lane, tile0 = (N + E) % P, (N + E) // P
                assert lane and tile0 + 1 < TILES
                rows = records.rearrange("(p q) k -> p q k", p=P)
                sp.dma_start(rows[:, tile0 + 1:TILES, :], pad_rec[:, 1:, :]).then_inc(s["pads_written"], 16)
                sp.dma_start(rows[lane:P, tile0, :], pad_rec[lane:P, 0, :]).then_inc(s["pads_written"], 16)
                store_table(sp)
                sp.wait_ge(s["pads_written"], 32)

            @block.vector
            def _(dve):
                dve.memset(zero_lo[:, :], 0.0)
                dve.memset(zeros[:, :], 0.0)
                dve.memset(lo[:, EC:], 0.0)
                dve.memset(hi[:, EC:], 0.0)
                dve.memset(recs[:, :, :, :], 0.0)
                dve.wait_ge(s["loaded"], 5 * 16)
                dve.tensor_scalar(lo_i[:, :], dst_i[:, :], P - 1, None, ALU.bitwise_and)
                dve.tensor_scalar(hi_i[:, :], dst_i[:, :], 7, None, ALU.arith_shift_right)
                dve.drain()
                dve.tensor_copy(lo[:, 0:EC], lo_i[:, :])
                dve.tensor_copy(hi[:, 0:EC], hi_i[:, :])
                dve.tensor_copy(dst_f[:, :], dst_i[:, :])
                dve.tensor_copy(tab_f[:, :], typ_i[:, :])
                dve.drain()
                dve.scalar_tensor_tensor(tab_f[:, :], src_i[:, :], float(REL), tab_f[:, :], ALU.mult,
                                         ALU.add).then_inc(s["prepared"], 1)
                dve.drain()
                with dve.Fori(0, SBATCHES // 2) as i:
                    for h in range(2):
                        b = i * 2 + h
                        dve.wait_ge(s["counted"], b + 1)
                        one_hots_hi(dve, env, hot_hi, hi, b, h)
                        for k in range(SB):
                            last = one_hot_lo(dve, env, hot_lo, lo, b, h, k)
                        last.then_inc(s["hot"], 1)
                dve.wait_ge(s["counted"], SBATCHES + 3)
                dve.tensor_scalar(count1[:, :], cnt[:, 0:BLKS], 1.0, None, ALU.add).then_inc(s["count1_ready"], 1)
                dve.wait_ge(s["summed"], 1)
                dve.tensor_copy(totals[:, :], sums[:, BLKS:2 * BLKS])
                dve.drain()
                dve.tensor_tensor_scan(cum[:, :], zeros[:, :], totals[:, :], 0.0, ALU.add, ALU.add)
                dve.drain()
                dve.tensor_tensor(cum[:, :], cum[:, :], totals[:, :], ALU.subtract)
                dve.drain()
                dve.tensor_tensor(first[:, :], cum[:, :], sums[:, 0:BLKS], ALU.add)
                dve.drain()
                dve.tensor_scalar(next_slot[:, :], first[:, :], 1.0, None, ALU.add)
                dve.tensor_copy(node_i[:, :, 0], first[:, :])
                dve.drain()
                slot_rows(dve, node_row[:, :], *(node_i[:, :, k] for k in range(3))).then_inc(s["node_rows"], 1)

            @block.tensor
            def _(pe):
                pe.wait_ge(s["prepared"], 1)
                pe.matmul(cnt[:, 0:BLKS], zero_lo[:, :], zero_lo[:, 0:BLKS], start=True, stop=True,
                          skip_group_check=True).then_inc(s["counted"], 2)

                def count(b, h):
                    pe.wait_ge(s["hot"], b + 1)
                    for k in range(SB):
                        mm = pe.matmul(cnt[:, 0:BLKS], hot_lo[:, h, k, :], hot_hi[:, h, k, :], start=False,
                                       stop=False, skip_group_check=True)
                    mm.then_inc(s["counted"], 1)

                start_table(pe)
                with pe.Fori(0, BLKS // 2) as i:
                    for q in range(4):
                        count(i * 4 + q, q % 2)
                        half_table(pe, i * 2 + q // 2, q % 2)
                done = BLKS * 2
                assert done <= SBATCHES and SBATCHES % 2 == 0
                with pe.Fori(0, (SBATCHES - done) // 2) as i:
                    for h in range(2):
                        count(i * 2 + (done + h), h)
                pe.matmul(cnt[:, 0:BLKS], zero_lo[:, :], zero_lo[:, 0:BLKS], start=False, stop=True,
                          skip_group_check=True).then_inc(s["counted"], 1)
                pe.wait_ge(s["count1_ready"], 1)
                pe.matmul(sums[:, 0:BLKS], env.above[:, :], count1[:, :], start=True, stop=True)
                pe.matmul(sums[:, BLKS:2 * BLKS], env.ones[:, :], count1[:, :], start=True,
                          stop=True).then_inc(s["summed"], 1)

            @block.scalar
            def _(act):
                table_on_act(act)

            @block.gpsimd
            def _(pool):
                pool.memset(node_rec[:, :, :], 0.0)
                pool.memset(pad_rec[:, :, :], 0.0).then_inc(s["node_recs"], 1)
                pool.wait_ge(s["node_recs"], 1)
                pool.memset(node_rec[:, :, R_START:R_START + 1], 1.0)
                for col, mult in ((R_SRC, 1), (R_DST, 1), (R_TAB, REL)):
                    pool.iota(node_rec[:, :, col], pattern=[[P * mult, BLKS]], base=0, channel_multiplier=mult,
                              allow_small_or_imprecise_dtypes=True)
                pool.memset(pad_rec[:, :, R_DST:R_DST + 1], float(N))
                pool.memset(pad_rec[:, :, R_START:R_START + 1], 1.0).then_inc(s["node_recs"], 1)
                pool.wait_ge(s["node_recs"], 2)
                pool.wait_ge(s["node_rows"], 1)
                for b in range(BLKS):
                    m = P if b < BLKS - 1 else LAST
                    pool.indirect_dma_start(records, bass.IndirectOffsetOnAxis(ap=node_row[0:m, b:b + 1], axis=0),
                                            node_rec[0:m, b, :], None).then_inc(s["self_written"], 16)
                pool.wait_ge(s["self_written"], 16 * BLKS)

        ea_in = sb("ea_in", [EP, EC, 4], F32)
        len_in = sb("len_in", [EP, EC, LEN], F32)
        dst_now = sb("dst_now", [EP, 2, SB], F32)
        hot_lo_t = sb("hot_lo_t", [P, 2, EP], F32)
        heads = sb("heads", [P, 2, BLKS], F32)
        same = sb("same", [EP, 2, EP], F32)
        own_head = sb("own_head", [EP, BLKS], F32)
        in_column = sb("in_column", [EP, SB], F32)
        before = sb("before", [EP, SB], F32)
        slot_i = sb("slot_i", [EP, 3, SB], I32)
        rows = sb("rows", [EP, 2, SB], I32)
        taken = ps("taken", [P, 512], F32)
        hot_ps = [ps(f"hot_ps{j}", [P, 1024], BF16) for j in range(2)]
        dst_ps = [ps(f"dst_ps{j}", [EP, 512], F32) for j in range(2)]
        head_ps = [ps(f"head_ps{j}", [EP, 512], F32) for j in range(2)]
        s = {n: env.sig(f"rank_{n}").sem for n in (
            "hot", "dst_staged", "recs_staged", "turned", "copied", "dst_wide", "ranked", "heads_ready",
            "looked", "added", "rows_ready", "attr_in")}
        scattered = [env.sig(f"rank_scattered{h}").sem for h in range(2)]
        issued = env.sig("dma_turn").sem
        block = ctx.enter_context(nc.Block())
        half = SBATCHES // 2
        per_batch = 16 * SB

        @block.sync
        def _(sp):
            sp.dma_start(ea_in[:, :, :], inp["edge_attr_4"].rearrange("(p c) k -> p c k", c=EC)).then_inc(s["attr_in"], 16)
            sp.dma_start(len_in[:, :, :], inp["edge_attr_10"].rearrange("(p c) k -> p c k", c=EC)).then_inc(s["attr_in"], 16)

        @block.scalar
        def _(act):
            def batch(i, h):
                b = i * 2 + h
                cols = bass.ds(b * SB, SB)
                if not (isinstance(i, int) and i == 0):
                    act.wait_ge(scattered[h], i * per_batch)
                act.copy(dst_now[:, h, :], dst_f[:, cols]).then_inc(s["dst_staged"], 1)
                for k in range(SB):
                    j = (h * SB + k) % 2
                    act.wait_ge(s["turned"], b * SB + k + 1)
                    act.wait_ge(s["looked"], b * SB + k + 1)
                    act.copy(hot_lo_t[:, j, :], hot_ps[j][:, 0:EP]).then_inc(s["copied"], 1)
                act.copy(recs[:, h, :, R_SRC], src_i[:, cols])
                act.copy(recs[:, h, :, R_TAB], tab_f[:, cols])
                act.copy(recs[:, h, :, R_DST], dst_f[:, cols])
                act.copy(recs[:, h, :, R_W], w_in[:, cols])
                act.copy(recs[:, h, :, R_W1], w1_in[:, cols])
                if isinstance(i, int) and b == 0:
                    act.wait_ge(s["attr_in"], 32)
                act.copy(recs[:, h, :, R_EA:R_EA + 4], ea_in[:, cols, :])
                act.copy(recs[:, h, :, R_LEN:R_LEN + LEN], len_in[:, cols, :]).then_inc(s["recs_staged"], 1)

            for h in range(2):
                batch(0, h)
            with act.Fori(1, half) as i:
                for h in range(2):
                    batch(i, h)

        @block.vector
        def _(dve):
            dve.sem_inc(s["ranked"], 2)
            one_hots_hi(dve, env, hot_hi, hi, 0, 0)
            for k in range(SB):
                last = one_hot_lo(dve, env, hot_lo, lo, 0, 0, k)
            last.then_inc(s["hot"], 1)

            def batch(i, h):
                b = i * 2 + h
                for k in range(SB):
                    c, j = b * SB + k, (h * SB + k) % 2
                    dve.wait_ge(s["added"], c + 1)
                    dve.tensor_tensor(heads[:, j, :], taken[:, 0:BLKS], next_slot[:, :],
                                      ALU.add).then_inc(s["heads_ready"], 1)
                    if k == 0:
                        one_hots_hi(dve, env, hot_hi, hi, b + 1, 1 - h)
                    ahead = one_hot_lo(dve, env, hot_lo, lo, b + 1, 1 - h, k)
                    dve.wait_ge(s["dst_wide"], c + 1)
                    dve.scalar_tensor_tensor(same[:, j, :], dst_ps[j][:, 0:EP], dst_now[:, h, k:k + 1],
                                             env.below[0:EP, 0:EP], ALU.is_equal, ALU.mult,
                                             accum_out=in_column[:, k:k + 1]).then_inc(s["ranked"], 1)
                    dve.wait_ge(s["looked"], c + 3)
                    dve.tensor_tensor_reduce(own_head[:, :], head_ps[j][:, 0:BLKS], hot_hi[:, h, k, :], 1.0, 0.0,
                                             ALU.mult, ALU.add, before[:, k:k + 1])
                ahead.then_inc(s["hot"], 1)
                dve.drain()
                if not (isinstance(i, int) and i == 0):
                    dve.wait_ge(scattered[h], i * per_batch)
                dve.tensor_tensor(slot_i[:, 0, :], in_column[:, :], before[:, :], ALU.add)
                dve.drain()
                slot_rows(dve, rows[:, h, :], *(slot_i[:, m, :] for m in range(3))).then_inc(s["rows_ready"], 1)

            for h in range(2):
                batch(0, h)
            with dve.Fori(1, half) as i:
                for h in range(2):
                    batch(i, h)

        @block.tensor
        def _(pe):
            pe.sem_inc(s["looked"], 2)
            pe.matmul(taken[:, 0:BLKS], zero_lo[:, :], zero_lo[:, 0:BLKS], start=True, stop=True,
                      skip_group_check=True).then_inc(s["added"], 1)

            def ahead(b, h, k):
                j = (h * SB + k) % 2
                pe.transpose(hot_ps[j][:, 0:EP], hot_lo[:, h, k, :], env.ident_bf[0:EP, 0:EP]).then_inc(s["turned"], 1)
                pe.wait_ge(s["ranked"], b * SB + k + 1)
                pe.matmul(dst_ps[j][:, 0:EP], dst_now[:, h, k:k + 1].to_broadcast([EP, EP]),
                          env.ident[0:EP, 0:EP], start=True, stop=True).then_inc(s["dst_wide"], 1)

            with pe.Fori(0, half) as i:
                for h in range(2):
                    b = i * 2 + h
                    pe.wait_ge(s["hot"], b + 1)
                    pe.wait_ge(s["dst_staged"], b + 1)
                    ahead(b, h, 0)
                    ahead(b, h, 1)
                    for k in range(SB):
                        c, j = b * SB + k, (h * SB + k) % 2
                        pe.wait_ge(s["copied"], c + 1)
                        pe.wait_ge(s["heads_ready"], c + 1)
                        pe.matmul(head_ps[j][:, 0:BLKS], hot_lo_t[:, j, :], heads[:, j, :], start=True,
                                  stop=True).then_inc(s["looked"], 1)
                        pe.matmul(taken[:, 0:BLKS], hot_lo[:, h, k, :], hot_hi[:, h, k, :], start=False, stop=True,
                                  skip_group_check=True).then_inc(s["added"], 1)
                        if k + 2 < SB:
                            ahead(b, h, k + 2)

        @block.gpsimd
        def _(pool):
            with pool.Fori(0, half) as i:
                for h in range(2):
                    pool.wait_ge(s["recs_staged"], i * 2 + (h + 1))
                    pool.wait_ge(s["rows_ready"], i * 2 + (h + 1))
                    pool.sem_inc(issued, 1)
                    for k in range(SB):
                        pool.indirect_dma_start(records, bass.IndirectOffsetOnAxis(ap=rows[:, h, k:k + 1], axis=0),
                                                recs[:, h, k, :], None).then_inc(scattered[h], 16)
            for h in range(2):
                pool.wait_ge(scattered[h], half * per_batch)


def load_sorted(env, records):
    nc = env.nc
    with ExitStack() as ctx:
        sb, ps = stage_memory(nc, ctx, "reload")
        rec = sb("rec", [P, TILES, REC], F32)
        dst = sb("dst", [P, FIRSTS * P], F32)
        base = ps("base", [P, 1024], F32)
        firsts = ps("firsts", [P, 512], F32)
        got, dst_ready, wide = (env.sig(f"reload_{n}").sem for n in ("got", "dst_ready", "wide"))
        block = ctx.enter_context(nc.Block())

        @block.sync
        def _(sp):
            sp.dma_start(rec[:, :, :], records.rearrange("(p q) k -> p q k", p=P)).then_inc(got, 16)

        @block.vector
        def _(dve):
            dve.memset(dst[:, TILES:], 0.0)
            dve.wait_ge(got, 16)
            dve.tensor_copy(dst[:, 0:TILES], rec[:, :, R_DST]).then_inc(dst_ready, 1)
            dve.tensor_copy(env.win[:, 2:], rec[0:1, :, R_DST])
            dve.tensor_copy(env.src_idx[:, 0:TILES], rec[:, :, R_SRC])
            dve.tensor_copy(env.tab_idx[:, 0:TILES], rec[:, :, R_TAB])
            dve.wait_ge(wide, 1)
            dve.tensor_tensor(env.dst_rel[:, 0:TILES], dst[:, 0:TILES], base[:, 0:TILES], ALU.subtract)
            dve.tensor_copy(env.first_idx[:, :], firsts[:, 0:FIRSTS])

        @block.scalar
        def _(act):
            act.wait_ge(got, 16)
            act.copy(env.w[:, 0:TILES], rec[:, :, R_W])
            act.copy(env.w1[:, 0:TILES], rec[:, :, R_W1])
            act.copy(env.start[:, 0:TILES], rec[:, :, R_START])

        @block.tensor
        def _(pe):
            pe.wait_ge(dst_ready, 1)
            assert FIRSTS * P == 1024
            for half in range(2):
                cols = slice(half * 512, half * 512 + 512)
                pe.matmul(base[:, cols], env.ones[0:1, :], dst[0:1, cols], start=True, stop=True)
            for j in range(FIRSTS):
                mm = pe.matmul(firsts[:, j:j + 1], dst[0:1, j * P:(j + 1) * P], env.ones[0:1, 0:1], start=True, stop=True)
            mm.then_inc(wide, 1)


def relation_weights(env, layers, weights_dram, early_loads):
    nc = env.nc
    cols = 512
    halves = 2
    chunks = D * D // cols // halves
    groups = chunks // 4
    parts = halves * len(layers)
    with ExitStack() as ctx:
        sb, ps = stage_memory(nc, ctx, "relw")
        basis_sb = sb("basis", [parts * BASES, D * D // halves], F32)
        coeff_t = sb("coeff_t", [parts * BASES, P], F32)
        mixed = sb("mixed", [P, 2, 4 * cols], F32)
        mix_ps = [ps(f"mix{j}", [P, cols], F32) for j in range(4)]
        s = {n: env.sig(f"relw_{n}").sem for n in ("loaded", "zeroed", "mixed", "copied")}
        stored = [env.sig(f"relw_stored{h}").sem for h in range(2)]
        assert parts * REL == P
        block = ctx.enter_context(nc.Block())

        def copy_out(eng, copy, parity):
            for c in range(parity, chunks, 2):
                group, k = c // 4, c % 4
                eng.wait_ge(s["mixed"], c + 1)
                if group >= 2 and k == parity:
                    eng.wait_ge(stored[group % 2], 16 * halves * (group // 2))
                copy(mixed[:, group % 2, k * cols:(k + 1) * cols], mix_ps[c % 4][:, :]).then_inc(s["copied"], 1)

        @block.vector
        def _(dve):
            dve.memset(coeff_t[:, :], 0.0).then_inc(s["zeroed"], 1)
            copy_out(dve, dve.tensor_copy, 1)

        @block.scalar
        def _(act):
            copy_out(act, act.copy, 0)

        @block.tensor
        def _(pe):
            pe.wait_ge(s["loaded"], 32 * parts)
            for c in range(chunks):
                if c >= 4 and c % 4 == 0:
                    pe.wait_ge(s["copied"], c)
                pe.matmul(mix_ps[c % 4][:, :], coeff_t[:, :], basis_sb[:, c * cols:(c + 1) * cols], start=True,
                          stop=True).then_inc(s["mixed"], 1)

        @block.sync
        def _(sp):
            sp.wait_ge(s["zeroed"], 1)
            for half in range(halves):
                for k, (basis, coeff) in enumerate(layers):
                    part = half * len(layers) + k
                    own = slice(part * BASES, (part + 1) * BASES)
                    features = slice(half * D // halves, (half + 1) * D // halves)
                    sp.dma_start(coeff_t[own, part * REL:(part + 1) * REL], coeff.rearrange("r b -> b r"),
                                 allow_slow_non_contiguous=True).then_inc(s["loaded"], 16)
                    sp.dma_start(basis_sb[own, :], basis[:, features, :].rearrange("b d f -> b (d f)")).then_inc(s["loaded"], 16)
            early_loads(sp)
            for group in range(groups):
                sp.wait_ge(s["copied"], 4 * group + 4)
                for half in range(halves):
                    at = half * (D * D // halves) + group * 4 * cols
                    sp.dma_start(weights_dram[:, at:at + 4 * cols],
                                 mixed[half * P // halves:(half + 1) * P // halves, group % 2, :]).then_inc(stored[group % 2], 16)
            for h in range(2):
                sp.wait_ge(stored[h], 16 * halves * groups // 2)


def first_table(env, sb, ps, weights_dram, table):
    cols = 512
    chunks = REL * D // cols
    weights = sb("table_weights", [P, REL, D], F32)
    x_now = sb("x_now", [P, D], F32)
    x_t = sb("x_t", [P, P], F32)
    row = sb("row", [P, 2, REL * D], F32)
    turn_ps = ps("table_turn", [P, 512], F32)
    out_ps = [ps(f"table_out{j}", [P, cols], F32) for j in range(4)]
    s = {n: env.sig(f"table1_{n}").sem for n in ("weights_in", "x_staged", "turned", "ready", "made", "out")}
    stored = [env.sig(f"table1_stored{h}").sem for h in range(2)]
    rows = table.rearrange("(n r) f -> n (r f)", r=REL)

    def load(sp):
        for h in range(2):
            sp.sem_inc(stored[h], 16)
        sp.dma_start(weights[:, :, :], weights_dram.rearrange("r (d f) -> d r f", d=D)).then_inc(s["weights_in"], 16)

    def store(sp):
        with sp.Fori(0, BLKS // 2) as i:
            for h in range(2):
                sp.wait_ge(s["out"], i * (2 * chunks) + (h + 1) * chunks + 4)
                sp.dma_start(rows[bass.ds(i * (2 * P) + h * P, P), :], row[:, h, :]).then_inc(stored[h], 16)
        for h in range(2):
            sp.wait_ge(stored[h], 16 * (BLKS // 2) + 16)

    def on_act(act):
        act.sem_inc(s["out"], 4)
        with act.Fori(0, BLKS // 2) as i:
            for h in range(2):
                blk = i * 2 + h
                act.wait_ge(s["turned"], blk + 1)
                act.copy(x_now[:, :], env.x[:, bass.ds(blk, 1), :]).then_inc(s["x_staged"], 1)
                act.wait_ge(s["turned"], blk + 2)
                act.copy(x_t[:, :], turn_ps[:, 0:P]).then_inc(s["ready"], 1)
                act.wait_ge(stored[h], i * 16 + 16)
                for c in range(chunks):
                    act.wait_ge(s["made"], blk * chunks + c + 1)
                    act.copy(row[:, h, c * cols:(c + 1) * cols], out_ps[c % 4][:, :]).then_inc(s["out"], 1)

    def start(pe):
        pe.sem_inc(s["turned"], 1)
        pe.wait_ge(s["weights_in"], 16)

    def half(pe, blk, part):
        if part == 0:
            pe.wait_ge(s["x_staged"], blk + 1)
            pe.transpose(turn_ps[:, 0:P], x_now[:, :], env.ident[:, :]).then_inc(s["turned"], 1)
            pe.wait_ge(s["ready"], blk + 1)
        for c in range(part * chunks // 2, (part + 1) * chunks // 2):
            pe.wait_ge(s["out"], blk * chunks + c + 1)
            pe.matmul(out_ps[c % 4][:, :], x_t[:, :], weights[:, 4 * c:4 * c + 4, :].rearrange("d r f -> d (r f)"),
                      start=True, stop=True).then_inc(s["made"], 1)

    return load, store, on_act, start, half


def second_table(env, weights_dram, table, hidden, bias):
    nc = env.nc
    cols = 512
    chunks = REL * D // cols
    with ExitStack() as ctx:
        sb, ps = stage_memory(nc, ctx, "table2")
        weights = sb("weights", [P, REL, D], F32)
        h_t = sb("h_t", [P, 2, P], F32)
        row = sb("row", [P, 2, REL * D], F32)
        bias_sb = sb("bias", [P, 1], F32)
        out_ps = [ps(f"out{j}", [P, cols], F32) for j in range(4)]
        s = {n: env.sig(f"table2_{n}").sem for n in ("bias_in", "weights_in", "ready", "made", "out_act", "out_dve")}
        stored = [env.sig(f"table2_stored{h}").sem for h in range(2)]
        rows = table.rearrange("(n r) f -> n (r f)", r=REL)
        block = ctx.enter_context(nc.Block())

        @block.scalar
        def _(act):
            def produce(blk, h):
                act.wait_ge(s["made"], blk * chunks + chunks)
                act.activation(h_t[:, h, :], hidden[:, bass.ds(blk * P, P)], ACT.Relu, bias=bias_sb[:, 0:1]).then_inc(s["ready"], 1)

            act.sem_inc(s["out_act"], 2)
            act.wait_ge(s["bias_in"], 16)
            produce(0, 0)
            with act.Fori(0, BLKS // 2) as i:
                for h in range(2):
                    blk = i * 2 + h
                    produce(blk + 1, 1 - h)
                    act.wait_ge(stored[h], i * 16 + 16)
                    for c in range(0, chunks, 2):
                        act.wait_ge(s["made"], blk * chunks + (2 * chunks + c + 1))
                        act.copy(row[:, h, c * cols:(c + 1) * cols], out_ps[c % 4][:, :]).then_inc(s["out_act"], 1)

        @block.vector
        def _(dve):
            dve.sem_inc(s["out_dve"], 2)
            with dve.Fori(0, BLKS // 2) as i:
                for h in range(2):
                    blk = i * 2 + h
                    dve.wait_ge(stored[h], i * 16 + 16)
                    for c in range(1, chunks, 2):
                        dve.wait_ge(s["made"], blk * chunks + (2 * chunks + c + 1))
                        dve.tensor_copy(row[:, h, c * cols:(c + 1) * cols], out_ps[c % 4][:, :]).then_inc(s["out_dve"], 1)

        @block.tensor
        def _(pe):
            pe.sem_inc(s["made"], 2 * chunks)
            pe.wait_ge(s["weights_in"], 16)
            with pe.Fori(0, BLKS // 2) as i:
                for h in range(2):
                    blk = i * 2 + h
                    pe.wait_ge(s["ready"], blk + 1)
                    for c in range(chunks):
                        pe.wait_ge(s["out_act" if c % 2 == 0 else "out_dve"], blk * (chunks // 2) + (c // 2 + 1))
                        pe.matmul(out_ps[c % 4][:, :], h_t[:, h, :],
                                  weights[:, 4 * c:4 * c + 4, :].rearrange("d r f -> d (r f)"),
                                  start=True, stop=True).then_inc(s["made"], 1)

        @block.sync
        def _(sp):
            sp.dma_start(bias_sb[:, :], bias.rearrange("(f o) -> f o", o=1)).then_inc(s["bias_in"], 16)
            sp.dma_start(weights[:, :, :], weights_dram.rearrange("r (d f) -> d r f", d=D)).then_inc(s["weights_in"], 16)
            for h in range(2):
                sp.sem_inc(stored[h], 16)
            with sp.Fori(0, BLKS // 2) as i:
                for h in range(2):
                    blk = i * 2 + h
                    sp.wait_ge(s["out_act"], blk * (chunks // 2) + (chunks // 2 + 2))
                    sp.wait_ge(s["out_dve"], blk * (chunks // 2) + (chunks // 2 + 2))
                    sp.dma_start(rows[bass.ds(blk * P, P), :], row[:, h, :]).then_inc(stored[h], 16)
            for h in range(2):
                sp.wait_ge(stored[h], 16 * (BLKS // 2) + 16)


def gather_program(pool, env, table, bufs, landed, free, free_at, staged, staged_at):
    with pool.Fori(0, GRPS) as g:
        for k in range(SLOT_BUFS):
            if k % 4 == 0:
                pool.wait_ge(staged, g * 4 + staged_at(k // 4 + 1))
                pool.wait_ge(free, g * SLOT_BUFS + free_at(k + 4))
                pool.sem_inc(env.sig("dma_turn").sem, 1)
            pool.indirect_dma_start(bufs[:, k, :], None, table,
                                    bass.IndirectOffsetOnAxis(ap=env.idx_stage[:, k:k + 1], axis=0)
                                    ).then_inc(landed[k].sem, 16)


def stage_indices(act, env, idx, g, turn, staged):
    cols = slice(4 * turn, 4 * turn + 4)
    act.copy(env.idx_stage[:, cols], idx[:, bass.ds(g * SLOT_BUFS + 4 * turn, 4)]).then_inc(staged, 1)


def window_starts(env, g, late=0):
    return env.nc.values_load_multi_w_load_instructions(
        env.win[0:1, bass.ds(g * SLOT_BUFS + (2 - late), SLOT_BUFS)], engines=[DVE_ENGINE], min_val=0, max_val=N,
        skip_runtime_bounds_check_because="sorted destinations are node numbers")[1]


def one_hots_on_act(act, env, tile, count, dist, hot, made, made_at, ready, ready_at):
    if ready_at is not None:
        act.wait_ge(ready, ready_at)
    for k in range(count):
        last = act.activation(dist[:, k, :], env.iota_row[:, :], ACT.Abs, scale=-1.0, bias=env.dst_rel[:, bass.ds(tile + k, 1)])
    last.then_inc(made, 1)
    act.wait_ge(made, made_at)
    act.activation(hot, dist[:, 0:count, :], ACT.Relu, scale=-1.0, bias=1.0).then_inc(ready, count)


def sum_over_slots(env, tag, idx, table, weight, acc, degree=False, side=None):
    nc = env.nc
    parts = 2 if degree else 1
    with ExitStack() as ctx:
        sb, ps = stage_memory(nc, ctx, tag)
        rows = sb("rows", [P, SLOT_BUFS, D], F32)
        hot = sb("hot", [P, 4, P], F32)
        sums = [ps(f"sums{j}", [P, 512], F32) for j in range(4)]
        landed = [env.sig(f"landed{k}") for k in range(SLOT_BUFS)]
        names = ("idx_staged", "hot_ready", "multiplied", "added")
        sig = {n: env.sig(f"sum_{n}") for n in names}
        s = {n: v.sem for n, v in sig.items()}
        v = {n: v.at for n, v in sig.items()}
        side_act, side_pe, side_dve, side_dve_first = side(sb, ps) if side else [lambda *of: None] * 4
        block = ctx.enter_context(nc.Block())

        @block.gpsimd
        def _(pool):
            gather_program(pool, env, table, rows, landed, s["multiplied"], v["multiplied"], s["idx_staged"],
                           v["idx_staged"])

        @block.scalar
        def _(act):
            for turn in range(4):
                stage_indices(act, env, idx, 0, turn, s["idx_staged"])
            with act.Fori(0, GRPS) as g:
                side_act(act, g)
                for turn in range(4):
                    act.wait_ge(s["multiplied"], g * SLOT_BUFS + v["multiplied"](SLOT_BUFS + 4 * turn + 4))
                    stage_indices(act, env, idx, g + 1, turn, s["idx_staged"])

        @block.vector
        def _(dve):
            def build(tile, j):
                c = bass.ds(tile, 1)
                dve.tensor_scalar(hot[:, j, :], env.iota_row[:, :], env.dst_rel[:, c], weight[:, c], ALU.is_equal,
                                  ALU.mult).then_inc(s["hot_ready"], 1)

            side_dve_first(dve)
            dve.memset(acc[:, :, :], 0.0)
            dve.drain().then_inc(s["added"], 4)
            for t in range(AHEAD):
                build(t, t)
            with dve.Fori(0, GRPS) as g:
                starts = window_starts(env, g)
                for k in range(SLOT_BUFS):
                    tile = g * SLOT_BUFS + k
                    if k == SLOT_BUFS // 2:
                        side_dve(dve, g)
                    build(tile + AHEAD, (k + AHEAD) % 4)
                    dve.wait_ge(s["multiplied"], g * SLOT_BUFS + v["multiplied"](SLOT_BUFS + k + 1))
                    dve.wait_ge(s["added"], g * SLOT_BUFS + v["added"](k + 4))
                    window = acc[:, :, bass.ds(starts[k], P)]
                    dve.tensor_tensor(window, window, sums[k % 4][:, 0:parts * P].rearrange("p (a n) -> p a n", a=parts),
                                      ALU.add).then_inc(s["added"], 1)

        @block.tensor
        def _(pe):
            pe.sem_inc(s["multiplied"], SLOT_BUFS)
            with pe.Fori(0, GRPS) as g:
                for k in range(SLOT_BUFS):
                    j = k % 4
                    if k == SLOT_BUFS // 4:
                        side_pe(pe, g)
                    pe.wait_ge(landed[k].sem, g * 16 + landed[k].at(16))
                    pe.wait_ge(s["hot_ready"], g * SLOT_BUFS + v["hot_ready"](k + 1))
                    pe.wait_ge(s["added"], g * SLOT_BUFS + v["added"](k + 1))
                    mm = pe.matmul(sums[j][:, 0:P], rows[:, k, :], hot[:, j, :], start=True, stop=True)
                    if degree:
                        mm = pe.matmul(sums[j][:, P:2 * P], env.ones[:, :], hot[:, j, :], start=True, stop=True)
                    mm.then_inc(s["multiplied"], 1)

        for n, count in (("idx_staged", 4 * GRPS + 4), ("hot_ready", TILES + AHEAD), ("multiplied", TILES + SLOT_BUFS),
                         ("added", TILES + 4)):
            sig[n].passed(count)
        for k in range(SLOT_BUFS):
            landed[k].passed(16 * GRPS)


def per_node_block(env, tag, from_x, prepare, apply, use, memory):
    nc = env.nc
    with ExitStack() as ctx:
        sb, ps = stage_memory(nc, ctx, tag)
        mem = memory(sb, ps)
        x_now = sb("x_now", [P, 2, D], F32)
        x_t = sb("x_t", [P, 2, P], F32)
        turn_ps = [ps(f"turn{h}", [P, 512], F32) for h in range(2)]
        out_ps = [ps(f"out{h}", [P, 512], F32) for h in range(2)]
        names = ("x_staged", "turned", "prepared", "applied", "used")
        sig = {n: env.sig(f"node_{n}") for n in names}
        s = {n: v.sem for n, v in sig.items()}
        v = {n: v.at for n, v in sig.items()}
        block = ctx.enter_context(nc.Block())

        @block.scalar
        def _(act):
            def stage_x(blk, h):
                act.copy(x_now[:, h, :], env.x[:, bass.ds(blk, 1), :]).then_inc(s["x_staged"], 1)

            if from_x:
                stage_x(0, 0)
            with act.Fori(0, BLKS // 2) as i:
                for h in range(2):
                    blk = i * 2 + h
                    if from_x:
                        stage_x(blk + 1, 1 - h)
                    act.wait_ge(s["applied"], blk + v["applied"](1))
                    last = prepare(act, mem, blk, h)
                    if from_x:
                        act.wait_ge(s["turned"], blk + v["turned"](1))
                        last = act.copy(x_t[:, h, :], turn_ps[h][:, 0:P])
                    last.then_inc(s["prepared"], 1)

        @block.tensor
        def _(pe):
            def turn(blk, h):
                pe.wait_ge(s["x_staged"], blk + v["x_staged"](1))
                pe.transpose(turn_ps[h][:, 0:P], x_now[:, h, :], env.ident[:, :]).then_inc(s["turned"], 1)

            pe.sem_inc(s["applied"], 2)
            if from_x:
                turn(0, 0)
            with pe.Fori(0, BLKS // 2) as i:
                for h in range(2):
                    blk = i * 2 + h
                    if from_x:
                        turn(blk + 1, 1 - h)
                    pe.wait_ge(s["prepared"], blk + v["prepared"](1))
                    pe.wait_ge(s["used"], blk + v["used"](1))
                    apply(pe, mem, h, x_t[:, h, :], out_ps[h]).then_inc(s["applied"], 1)

        @block.vector
        def _(dve):
            dve.sem_inc(s["used"], 2)
            with dve.Fori(0, BLKS // 2) as i:
                for h in range(2):
                    blk = i * 2 + h
                    dve.wait_ge(s["applied"], blk + v["applied"](3))
                    use(dve, mem, blk, h, out_ps[h]).then_inc(s["used"], 1)

        turns = BLKS + 1 if from_x else 0
        for n, count in (("x_staged", turns), ("turned", turns), ("prepared", BLKS), ("applied", BLKS + 2),
                         ("used", BLKS + 2)):
            sig[n].passed(count)


def add_and_measure(env, dve, mem, blk, h, update, scale=None, bias_row=None):
    x_blk = env.x[:, bass.ds(blk, 1), :].rearrange("p o f -> p (o f)")
    if scale is None:
        dve.tensor_tensor(x_blk, x_blk, update, ALU.add)
    else:
        dve.scalar_tensor_tensor(x_blk, update, scale[:, bass.ds(blk, 1)], x_blk, ALU.mult, ALU.add)
    dve.drain()
    if bias_row is not None:
        dve.tensor_tensor(x_blk, x_blk, bias_row, ALU.add)
        dve.drain()
    return dve.bn_stats(env.stats[:, bass.ds(blk, 1), :].rearrange("p o t -> p (o t)"), x_blk)


def normalize(env, tag, store=None):
    nc = env.nc
    measured, rooted, normed, stored = (env.sig(f"norm_{n}") for n in ("measured", "rooted", "normed", "stored"))
    with nc.Block() as block:
        @block.scalar
        def _(act):
            act.wait_ge(measured.sem, measured.at(1))
            act.activation(env.rstd[:, :], env.rstd[:, :], ACT.Sqrt, bias=env.eps[:, 0:1]).then_inc(rooted.sem, 1)

        @block.vector
        def _(dve):
            (even_mean, even_m2), (odd_mean, odd_m2) = ((env.stats[:, :, k + 1], env.stats[:, :, k + 2]) for k in (0, 3))
            dve.tensor_tensor(env.mean[:, :], even_mean, odd_mean, ALU.add)
            dve.tensor_tensor(env.spread[:, :], even_mean, odd_mean, ALU.subtract)
            dve.tensor_tensor(env.rstd[:, :], even_m2, odd_m2, ALU.add)
            dve.drain()
            dve.tensor_scalar(env.mean[:, :], env.mean[:, :], 0.5, None, ALU.mult)
            dve.scalar_tensor_tensor(env.spread[:, :], env.spread[:, :], 0.25, env.spread[:, :], ALU.mult, ALU.mult)
            dve.drain()
            dve.scalar_tensor_tensor(env.rstd[:, :], env.rstd[:, :], 1.0 / D, env.spread[:, :], ALU.mult,
                                     ALU.add).then_inc(measured.sem, 1)
            dve.wait_ge(rooted.sem, rooted.at(1))
            dve.reciprocal(env.rstd[:, :], env.rstd[:, :])
            dve.drain()
            with dve.Fori(0, BLKS // 2) as i:
                for h in range(2):
                    blk = bass.ds(i * 2 + h, 1)
                    x_blk = env.x[:, blk, :].rearrange("p o f -> p (o f)")
                    dve.tensor_scalar(x_blk, x_blk, env.mean[:, blk], env.rstd[:, blk], ALU.subtract,
                                      ALU.mult).then_inc(normed.sem, 1)

        if store is not None:
            @block.sync
            def _(sp):
                sp.wait_ge(normed.sem, normed.at(BLKS))
                count = store(sp, stored.sem)
                sp.wait_ge(stored.sem, stored.at(16 * count))
                stored.passed(16 * count)

    measured.passed(1)
    rooted.passed(1)
    normed.passed(BLKS)


def store_x(env, table):
    def store(sp, stored):
        sp.dma_start(table.rearrange("(b p) f -> p b f", p=P), env.x[:, 0:BLKS, :]).then_inc(stored, 16)
        return 1
    return store


def store_output(env, out):
    def store(sp, stored):
        sp.dma_start(out[0:(BLKS - 1) * P, :].rearrange("(b p) f -> p b f", p=P), env.x[:, 0:BLKS - 1, :]).then_inc(stored, 16)
        sp.dma_start(out[(BLKS - 1) * P:N, :], env.x[0:LAST, BLKS - 1, :]).then_inc(stored, 16)
        return 2
    return store


def relational_layer(env, inp, weights_dram, table, x_table):
    with ExitStack() as ctx:
        acc = ctx.enter_context(env.nc.sbuf_tensor("rel_acc", [P, 1, ACC], F32))
        sum_over_slots(env, "relsum1", env.tab_idx, table, env.w1, acc)
        second_table(env, weights_dram[REL:2 * REL, :], table, acc[:, 0, :], inp["L0_gnn_bias1"])
        sum_over_slots(env, "relsum2", env.tab_idx, table, env.w1, acc)
        add_rows(env, "relout", acc, inp["L0_gnn_bias2"])
    normalize(env, "norm0", store_x(env, x_table))


def load_columns(env, tag, pairs):
    sig = env.sig("small_loaded")
    with env.nc.Block() as block:
        @block.sync
        def _(sp):
            for to, frm in pairs:
                sp.dma_start(to, frm, allow_slow_non_contiguous=True).then_inc(sig.sem, 16)
            sp.wait_ge(sig.sem, sig.at(16 * len(pairs)))
    sig.passed(16 * len(pairs))


def add_rows(env, tag, acc, bias):
    with ExitStack() as ctx:
        bias_sb = ctx.enter_context(env.nc.sbuf_tensor(f"{tag}_bias", [P, 1], F32))
        load_columns(env, tag, [(bias_sb[:, :], bias.rearrange("(f o) -> f o", o=1))])

        def memory(sb, ps):
            return {"val": sb("val", [P, 2, P], F32)}

        def prepare(act, mem, blk, h):
            return act.activation(mem["val"][:, h, :], acc[:, 0, bass.ds(blk * P, P)], ACT.Identity, bias=bias_sb[:, 0:1])

        def apply(pe, mem, h, x_t, out):
            return pe.transpose(out[:, 0:P], mem["val"][:, h, :], env.ident[:, :])

        def use(dve, mem, blk, h, out):
            return add_and_measure(env, dve, mem, blk, h, out[:, 0:P])

        per_node_block(env, tag, False, prepare, apply, use, memory)


def gcn_layer(env, inp, x_in, side):
    nc = env.nc
    with ExitStack() as ctx:
        acc = ctx.enter_context(nc.sbuf_tensor("gcn_acc", [P, 2, ACC], F32))
        weight = ctx.enter_context(nc.sbuf_tensor("gcn_weight", [P, D], F32))
        bias_row = ctx.enter_context(nc.sbuf_tensor("gcn_bias", [P, D], F32))
        dinv = ctx.enter_context(nc.sbuf_tensor("gcn_dinv", [P, BLKS], F32))
        load_columns(env, "gcn", [(weight[:, :], inp["L1_gnn_weight"]),
                                  (bias_row[:, :], inp["L1_gnn_bias"].partition_broadcast(P))])
        sum_over_slots(env, "gcnsum", env.src_idx, x_in, env.w, acc, degree=True, side=side)
        with ExitStack() as inner:
            deg_ps = inner.enter_context(nc.psum_tensor("gcn_deg", [P, 512], F32))
            turned, floored, rooted = (env.sig(f"gcn_{n}").sem for n in ("deg_turned", "deg_floored", "deg_rooted"))
            block = inner.enter_context(nc.Block())

            @block.tensor
            def _(pe):
                for b in range(BLKS):
                    mm = pe.matmul(deg_ps[:, b:b + 1], acc[0:1, 1, b * P:(b + 1) * P], env.ones[0:1, 0:1], start=True,
                                   stop=True)
                mm.then_inc(turned, 1)

            @block.vector
            def _(dve):
                dve.wait_ge(turned, 1)
                dve.tensor_scalar(dinv[:, :], deg_ps[:, 0:BLKS], 1.0, None, ALU.max).then_inc(floored, 1)
                dve.wait_ge(rooted, 1)
                dve.reciprocal(dinv[:, :], dinv[:, :])

            @block.scalar
            def _(act):
                act.wait_ge(floored, 1)
                act.activation(dinv[:, :], dinv[:, :], ACT.Sqrt).then_inc(rooted, 1)

        def memory(sb, ps):
            return {"agg": sb("agg", [P, 2, P], F32)}

        def prepare(act, mem, blk, h):
            return act.copy(mem["agg"][:, h, :], acc[:, 0, bass.ds(blk * P, P)])

        def apply(pe, mem, h, x_t, out):
            pe.matmul(out[:, 0:D], x_t, weight[:, :], start=True, stop=False)
            return pe.matmul(out[:, 0:D], mem["agg"][:, h, :], weight[:, :], start=False, stop=True)

        def use(dve, mem, blk, h, out):
            return add_and_measure(env, dve, mem, blk, h, out[:, 0:D], scale=dinv, bias_row=bias_row[:, :])

        per_node_block(env, "gcnout", True, prepare, apply, use, memory)
    normalize(env, "norm1")


def project_nodes(env, tag, from_x, prepare, weights, width, table, scale=None):
    nc = env.nc
    with ExitStack() as ctx:
        rows = ctx.enter_context(nc.sbuf_tensor(f"{tag}_rows", [P, BLKS, width], F32))

        def memory(sb, ps):
            return {"own": None if from_x else sb("own", [P, 2, P], F32)}

        def ready(act, mem, blk, h):
            return None if from_x else prepare(act, mem, blk, h)

        def apply(pe, mem, h, x_t, out):
            return pe.matmul(out[:, 0:width], x_t if from_x else mem["own"][:, h, :], weights[:, 0:width], start=True,
                             stop=True)

        def use(dve, mem, blk, h, out):
            to = rows[:, bass.ds(blk, 1), :].rearrange("p o f -> p (o f)")
            if scale is None:
                return dve.tensor_copy(to, out[:, 0:width])
            return dve.tensor_scalar(to, out[:, 0:width], scale[:, bass.ds(blk, 1)], None, ALU.mult)

        per_node_block(env, tag, from_x, ready, apply, use, memory)
        sig = env.sig("table_stored")
        with nc.Block() as block:
            @block.sync
            def _(sp):
                sp.dma_start(table.rearrange("(b p) f -> p b f", p=P), rows[:, :, :]).then_inc(sig.sem, 16)
                sp.wait_ge(sig.sem, sig.at(16))
        sig.passed(16)


def attention_weights(env, tag, w_in, att_src, att_dst, combined):
    nc = env.nc
    with ExitStack() as ctx:
        sb, ps = stage_memory(nc, ctx, tag)
        att = sb("att", [P, 2], F32)
        load_columns(env, tag, [(combined[:, 0:D], w_in), (att[:, 0:1], att_src.rearrange("h (c o) -> (h c) o", o=1)),
                                (att[:, 1:2], att_dst.rearrange("h (c o) -> (h c) o", o=1))])
        per_head = sb("per_head", [P, 2 * HEADS], F32)
        w_t = sb("w_t", [P, P], F32)
        turn_ps, score_ps = ps("turn", [P, 512], F32), ps("score", [P, 512], F32)
        sig = {n: env.sig(f"att_{n}") for n in ("turned", "copied", "scored")}
        block = ctx.enter_context(nc.Block())

        @block.tensor
        def _(pe):
            pe.transpose(turn_ps[:, 0:P], combined[:, 0:D], env.ident[:, :]).then_inc(sig["turned"].sem, 1)
            pe.wait_ge(sig["copied"].sem, sig["copied"].at(1))
            pe.matmul(score_ps[:, 0:2 * HEADS], w_t[:, :], per_head[:, :], start=True, stop=True).then_inc(sig["scored"].sem, 1)

        @block.vector
        def _(dve):
            for k in range(2):
                dve.tensor_scalar(per_head[:, k * HEADS:(k + 1) * HEADS], env.head_mask[:, :], att[:, k:k + 1], None, ALU.mult)
            dve.wait_ge(sig["turned"].sem, sig["turned"].at(1))
            dve.tensor_copy(w_t[:, :], turn_ps[:, 0:P]).then_inc(sig["copied"].sem, 1)
            dve.wait_ge(sig["scored"].sem, sig["scored"].at(1))
            dve.tensor_copy(combined[:, D:D + 2 * HEADS], score_ps[:, 0:2 * HEADS])

        for n in sig:
            sig[n].passed(1)


def segment_flags(env, flags):
    s = {n: env.sig(f"flags_{n}").sem for n in ("wide", "turned", "kept")}

    def side(sb, ps):
        wide = sb("flags_wide", [P, SLOT_BUFS, HEADS], F32)
        turn_ps = ps("flags_turn", [P, 512], F32)

        def on_act(act, g):
            act.wait_ge(s["kept"], g + 1)
            act.copy(wide[:, :, :], over_columns(env.start[:, bass.ds(g * SLOT_BUFS, SLOT_BUFS)], HEADS)).then_inc(s["wide"], 1)

        def on_pe(pe, g):
            pe.wait_ge(s["wide"], g + 1)
            pe.transpose(turn_ps[:, 0:P], wide[:, :, :].rearrange("p c h -> p (c h)"), env.ident[:, :]).then_inc(s["turned"], 1)

        def on_dve_first(dve):
            last = slice(GRPS * P, None)
            for name, fill in (("goes_on", 0.0), ("reset", -BIG), ("lead", 0.0)):
                dve.memset(flags[name][:, last], fill)
                firsts = flags[name][:, 0:GRPS * P].rearrange("p (g e) -> p g e", e=P)[:, :, 0:1]
                dve.memset(firsts, fill)
            dve.memset(flags["entered"][:, GRPS:], -BIG)
            dve.drain().then_inc(s["kept"], 1)

        def on_dve(dve, g):
            cols = bass.ds(g * P + 1, P - 1)
            dve.wait_ge(s["turned"], g + 1)
            starts = turn_ps[:, 1:P]
            dve.tensor_scalar(flags["goes_on"][:, cols], starts, -1.0, 1.0, ALU.mult, ALU.add)
            dve.tensor_scalar(flags["reset"][:, cols], starts, -BIG, None, ALU.mult)
            dve.tensor_scalar(flags["entered"][:, bass.ds(g, 1)], turn_ps[:, 0:1], -BIG, None, ALU.mult).then_inc(s["kept"], 1)
            dve.drain()
            dve.tensor_tensor_scan(flags["lead"][:, cols], flags["reset"][:, cols], flags["reset"][:, cols], 0.0,
                                   ALU.min, ALU.min)

        return on_act, on_pe, on_dve, on_dve_first

    return side


def crossing_runs(env, flags):
    nc = env.nc
    with ExitStack() as ctx:
        sb, ps = stage_memory(nc, ctx, "crossing")
        row_crossed = sb("row_crossed", [P, GRPS], F32)
        by_tile = sb("by_tile", [P, 1024], F32)
        fold_ps = ps("fold", [P, 1024], F32)
        s = {n: env.sig(f"crossing_{n}").sem for n in ("by_tile", "folded")}
        block = ctx.enter_context(nc.Block())

        @block.tensor
        def _(pe):
            pe.wait_ge(s["by_tile"], 1)
            for half in range(2):
                mm = pe.matmul(fold_ps[0:HEADS, half * 512:half * 512 + 512], env.head_sel[:, :],
                               by_tile[:, half * 512:half * 512 + 512], start=True, stop=True)
            mm.then_inc(s["folded"], 1)

        @block.vector
        def _(dve):
            dve.memset(flags["crossed"][:, :], -BIG)
            dve.memset(by_tile[:, TILES:], 0.0)
            ends = flags["lead"][:, 0:GRPS * P].rearrange("p (g e) -> p g e", e=P)[:, :, P - 1:P]
            dve.tensor_tensor(row_crossed[:, :].unsqueeze(2), ends, flags["entered"][:, 0:GRPS].unsqueeze(2), ALU.min)
            dve.drain()
            dve.tensor_tensor(by_tile[:, 0:TILES].rearrange("p (g k) -> p g k", k=SLOT_BUFS),
                              over_columns(row_crossed[:, :], SLOT_BUFS), over_rows(env.tile_mask[:, :], GRPS),
                              ALU.mult).then_inc(s["by_tile"], 1)
            dve.wait_ge(s["folded"], 1)
            dve.tensor_copy(flags["crossed"][:, 0:TILES], fold_ps[0:HEADS, 0:TILES])


def first_scores(env, tag, table, first_dst):
    nc = env.nc
    width = D + 2 * HEADS
    with ExitStack() as ctx:
        sb, ps = stage_memory(nc, ctx, tag)
        rows = sb("rows", [P, FIRSTS, width], F32)
        spread = sb("spread", [P, FIRSTS, SLOT_BUFS, HEADS], F32)
        out_ps = ps("out", [P, 512], F32)
        sig = {n: env.sig(f"first_{n}") for n in ("gathered", "spread", "turned")}
        block = ctx.enter_context(nc.Block())

        @block.gpsimd
        def _(pool):
            for j in range(FIRSTS):
                pool.indirect_dma_start(rows[:, j, :], None, table,
                                        bass.IndirectOffsetOnAxis(ap=env.first_idx[:, j:j + 1], axis=0)
                                        ).then_inc(sig["gathered"].sem, 16)

        @block.vector
        def _(dve):
            dve.wait_ge(sig["gathered"].sem, sig["gathered"].at(16 * FIRSTS))
            for j in range(FIRSTS):
                last = dve.tensor_tensor(spread[:, j, :, :], over_rows(rows[:, j, D + HEADS:width], SLOT_BUFS),
                                         over_columns(env.tile_sel[:, :], HEADS), ALU.mult)
            last.then_inc(sig["spread"].sem, 1)
            dve.wait_ge(sig["turned"].sem, sig["turned"].at(1))
            dve.tensor_scalar(first_dst[:, :], out_ps[:, 0:HEADS * FIRSTS], -1.0, None, ALU.mult)

        @block.tensor
        def _(pe):
            pe.wait_ge(sig["spread"].sem, sig["spread"].at(1))
            for j in range(FIRSTS):
                mm = pe.matmul(out_ps[:, j * HEADS:(j + 1) * HEADS], spread[:, j, :, :].rearrange("p k h -> p (k h)"),
                               env.head_mask[:, :], start=True, stop=True)
            mm.then_inc(sig["turned"].sem, 1)

        for n, count in (("gathered", 16 * FIRSTS), ("spread", 1), ("turned", 1)):
            sig[n].passed(count)


def attend(env, tag, table, flags, first_dst, acc):
    nc = env.nc
    width = D + 2 * HEADS
    with ExitStack() as ctx:
        sb, ps = stage_memory(nc, ctx, tag)
        rows = sb("rows", [P, PHASES * SLOT_BUFS, width], F32)
        scores = sb("scores", [P, PHASES, 2, SLOT_BUFS, HEADS], F32)
        score = sb("score", [P, P], F32)
        own_dst = sb("own_dst", [P, P], F32)
        neg_dst = sb("neg_dst", [P, P], F32)
        so_far = sb("so_far", [P, P], F32)
        next_reset = sb("next_reset", [P, P], BF16)
        largest = sb("largest", [P, P], F32)
        numer = sb("numer", [P, PHASES, P], F32)
        ends = sb("ends", [P, SLOT_BUFS], F32)
        chain = sb("chain", [HEADS, SLOT_BUFS + 1], F32)
        picked = sb("picked", [P, SLOT_BUFS], F32)
        came_in = sb("came_in", [P, 1], F32)
        first_max = sb("first_max", [P, 1], F32)
        drop = sb("drop", [P, SLOT_BUFS], F32)
        factor_row = sb("factor_row", [P, SLOT_BUFS], F32)
        p_col = sb("p_col", [P, P], F32)
        p_wide = sb("p_wide", [P, PHASES, SLOT_BUFS, D], F32)
        factor = sb("factor", [P, PHASES, SLOT_BUFS], F32)
        scaled = sb("scaled", [P, 4, HEADS, CH], F32)
        hot = sb("hot", [P, SLOT_BUFS, P], F32)
        dist = sb("dist", [P, 4, P], F32)
        turn_ps = ps("turn", [P, 2, 256], F32)
        p_ps = [ps(f"p{f}", [P, 512], F32) for f in range(PHASES)]
        small_ps = ps("small", [P, 512], F32)
        fold_ps, spread_ps, factor_ps = (small_ps[:, k * SLOT_BUFS:(k + 1) * SLOT_BUFS] for k in range(3))
        sums = [ps(f"sums{j}", [P, 2, 256], F32) for j in range(3)]
        landed = [env.sig(f"landed{k}") for k in range(SLOT_BUFS)]
        names = ("idx_staged", "arrived", "scores_staged", "turned", "kept", "ends_ready", "folded", "chained", "spread", "shifted",
                 "exped", "p_turned", "p_ready", "wide_ready", "dist_ready", "hot_ready", "scaled_ready", "multiplied", "added")
        sig = {n: env.sig(f"attend_{n}") for n in names}
        s = {n: x.sem for n, x in sig.items()}
        v = {n: x.at for n, x in sig.items()}
        held = PHASES * SLOT_BUFS
        block = ctx.enter_context(nc.Block())

        @block.gpsimd
        def _(pool):
            with pool.Fori(0, GRPS // PHASES) as i:
                for f in range(PHASES):
                    for k in range(SLOT_BUFS):
                        if k % 4 == 0:
                            g = i * PHASES + f
                            pool.wait_ge(s["idx_staged"], g * 4 + v["idx_staged"](k // 4 + 1))
                            pool.wait_ge(s["multiplied"], g * SLOT_BUFS + v["multiplied"](k + 4))
                            pool.sem_inc(env.sig("dma_turn").sem, 1)
                        pool.indirect_dma_start(rows[:, f * SLOT_BUFS + k, :], None, table,
                                                bass.IndirectOffsetOnAxis(ap=env.idx_stage[:, k:k + 1], axis=0)
                                                ).then_inc(landed[k].sem, 16)

        @block.sync
        def _(sp):
            with sp.Fori(0, GRPS) as g:
                for k in range(SLOT_BUFS):
                    sp.wait_ge(landed[k].sem, g * 16 + landed[k].at(16))
                    sp.sem_inc(s["arrived"], 1)
            sp.sem_inc(s["arrived"], 2 * SLOT_BUFS)

        @block.scalar
        def _(act):
            def take_scores(g, f, turn):
                four = slice(4 * turn, 4 * turn + 4)
                bufs = slice(f * SLOT_BUFS + 4 * turn, f * SLOT_BUFS + 4 * turn + 4)
                if turn == 0:
                    act.wait_ge(s["turned"], g + v["turned"](1))
                act.wait_ge(s["arrived"], g * SLOT_BUFS + v["arrived"](4 * turn + 4))
                act.copy(scores[:, f, 0, four, :], rows[:, bufs, D:D + HEADS])
                act.copy(scores[:, f, 1, four, :], rows[:, bufs, D + HEADS:width]).then_inc(s["scores_staged"], 1)
                stage_indices(act, env, env.src_idx, g + 1, turn, s["idx_staged"])

            def stage_resets(g):
                act.copy(next_reset[:, :], flags["reset"][:, bass.ds(g * P + 1, P)])

            def exponentials(g, f):
                act.wait_ge(s["shifted"], g + v["shifted"](1))
                act.activation(numer[:, f, :], score[:, :], ACT.Exp)
                act.activation(factor_row[:, :], drop[:, :], ACT.Exp).then_inc(s["exped"], 1)
                stage_resets(g + 1)

            def keep_numerators(g, f):
                act.wait_ge(s["p_turned"], g + v["p_turned"](1))
                act.copy(p_col[:, :], p_ps[f][:, 0:P])
                act.copy(factor[:, f, :], factor_ps).then_inc(s["p_ready"], 1)
                act.wait_ge(s["p_ready"], g + v["p_ready"](1))
                for turn in range(4):
                    act.copy(p_wide[:, f, 4 * turn:4 * turn + 4, :].rearrange("p k (h c) -> p (k h) c", c=CH),
                             over_columns(p_col[:, 4 * turn * HEADS:4 * (turn + 1) * HEADS], CH)).then_inc(s["wide_ready"], 1)

            def build(g, turn):
                act.wait_ge(s["multiplied"], g * SLOT_BUFS + v["multiplied"](held - SLOT_BUFS + 4 * turn + 4))
                to = slice(turn % 4 * 4, turn % 4 * 4 + 4)
                one_hots_on_act(act, env, g * SLOT_BUFS + 4 * turn, 4, dist, hot[:, to, :], s["dist_ready"],
                                g * 4 + v["dist_ready"](turn + 1), s["hot_ready"],
                                None if turn == 0 else g * SLOT_BUFS + v["hot_ready"](4 * turn))

            for turn in range(4):
                stage_indices(act, env, env.src_idx, 0, turn, s["idx_staged"])
            for turn in range(2):
                build(0, turn)
            stage_resets(0)
            for g in range(2):
                for turn in range(4):
                    take_scores(g, g, turn)
            exponentials(0, 0)
            keep_numerators(0, 0)
            with act.Fori(0, GRPS // PHASES) as i:
                for f in range(PHASES):
                    g = i * PHASES + f
                    ahead, next_f = (f + 2) % PHASES, (f + 1) % PHASES
                    build(g, 2)
                    take_scores(g + 2, ahead, 0)
                    take_scores(g + 2, ahead, 1)
                    build(g, 3)
                    take_scores(g + 2, ahead, 2)
                    take_scores(g + 2, ahead, 3)
                    build(g, 4)
                    exponentials(g + 1, next_f)
                    keep_numerators(g + 1, next_f)
                    build(g, 5)

        @block.vector
        def _(dve):
            def softmax_step(g, step):
                cols = bass.ds(g * P, P)
                source, dest = turn_ps[:, 0, 0:P], turn_ps[:, 1, 0:P]
                if step == 1:
                    dve.wait_ge(s["turned"], g + v["turned"](PHASES + 1))
                    dve.scalar_tensor_tensor(own_dst[:, 1:P], flags["goes_on"][:, bass.ds(g * P + 1, P - 1)], 1.0,
                                             dest[:, 1:P], ALU.subtract, ALU.mult)
                    dve.tensor_copy(own_dst[:, 0:1], first_dst[:, bass.ds(g, 1)])
                    dve.drain()
                    dve.tensor_tensor_scan(neg_dst[:, :], flags["goes_on"][:, cols], own_dst[:, :], 0.0, ALU.mult, ALU.add)
                elif step == 2:
                    dve.drain()
                    dve.tensor_tensor(score[:, :], source, neg_dst[:, :], ALU.subtract).then_inc(s["kept"], 1)
                elif step == 3:
                    dve.drain()
                    dve.scalar_tensor_tensor(score[:, :], score[:, :], 0.2, score[:, :], ALU.mult, ALU.max)
                elif step == 4:
                    dve.drain()
                    dve.tensor_tensor_scan(so_far[:, :], flags["reset"][:, cols], score[:, :], -BIG, ALU.add, ALU.max)
                elif step == 5:
                    dve.drain()
                    dve.tensor_scalar(ends[:, :], env.tile_mask[:, :], so_far[:, P - 1:P], None, ALU.mult).then_inc(s["ends_ready"], 1)
                    dve.tensor_tensor_scan(largest[:, ::-1], next_reset[:, ::-1], so_far[:, ::-1], -BIG, ALU.add,
                                           ALU.max)
                elif step == 7:
                    dve.tensor_copy(chain[:, 0:1], chain[:, SLOT_BUFS:])
                    dve.drain()
                    dve.wait_ge(s["folded"], g + v["folded"](1))
                    dve.tensor_tensor_scan(chain[:, 1:], flags["crossed"][:, bass.ds(g * SLOT_BUFS, SLOT_BUFS)],
                                           fold_ps[0:HEADS, :], chain[:, 0:1], ALU.add, ALU.max).then_inc(s["chained"], 1)
                elif step == 9:
                    dve.wait_ge(s["spread"], g + v["spread"](1))
                    dve.tensor_tensor_reduce(picked[:, :], spread_ps, env.tile_mask[:, :], 1.0, 0.0, ALU.mult, ALU.add,
                                             came_in[:, 0:1])
                elif step == 10:
                    dve.drain()
                    dve.tensor_tensor(first_max[:, :], came_in[:, 0:1], largest[:, 0:1], ALU.max)
                    dve.drain()
                    dve.tensor_scalar(drop[:, :], env.other_tile[:, :], came_in[:, 0:1], first_max[:, 0:1], ALU.add, ALU.subtract)
                    dve.scalar_tensor_tensor(largest[:, :], flags["lead"][:, cols], first_max[:, 0:1], largest[:, :], ALU.add,
                                             ALU.max)
                elif step == 11:
                    dve.drain()
                    dve.tensor_tensor(score[:, :], score[:, :], largest[:, :], ALU.subtract).then_inc(s["shifted"], 1)

            dve.memset(acc[:, :, :], 0.0)
            dve.memset(factor[:, PHASES - 1, :], 0.0)
            dve.memset(chain[:, :], -BIG)
            for j in range(3):
                dve.memset(sums[j][:, :, :], 0.0)
            dve.sem_inc(s["kept"], 1)
            dve.drain().then_inc(s["added"], 1)
            for step in range(12):
                softmax_step(0, step)
            with dve.Fori(0, GRPS // PHASES) as i:
                for f in range(PHASES):
                    g = i * PHASES + f
                    starts = window_starts(env, g, late=2)
                    dve.wait_ge(s["p_ready"], g + v["p_ready"](1))
                    for k in range(SLOT_BUFS):
                        tile, j, buf = g * SLOT_BUFS + k, k % 4, f * SLOT_BUFS + k
                        dve.tensor_tensor(scaled[:, j, :, :], rows[:, buf, 0:D].rearrange("p (h c) -> p h c", h=HEADS),
                                          over_columns(p_ps[f][:, k * HEADS:(k + 1) * HEADS], CH),
                                          ALU.mult).then_inc(s["scaled_ready"], 1)
                        softmax_step(g + 1, k)
                        dve.wait_ge(s["multiplied"], tile + v["multiplied"](held - 1))
                        dve.wait_ge(s["added"], tile + v["added"](1))
                        before, bank = (buf - 2) % held, sums[(buf - 2) % 3]
                        first = acc[:, :, bass.ds(starts[k], 1)]
                        dve.scalar_tensor_tensor(first, first, factor[:, before // SLOT_BUFS, before % SLOT_BUFS:before % SLOT_BUFS + 1],
                                                 bank[:, :, 0:1], ALU.mult, ALU.add)
                        others = acc[:, :, bass.ds(starts[k] + 1, P - 1)]
                        dve.tensor_tensor(others, others, bank[:, :, 1:P], ALU.add).then_inc(s["added"], 1)
            assert SLOTS - (N + E) >= 2 * P

        @block.tensor
        def _(pe):
            def turn_scores(g, f):
                pe.wait_ge(s["scores_staged"], g * 4 + v["scores_staged"](4))
                pe.wait_ge(s["kept"], g + v["kept"](1))
                for k in range(2):
                    mm = pe.transpose(turn_ps[:, k, 0:P], scores[:, f, k, :, :].rearrange("p k h -> p (k h)"), env.ident[:, :])
                mm.then_inc(s["turned"], 1)

            def fold_ends(g):
                pe.wait_ge(s["ends_ready"], g + v["ends_ready"](1))
                pe.matmul(fold_ps[0:HEADS, :], env.head_sel[:, :], ends[:, :], start=True, stop=True).then_inc(s["folded"], 1)

            def spread_chain(g):
                pe.wait_ge(s["chained"], g + v["chained"](1))
                pe.matmul(spread_ps, env.ident[:, :], flags["entered"][:, bass.ds(g, 1)].to_broadcast([P, SLOT_BUFS]),
                          start=True, stop=False)
                pe.matmul(spread_ps, env.head_sel_t[:, :], chain[:, 0:SLOT_BUFS], start=False, stop=True).then_inc(s["spread"], 1)

            def turn_numerators(g, f):
                pe.wait_ge(s["exped"], g + v["exped"](1))
                pe.transpose(p_ps[f][:, 0:P], numer[:, f, :], env.ident[:, :])
                pe.matmul(factor_ps, env.head_rows[:, :], factor_row[:, :], start=True, stop=True).then_inc(s["p_turned"], 1)

            pe.sem_inc(s["multiplied"], held)
            pe.sem_inc(s["turned"], PHASES)
            turn_scores(0, 0)
            fold_ends(0)
            spread_chain(0)
            turn_numerators(0, 0)
            with pe.Fori(0, GRPS // PHASES) as i:
                for f in range(PHASES):
                    g, next_f = i * PHASES + f, (f + 1) % PHASES
                    pe.wait_ge(s["p_ready"], g + v["p_ready"](1))
                    for k in range(SLOT_BUFS):
                        tile, j, bank = g * SLOT_BUFS + k, k % 4, sums[(f * SLOT_BUFS + k) % 3]
                        if k == 0:
                            turn_scores(g + 1, next_f)
                        elif k == 6:
                            fold_ends(g + 1)
                        elif k == 8:
                            spread_chain(g + 1)
                        elif k == 12:
                            turn_numerators(g + 1, next_f)
                        if k % 4 == 0:
                            pe.wait_ge(s["wide_ready"], g * 4 + v["wide_ready"](k // 4 + 1))
                        pe.wait_ge(s["scaled_ready"], tile + v["scaled_ready"](1))
                        pe.wait_ge(s["hot_ready"], tile + v["hot_ready"](1))
                        pe.wait_ge(s["added"], tile + v["added"](1))
                        pe.matmul(bank[:, 0, 0:P], scaled[:, j, :, :].rearrange("p h c -> p (h c)"), hot[:, k, :], start=True,
                                  stop=True)
                        pe.matmul(bank[:, 1, 0:P], p_wide[:, f, k, :], hot[:, k, :], start=True,
                                  stop=True).then_inc(s["multiplied"], 1)

        for n, count in (("idx_staged", 4 * GRPS + 12), ("arrived", TILES + 2 * SLOT_BUFS), ("scores_staged", 4 * GRPS + 8), ("turned", GRPS + 1 + PHASES),
                         ("kept", GRPS + 2), ("ends_ready", GRPS + 1), ("folded", GRPS + 1), ("chained", GRPS + 1),
                         ("spread", GRPS + 1), ("shifted", GRPS + 1), ("exped", GRPS + 1), ("p_turned", GRPS + 1),
                         ("p_ready", GRPS + 1), ("wide_ready", 4 * GRPS + 4), ("dist_ready", 4 * GRPS + 2), ("hot_ready", TILES + 8), ("scaled_ready", TILES),
                         ("multiplied", TILES + held), ("added", TILES + 1)):
            sig[n].passed(count)
        for k in range(SLOT_BUFS):
            landed[k].passed(16 * GRPS)


def divide_sums(env, acc):
    with env.nc.Block() as block:
        @block.vector
        def _(dve):
            dve.tensor_scalar(acc[:, 1, 0:NPAD], acc[:, 1, 0:NPAD], 1e-30, None, ALU.max)
            dve.drain()
            dve.reciprocal(acc[:, 1, 0:NPAD], acc[:, 1, 0:NPAD])
            dve.drain()
            dve.tensor_tensor(acc[:, 0, 0:NPAD], acc[:, 0, 0:NPAD], acc[:, 1, 0:NPAD], ALU.mult)


def run_flags(env, ctx):
    def sb(name, shape, dt=F32):
        return ctx.enter_context(env.nc.sbuf_tensor(f"flags_{name}", shape, dt))

    slots = (GRPS + 1) * P
    return {"goes_on": sb("goes_on", [P, slots], BF16), "reset": sb("reset", [P, slots + P + 1], BF16),
            "lead": sb("lead", [P, slots], BF16), "entered": sb("entered", [P, GRPS + 1]),
            "crossed": sb("crossed", [HEADS, TILES + SLOT_BUFS])}


def gat_layer(env, inp, flags):
    nc = env.nc
    width = D + 2 * HEADS
    table = nc.dram_tensor("gat_table", (NPAD, width), F32, kind="Internal").ap()
    with ExitStack() as ctx:
        def sb(name, shape, dt=F32):
            return ctx.enter_context(nc.sbuf_tensor(f"gat_{name}", shape, dt))

        first_dst = sb("first_dst", [P, HEADS * FIRSTS])
        combined = sb("combined", [P, width])
        bias = sb("bias", [P, 1])
        acc = sb("acc", [P, 2, ACC])
        crossing_runs(env, flags)
        attention_weights(env, "gat1w", inp["L2_gnn_W1"], inp["L2_gnn_as1"], inp["L2_gnn_ad1"], combined)
        project_nodes(env, "gat1tab", True, None, combined, width, table)
        first_scores(env, "gat1first", table, first_dst)
        attend(env, "gat1sum", table, flags, first_dst, acc)
        divide_sums(env, acc)
        load_columns(env, "gat1bias", [(bias[:, :], inp["L2_gnn_b1"].rearrange("(f o) -> f o", o=1))])
        attention_weights(env, "gat2w", inp["L2_gnn_W2"], inp["L2_gnn_as2"], inp["L2_gnn_ad2"], combined)

        def hidden(act, mem, blk, h):
            return act.activation(mem["own"][:, h, :], acc[:, 0, bass.ds(blk * P, P)], ACT.Relu, bias=bias[:, 0:1])

        project_nodes(env, "gat2tab", False, hidden, combined, width, table)
        first_scores(env, "gat2first", table, first_dst)
        attend(env, "gat2sum", table, flags, first_dst, acc)
        divide_sums(env, acc)
        add_rows(env, "gatout", acc, inp["L2_gnn_b2"])
    normalize(env, "norm2")


def tensor_weights(env, inp, wy, w_out, fc1, w2):
    nc = env.nc
    mix, keep = math.cos(math.pi / 8.0), math.sin(math.pi / 8.0)
    fan, fan_two, neighbors = math.sqrt(MUL), math.sqrt(2 * MUL), math.sqrt(16.0)
    edge_part = mix / (fan_two * neighbors)
    scales = (keep / fan, edge_part, edge_part, edge_part / math.sqrt(3.0))
    with ExitStack() as ctx:
        sb, ps = stage_memory(nc, ctx, "tpw")
        wy_in = sb("wy_in", [P, D], F32)
        w_in = sb("w_in", [P, 4, 4, MUL], F32)
        fc2_in = sb("fc2_in", [HID, 4 * MUL], F32)
        zeroed, loaded = env.sig("tpw_zeroed").sem, env.sig("tpw_loaded").sem
        block = ctx.enter_context(nc.Block())

        @block.sync
        def _(sp):
            def vectors(m):
                return slice(MUL + m, D, 3)

            l20, l21 = inp["L3_gnn_W_l20"], inp["L3_gnn_W_l21"]
            loads = [(wy_in[0:MUL, 0:MUL], inp["L3_gnn_W_l10"]), (w_in[0:MUL, 0, 0, :], inp["L3_gnn_W_sc0"]),
                     (w_in[0:MUL, 1, 0, :], l20[0:MUL, :]), (fc2_in[:, :], inp["L3_gnn_W_fc2"])]
            for m in range(3):
                lo = MUL + MUL * m
                loads += [(wy_in[vectors(m), lo:lo + MUL], inp["L3_gnn_W_l11"]),
                          (w_in[vectors(m), 0, 1 + m, :], inp["L3_gnn_W_sc1"]),
                          (w_in[lo:lo + MUL, 1, 1 + m, :], l21[MUL:2 * MUL, :]),
                          (w_in[MUL * m:MUL * (m + 1), 2, 1 + m, :], l21[0:MUL, :]),
                          (w_in[MUL * m:MUL * (m + 1), 3, 0, :], l20[MUL:2 * MUL, :])]
            for i in range(8):
                loads.append((fc1[LEN * i:LEN * (i + 1), i, :], inp["L3_gnn_W_fc1"]))
            sp.wait_ge(zeroed, 1)
            for to, frm in loads:
                sp.dma_start(to, frm).then_inc(loaded, 16)
            sp.wait_ge(loaded, 16 * len(loads))
            sp.sem_inc(zeroed, 1)

        @block.vector
        def _(dve):
            dve.memset(wy_in[:, :], 0.0)
            dve.memset(w_in[:, :, :, :], 0.0)
            dve.memset(fc1[:, :, :], 0.0)
            dve.drain().then_inc(zeroed, 1)
            dve.wait_ge(zeroed, 2)
            dve.tensor_scalar(wy[:, :], wy_in[:, :], 1.0 / fan, None, ALU.mult)
            for i, scale in enumerate(scales):
                dve.tensor_scalar(w_out[:, i, 0:MUL], w_in[:, i, 0, :], scale, None, ALU.mult)
                dve.tensor_scalar(w_out[:, i, MUL:D].rearrange("p (w m) -> p m w", m=3), w_in[:, i, 1:4, :], scale, None,
                                  ALU.mult)
            norm = 1.0 / math.sqrt(HID)
            for to, frm in ((0, 0), (1, 2), (2, 2), (3, 2), (4, 1), (5, 3)):
                dve.tensor_scalar(w2[:, to * MUL:(to + 1) * MUL], fc2_in[:, frm * MUL:(frm + 1) * MUL], norm, None, ALU.mult)


def convolve(env, tag, table, records, fc1, w2, acc):
    nc = env.nc
    vec = 3 * MUL
    octets, turns = 2 * GRPS, 4 * GRPS
    with ExitStack() as ctx:
        sb, ps = stage_memory(nc, ctx, tag)
        rec = sb("rec", [P, TILES + SLOT_BUFS, REC], F32)
        rows = sb("rows", [P, SLOT_BUFS, D], F32)
        hot = sb("hot", [P, 8, P], F32)
        dist = sb("dist", [P, 4, P], F32)
        message = sb("message", [P, 4, D + 2 * vec], F32)
        rows_attr = sb("rows_attr", [P, 8, 3, 2 * MUL], F32)
        lens = sb("lens", [P, 2, 8, LEN], F32)
        lens_t = sb("lens_t", [8 * LEN, 2, P], F32)
        hidden = sb("hidden", [HID, 2, 4, P], F32)
        lens_ps = ps("lens_ps", [P, 512], F32)
        hidden_ps = ps("hidden_ps", [P, 512], F32)
        w_ps = [ps(f"w{j}", [P, 2, 256], F32) for j in range(2)]
        sums = [ps(f"sums{j}", [P, 512], F32) for j in range(4)]
        landed = [env.sig(f"landed{k}") for k in range(SLOT_BUFS)]
        names = ("loaded", "arrived", "tail_zeroed", "idx_staged", "lens_staged", "lens_turned", "lens_ready", "hidden_made",
                 "hidden_ready", "w_made", "dist_ready", "hot_ready", "hot_dve", "rows_ready", "message_ready", "multiplied", "added")
        s = {n: env.sig(f"conv_{n}").sem for n in names}
        block = ctx.enter_context(nc.Block())

        def attr(tile, m):
            return rec[:, bass.ds(tile, 1), R_EA + m:R_EA + m + 1].rearrange("p o k -> p (o k)")

        @block.sync
        def _(sp):
            sp.dma_start(rec[:, 0:TILES, :], records.rearrange("(p q) k -> p q k", p=P)).then_inc(s["loaded"], 16)
            with sp.Fori(0, GRPS) as g:
                for k in range(SLOT_BUFS):
                    sp.wait_ge(landed[k].sem, g * 16 + landed[k].at(16))
                    sp.sem_inc(s["arrived"], 1)
            sp.sem_inc(s["arrived"], 4)

        @block.gpsimd
        def _(pool):
            gather_program(pool, env, table, rows, landed, s["multiplied"], lambda n: n, s["idx_staged"], lambda n: n)

        @block.scalar
        def _(act):
            def stage_lens(octet, u):
                act.copy(lens[:, u, :, :], rec[:, bass.ds(octet * 8, 8), R_LEN:REC]).then_inc(s["lens_staged"], 1)

            def keep_lens(octet, u):
                act.wait_ge(s["lens_turned"], octet + 1)
                act.copy(lens_t[:, u, :], lens_ps[0:8 * LEN, u * P:(u + 1) * P]).then_inc(s["lens_ready"], 1)

            def activate(turn, h):
                act.wait_ge(s["hidden_made"], turn + 1)
                act.activation(hidden[:, h, :, :].rearrange("p k e -> p (k e)"), hidden_ps[0:HID, :], ACT.Silu,
                               scale=1.0 / math.sqrt(LEN)).then_inc(s["hidden_ready"], 1)

            def build(g, turn):
                act.wait_ge(s["multiplied"], g * SLOT_BUFS + (SLOT_BUFS - 8 + 4 * turn + 4))
                to = slice(turn % 2 * 4, turn % 2 * 4 + 2)
                one_hots_on_act(act, env, g * SLOT_BUFS + 4 * turn, 2, dist, hot[:, to, :], s["dist_ready"], g * 4 + (turn + 1),
                                s["hot_ready"], None if turn == 0 else g * 8 + 2 * turn)
                for k in range(4 * turn, 4 * turn + 4):
                    j, tile = k % SLOT_BUFS, g * SLOT_BUFS + k
                    act.wait_ge(s["arrived"], tile + 1)
                    by_block = rows[:, j, :].rearrange("p (b u) -> p b u", b=4)
                    for m in range(3):
                        last = act.activation(rows_attr[:, k % 8, m, :].rearrange("p (i u) -> p i u", i=2),
                                              by_block[:, 0:m + 2:m + 1, :], ACT.Identity, scale=attr(tile, 1 + m))
                    last.then_inc(s["rows_ready"], 1)

            for turn in range(4):
                stage_indices(act, env, env.src_idx, 0, turn, s["idx_staged"])
            act.wait_ge(s["loaded"], 16)
            act.wait_ge(s["tail_zeroed"], 1)
            stage_lens(0, 0)
            stage_lens(1, 1)
            keep_lens(0, 0)
            activate(0, 0)
            build(0, 0)
            with act.Fori(0, GRPS) as g:
                for t in range(4):
                    if t % 2 == 0:
                        octet, u = g * 2 + t // 2, t // 2
                        keep_lens(octet + 1, 1 - u)
                        stage_lens(octet + 2, u)
                    act.wait_ge(s["w_made"], g * (SLOT_BUFS // 2) + (2 * t + 2))
                    activate(g * 4 + (t + 1), (t + 1) % 2)
                    build(g, t + 1)
                    act.wait_ge(s["multiplied"], g * SLOT_BUFS + (SLOT_BUFS + 4 * t + 4))
                    stage_indices(act, env, env.src_idx, g + 1, t, s["idx_staged"])

        @block.vector
        def _(dve):
            def build(tile, j):
                dve.tensor_scalar(hot[:, j, :], env.iota_row[:, :], env.dst_rel[:, bass.ds(tile, 1)], None,
                                  ALU.is_equal).then_inc(s["hot_dve"], 1)

            build(2, 2)
            build(3, 3)
            dve.memset(rec[:, TILES:, :], 0.0).then_inc(s["tail_zeroed"], 1)
            dve.memset(acc[:, :, :], 0.0)
            for j in range(4):
                dve.memset(sums[j][:, :], 0.0)
            dve.drain().then_inc(s["added"], 2)
            dve.wait_ge(s["loaded"], 16)
            with dve.Fori(0, GRPS) as g:
                starts = window_starts(env, g, late=2)
                for k in range(SLOT_BUFS):
                    tile, j = g * SLOT_BUFS + k, k % 4
                    dve.wait_ge(s["rows_ready"], tile + 1)
                    dve.wait_ge(s["w_made"], g * (SLOT_BUFS // 2) + (k // 2 + 3))
                    w = w_ps[k // 2 % 2][:, k % 2, :]
                    dve.scalar_tensor_tensor(message[:, j, 0:D], w[:, 0:D], attr(tile, 0), rows[:, k, :], ALU.mult, ALU.mult)
                    w_parts = over_rows(w[:, D:D + 2 * MUL], 3).rearrange("p m (i u) -> p m i u", i=2)
                    dve.tensor_tensor(message[:, j, D:].rearrange("p (i m u) -> p m i u", i=2, m=3),
                                      rows_attr[:, k % 8, :, :].rearrange("p m (i u) -> p m i u", i=2), w_parts,
                                      ALU.mult).then_inc(s["message_ready"], 1)
                    if k % 4 >= 2:
                        build(tile + 4, (k + 4) % 8)
                    dve.wait_ge(s["multiplied"], tile + (SLOT_BUFS - 1))
                    dve.wait_ge(s["added"], tile + 2)
                    window = acc[:, :, bass.ds(starts[k], P)]
                    dve.tensor_tensor(window, window, sums[(k - 2) % 4][:, 0:3 * P].rearrange("p (a n) -> p a n", a=3),
                                      ALU.add).then_inc(s["added"], 1)
            assert SLOTS - (N + E) >= 2 * P

        @block.tensor
        def _(pe):
            def turn_lens(octet, u):
                pe.wait_ge(s["lens_staged"], octet + 1)
                pe.transpose(lens_ps[0:8 * LEN, u * P:(u + 1) * P], lens[:, u, :, :].rearrange("p k l -> p (k l)"),
                             env.ident[:, :]).then_inc(s["lens_turned"], 1)

            def make_hidden(octet, u, half):
                pe.wait_ge(s["lens_ready"], octet + 1)
                for i in range(4):
                    mm = pe.matmul(hidden_ps[0:HID, i * P:(i + 1) * P], fc1[:, 4 * half + i, :], lens_t[:, u, :], start=True,
                                   stop=True)
                mm.then_inc(s["hidden_made"], 1)

            def make_w(first):
                for k in (first, first + 1):
                    mm = pe.matmul(w_ps[k // 2 % 2][:, k % 2, 0:D + 2 * MUL], hidden[:, k // 4 % 2, k % 4, :], w2[:, :],
                                   start=True, stop=True)
                mm.then_inc(s["w_made"], 1)

            pe.sem_inc(s["multiplied"], SLOT_BUFS)
            pe.sem_inc(s["w_made"], 2)
            turn_lens(0, 0)
            make_hidden(0, 0, 0)
            pe.wait_ge(s["hidden_ready"], 1)
            make_w(0)
            with pe.Fori(0, GRPS) as g:
                for k in range(SLOT_BUFS):
                    t, j, tile = k // 4, k % 4, g * SLOT_BUFS + k
                    octet, u = g * 2 + t // 2, t // 2
                    if k % 8 == 0:
                        turn_lens(octet + 1, 1 - u)
                    if k % 4 == 0:
                        if t % 2 == 0:
                            make_hidden(octet, u, 1)
                        else:
                            make_hidden(octet + 1, 1 - u, 0)
                    if k % 4 == 2:
                        pe.wait_ge(s["hidden_ready"], g * 4 + (t + 2))
                    if k % 2 == 0:
                        make_w(k + 2)
                    if j < 2:
                        pe.wait_ge(s["hot_ready"], g * 8 + (2 * t + j + 1))
                    else:
                        pe.wait_ge(s["hot_dve"], g * 8 + (2 * t + j - 1))
                    pe.wait_ge(s["message_ready"], tile + 1)
                    pe.wait_ge(s["added"], tile + 1)
                    pe.matmul(sums[j][:, 0:P], message[:, j, 0:D], hot[:, k % 8, :], start=True, stop=True)
                    for i in range(2):
                        mm = pe.matmul(sums[j][0:vec, (i + 1) * P:(i + 2) * P], message[:, j, D + i * vec:D + (i + 1) * vec],
                                       hot[:, k % 8, :], start=True, stop=True)
                    mm.then_inc(s["multiplied"], 1)

        for k in range(SLOT_BUFS):
            landed[k].passed(16 * GRPS)


def tensor_layer(env, inp, records, out):
    nc = env.nc
    table = nc.dram_tensor("tensor_table", (NPAD, D), F32, kind="Internal").ap()
    with ExitStack() as ctx:
        def sb(name, shape):
            return ctx.enter_context(nc.sbuf_tensor(f"tp_{name}", shape, F32))

        attr = sb("attr", [P, BLKS])
        wy, w_out = sb("wy", [P, D]), sb("w_out", [P, 4, D])
        fc1, w2 = sb("fc1", [8 * LEN, 8, HID]), sb("w2", [HID, D + 2 * MUL])
        tensor_weights(env, inp, wy, w_out, fc1, w2)
        with nc.Block() as block:
            @block.vector
            def _(dve):
                dve.memset(attr[:, :], 0.0)
        whole = (BLKS - 1) * P
        load_columns(env, "attr", [(attr[:, 0:BLKS - 1], inp["node_vec1"][0:whole, :].rearrange("(b p) o -> p (b o)", p=P)),
                                   (attr[0:LAST, BLKS - 1:BLKS], inp["node_vec1"][whole:N, :])])
        project_nodes(env, "tptab", True, None, wy, D, table, scale=attr)
        acc = ctx.enter_context(nc.sbuf_tensor("tp_acc", [P, 3, ACC], F32))
        convolve(env, "conv", table, records, fc1, w2, acc)

        def memory(sb, ps):
            return {"sums": sb("sums", [P, 2, 3, P], F32)}

        def prepare(act, mem, blk, h):
            return act.copy(mem["sums"][:, h, :, :], acc[:, :, bass.ds(blk * P, P)])

        def apply(pe, mem, h, x_t, out):
            pe.matmul(out[:, 0:D], x_t, w_out[:, 0, :], start=True, stop=False)
            for i in range(3):
                mm = pe.matmul(out[:, 0:D], mem["sums"][:, h, i, :], w_out[:, 1 + i, :], start=False, stop=i == 2)
            return mm

        def use(dve, mem, blk, h, out):
            return add_and_measure(env, dve, mem, blk, h, out[:, 0:D], scale=attr)

        per_node_block(env, "tpout", True, prepare, apply, use, memory)
    normalize(env, "norm3", store_output(env, out))


def build(nc, inp, out):
    with ExitStack() as ctx:
        till_last = ctx.enter_context(ExitStack())
        env = Env(nc, ctx, till_last)
        records = nc.dram_tensor("records", (SLOTS, REC), F32, kind="Internal").ap()
        x_table = nc.dram_tensor("x_table", (NPAD, D), F32, kind="Internal").ap()
        relation_rows = nc.dram_tensor("relation_table", (NPAD * REL, D), F32, kind="Internal").ap()
        weights_dram = nc.dram_tensor("relation_weights", (2 * REL, D * D), F32, kind="Internal").ap()
        setup(env, inp)
        relation_layers = [(inp["L0_gnn_basis1"], inp["L0_gnn_coeff1"]), (inp["L0_gnn_basis2"], inp["L0_gnn_coeff2"])]
        sort_edges(env, inp, records, relation_layers, weights_dram, relation_rows)
        load_sorted(env, records)
        relational_layer(env, inp, weights_dram, relation_rows, x_table)
        flags = run_flags(env, till_last)
        gcn_layer(env, inp, x_table, segment_flags(env, flags))
        gat_layer(env, inp, flags)
        till_last.close()
        tensor_layer(env, inp, records, out)


def kernel(**inputs):
    import numpy as _np
    import concourse.bacc as _bacc
    from concourse import mybir as _mybir
    from concourse.bass_utils import run_bass_kernel_spmd as _run

    nc = _bacc.Bacc("TRN2", target_bir_lowering=False, num_devices=1)
    arrays, inp = {}, {}
    for name, value in inputs.items():
        a = _np.ascontiguousarray(value)
        arrays[f"in_{name}_dram"] = a
        inp[name] = nc.dram_tensor(f"in_{name}_dram", a.shape, _mybir.dt.from_np(a.dtype), kind="ExternalInput").ap()
    out = nc.dram_tensor("out_0_dram", (N, D), F32, kind="ExternalOutput").ap()
    build(nc, inp, out)
    r = _run(nc, [arrays], core_ids=[0])
    return r.results[0]["out_0_dram"]
```
